# Optimizing a Trainium2 kernel written in Bass

```python
import numpy as np
import jax
import jax.numpy as jnp

def _softmax(x, axis=-1):
    return jax.nn.softmax(x, axis=axis)

def _gelu(x):
    return jax.nn.gelu(x, approximate=True)

def _silu(x):
    return jax.nn.silu(x)

def _sigmoid(x):
    return jax.nn.sigmoid(x)

def _layernorm(x, axis=-1, eps=1e-05):
    m = jnp.mean(x, axis=axis, keepdims=True)
    v = jnp.var(x, axis=axis, keepdims=True)
    return (x - m) / jnp.sqrt(v + eps)

def _scatter_add(tgt, idx, src, axis=0):
    return tgt.at[idx].add(src)

def _segment_sum(src, seg, n):
    return jax.ops.segment_sum(src, seg, n)
kernel_name = 'mk_cond_seq_d4_seqx_r4_57fb8c'

def setup_inputs(seed: int=0):
    np.random.seed(seed)
    _w = jnp.asarray

    def _rec_inputs():
        import jax
        import jax.numpy as jnp
        _rk = jax.random.key(seed)
        x = -0.0003929 + 0.9999 * jax.random.normal(jax.random.fold_in(_rk, 1), (2, 1024, 256), jnp.float32)
        _lenS = 1024 - jax.random.randint(jax.random.fold_in(_rk, 7), (2,), 0, max(1, 1024 // 4) + 1, jnp.int32)
        _lenS2 = 1024 - jax.random.randint(jax.random.fold_in(_rk, 8), (2,), 0, max(1, 1024 // 4) + 1, jnp.int32)
        cond_1024 = 0.00782532 + 1.00527 * jax.random.normal(jax.random.fold_in(_rk, 11), (2, 256), jnp.float32)
        return (x, cond_1024)
    x, cond_1024 = _rec_inputs()

    def _L0_cond_setup():
        import jax, jax.numpy as jnp
        import numpy as np
        B, L, D, P = (8, 512, 256, 64)

        def _ln(x):
            m = x.mean(-1, keepdims=True)
            v = x.var(-1, keepdims=True)
            return (x - m) * jax.lax.rsqrt(v + 1e-05)

        def _s5(u, Lam_re, Lam_im, B_re, B_im, C_re, C_im, D_diag, log_step):
            Lam = Lam_re + 1j * Lam_im
            dt = jnp.exp(log_step)
            Lam_bar = jnp.exp(Lam * dt)
            Bc = B_re + 1j * B_im
            B_bar = ((Lam_bar - 1.0) / Lam)[:, None] * Bc
            Bu = jnp.einsum('bld,pd->blp', u.astype(B_bar.dtype), B_bar)
            A = jnp.broadcast_to(Lam_bar, Bu.shape)

            def binop(e1, e2):
                a1, b1 = e1
                a2, b2 = e2
                return (a1 * a2, a2 * b1 + b2)
            _, xs = jax.lax.associative_scan(binop, (A, Bu), axis=1)
            Cc = C_re + 1j * C_im
            return 2.0 * jnp.einsum('blp,dp->bld', xs, Cc).real + D_diag * u
        key = jax.random.key(seed)
        ks = jax.random.split(key, 16)
        inp = {'y': jax.random.normal(ks[0], (B, L, D), jnp.float32), 't': jax.random.normal(ks[1], (B, D), jnp.float32), 'Wm': jax.random.normal(ks[2], (D, 6 * D), jnp.float32) * 0.02, 'bm': jax.random.normal(ks[3], (6 * D,), jnp.float32) * 0.02, 'Lam_re': -0.5 * jnp.ones((P,), jnp.float32), 'Lam_im': jnp.pi * jnp.arange(P, dtype=jnp.float32), 'B_re': jax.random.normal(ks[4], (P, D), jnp.float32) / np.sqrt(D), 'B_im': jax.random.normal(ks[5], (P, D), jnp.float32) / np.sqrt(D), 'C_re': jax.random.normal(ks[6], (D, P), jnp.float32) / np.sqrt(P), 'C_im': jax.random.normal(ks[7], (D, P), jnp.float32) / np.sqrt(P), 'D_diag': jax.random.normal(ks[8], (D,), jnp.float32), 'log_step': jax.random.uniform(ks[9], (P,), jnp.float32, np.log(0.001), np.log(0.1)), 'Wc': jax.random.normal(ks[10], (D, 2 * D), jnp.float32) * 0.02, 'bc': jax.random.normal(ks[11], (2 * D,), jnp.float32) * 0.02, 'W1': jax.random.normal(ks[12], (D, 4 * D), jnp.float32) / np.sqrt(D), 'b1': jnp.zeros((4 * D,), jnp.float32), 'W2': jax.random.normal(ks[13], (4 * D, D), jnp.float32) / np.sqrt(4 * D) * 0.1, 'b2': jnp.zeros((D,), jnp.float32)}
        return inp
    _L0_cond_all = _L0_cond_setup()
    _L0_cond_in = {k: v for k, v in _L0_cond_all.items() if k in ('Wm', 'bm', 'Lam_re', 'Lam_im', 'B_re', 'B_im', 'C_re', 'C_im', 'D_diag', 'log_step', 'Wc', 'bc', 'W1', 'b1', 'W2', 'b2')}
    del _L0_cond_all

    def _L1_cond_setup():
        import jax, jax.numpy as jnp
        import numpy as np
        DIM = 256
        MLP_RATIO = 4
        EPS = 1e-06

        def rmsnorm(x, w):
            return x * jax.lax.rsqrt(jnp.mean(x * x, axis=-1, keepdims=True) + EPS) * w

        def film(x, cond, w, b):
            ss = cond @ w + b
            scale, shift = jnp.split(ss, 2, axis=-1)
            return x * (1.0 + scale[:, None, :]) + shift[:, None, :]
        key = jax.random.key(seed)
        ks = jax.random.split(key, 16)
        B, N, D = (4, 512, DIM)
        H = D * MLP_RATIO
        s = lambda fan_in: 1.0 / np.sqrt(fan_in)
        return {'x': jax.random.normal(ks[0], (B, N, D), jnp.float32), 'cond': jax.random.normal(ks[1], (B, D), jnp.float32), 'norm1_w': jnp.ones((D,), jnp.float32), 'film1_w': jax.random.normal(ks[2], (D, 2 * D), jnp.float32) * s(D), 'film1_b': jnp.zeros((2 * D,), jnp.float32), 'q_w': jax.random.normal(ks[3], (D, D), jnp.float32) * s(D), 'q_b': jnp.zeros((D,), jnp.float32), 'k_w': jax.random.normal(ks[4], (D, D), jnp.float32) * s(D), 'k_b': jnp.zeros((D,), jnp.float32), 'v_w': jax.random.normal(ks[5], (D, D), jnp.float32) * s(D), 'v_b': jnp.zeros((D,), jnp.float32), 'proj_w': jax.random.normal(ks[6], (D, D), jnp.float32) * s(D), 'proj_b': jnp.zeros((D,), jnp.float32), 'norm2_w': jnp.ones((D,), jnp.float32), 'film2_w': jax.random.normal(ks[7], (D, 2 * D), jnp.float32) * s(D), 'film2_b': jnp.zeros((2 * D,), jnp.float32), 'mlp_w1': jax.random.normal(ks[8], (D, H), jnp.float32) * s(D), 'mlp_b1': jnp.zeros((H,), jnp.float32), 'mlp_w2': jax.random.normal(ks[9], (H, D), jnp.float32) * s(H), 'mlp_b2': jnp.zeros((D,), jnp.float32)}
    _L1_cond_all = _L1_cond_setup()
    _L1_cond_in = {k: v for k, v in _L1_cond_all.items() if k in ('norm1_w', 'film1_w', 'film1_b', 'q_w', 'q_b', 'k_w', 'k_b', 'v_w', 'v_b', 'proj_w', 'proj_b', 'norm2_w', 'film2_w', 'film2_b', 'mlp_w1', 'mlp_b1', 'mlp_w2', 'mlp_b2')}
    del _L1_cond_all

    def _L2_cond_setup():
        import jax, jax.numpy as jnp
        import numpy as np
        FEAT = 256
        ADA = 256
        INTER = 256
        RANK = 8
        EPS = 1e-05

        def _layernorm(a, g, b):
            mu = jnp.mean(a, axis=-1, keepdims=True)
            var = jnp.mean(jnp.square(a - mu), axis=-1, keepdims=True)
            return (a - mu) * jax.lax.rsqrt(var + EPS) * g + b
        key = jax.random.key(seed)
        ks = jax.random.split(key, 6)
        B, T = (16, 256)
        x = jax.random.normal(ks[0], (B, T, FEAT), dtype=jnp.float32)
        ada_emb = jax.random.normal(ks[1], (B, ADA), dtype=jnp.float32)
        W1 = jax.random.normal(ks[2], (ADA, INTER), dtype=jnp.float32) / np.sqrt(ADA)
        b1 = jnp.zeros((INTER,), dtype=jnp.float32)
        W2 = jax.random.normal(ks[3], (INTER, FEAT * RANK * 4), dtype=jnp.float32) * (0.1 / np.sqrt(INTER))
        b2 = jnp.zeros((FEAT * RANK * 4,), dtype=jnp.float32)
        ln_g = jnp.ones((ADA,), dtype=jnp.float32)
        ln_b = jnp.zeros((ADA,), dtype=jnp.float32)
        return {'x': x, 'ada_emb': ada_emb, 'ln_g': ln_g, 'ln_b': ln_b, 'W1': W1, 'b1': b1, 'W2': W2, 'b2': b2}
    _L2_cond_all = _L2_cond_setup()
    _L2_cond_in = {k: v for k, v in _L2_cond_all.items() if k in ('ln_g', 'ln_b', 'W1', 'b1', 'W2', 'b2')}
    del _L2_cond_all

    def _L3_cond_setup():
        import jax, jax.numpy as jnp
        import numpy as np
        EPS = 1e-05

        def _sln(h, w, ln_g, ln_b, Wg, bg, Wb, bb):
            mu = jnp.mean(h, axis=-1, keepdims=True)
            var = jnp.mean((h - mu) ** 2, axis=-1, keepdims=True)
            ln = (h - mu) / jnp.sqrt(var + EPS) * ln_g + ln_b
            gamma = (w @ Wg.T + bg)[:, None, :]
            beta = (w @ Wb.T + bb)[:, None, :]
            return gamma * ln + beta
        key = jax.random.key(seed)
        ks = jax.random.split(key, 20)
        B, N, D = (4, 256, 256)
        F = 4 * D
        s = lambda fan: 1.0 / np.sqrt(fan)
        inp = {'hidden': jax.random.normal(ks[0], (B, N, D), jnp.float32), 'w': jax.random.normal(ks[1], (B, D), jnp.float32), 'ln_g': jnp.ones((D,), jnp.float32), 'ln_b': jnp.zeros((D,), jnp.float32), 'Wg': jax.random.normal(ks[2], (D, D), jnp.float32) * s(D), 'bg': jnp.zeros((D,), jnp.float32), 'Wb': jax.random.normal(ks[3], (D, D), jnp.float32) * s(D), 'bb': jnp.zeros((D,), jnp.float32), 'Wqkv': jax.random.normal(ks[4], (3 * D, D), jnp.float32) * s(D), 'bqkv': jnp.zeros((3 * D,), jnp.float32), 'Wp': jax.random.normal(ks[5], (D, D), jnp.float32) * s(D), 'bp': jnp.zeros((D,), jnp.float32), 'W1': jax.random.normal(ks[6], (F, D), jnp.float32) * s(D), 'b1': jnp.zeros((F,), jnp.float32), 'W2': jax.random.normal(ks[7], (D, F), jnp.float32) * s(F), 'b2': jnp.zeros((D,), jnp.float32), 'num_heads': 16}
        return inp
    _L3_cond_all = _L3_cond_setup()
    _L3_cond_in = {k: v for k, v in _L3_cond_all.items() if k in ('ln_g', 'ln_b', 'Wg', 'bg', 'Wb', 'bb', 'Wqkv', 'bqkv', 'Wp', 'bp', 'W1', 'b1', 'W2', 'b2')}
    del _L3_cond_all
    return {'x': x, 'cond_1024': cond_1024, 'L0_cond_Wm': _L0_cond_in['Wm'], 'L0_cond_bm': _L0_cond_in['bm'], 'L0_cond_Lam_re': _L0_cond_in['Lam_re'], 'L0_cond_Lam_im': _L0_cond_in['Lam_im'], 'L0_cond_B_re': _L0_cond_in['B_re'], 'L0_cond_B_im': _L0_cond_in['B_im'], 'L0_cond_C_re': _L0_cond_in['C_re'], 'L0_cond_C_im': _L0_cond_in['C_im'], 'L0_cond_D_diag': _L0_cond_in['D_diag'], 'L0_cond_log_step': _L0_cond_in['log_step'], 'L0_cond_Wc': _L0_cond_in['Wc'], 'L0_cond_bc': _L0_cond_in['bc'], 'L0_cond_W1': _L0_cond_in['W1'], 'L0_cond_b1': _L0_cond_in['b1'], 'L0_cond_W2': _L0_cond_in['W2'], 'L0_cond_b2': _L0_cond_in['b2'], 'L1_cond_norm1_w': _L1_cond_in['norm1_w'], 'L1_cond_film1_w': _L1_cond_in['film1_w'], 'L1_cond_film1_b': _L1_cond_in['film1_b'], 'L1_cond_q_w': _L1_cond_in['q_w'], 'L1_cond_q_b': _L1_cond_in['q_b'], 'L1_cond_k_w': _L1_cond_in['k_w'], 'L1_cond_k_b': _L1_cond_in['k_b'], 'L1_cond_v_w': _L1_cond_in['v_w'], 'L1_cond_v_b': _L1_cond_in['v_b'], 'L1_cond_proj_w': _L1_cond_in['proj_w'], 'L1_cond_proj_b': _L1_cond_in['proj_b'], 'L1_cond_norm2_w': _L1_cond_in['norm2_w'], 'L1_cond_film2_w': _L1_cond_in['film2_w'], 'L1_cond_film2_b': _L1_cond_in['film2_b'], 'L1_cond_mlp_w1': _L1_cond_in['mlp_w1'], 'L1_cond_mlp_b1': _L1_cond_in['mlp_b1'], 'L1_cond_mlp_w2': _L1_cond_in['mlp_w2'], 'L1_cond_mlp_b2': _L1_cond_in['mlp_b2'], 'L2_cond_ln_g': _L2_cond_in['ln_g'], 'L2_cond_ln_b': _L2_cond_in['ln_b'], 'L2_cond_W1': _L2_cond_in['W1'], 'L2_cond_b1': _L2_cond_in['b1'], 'L2_cond_W2': _L2_cond_in['W2'], 'L2_cond_b2': _L2_cond_in['b2'], 'L3_cond_ln_g': _L3_cond_in['ln_g'], 'L3_cond_ln_b': _L3_cond_in['ln_b'], 'L3_cond_Wg': _L3_cond_in['Wg'], 'L3_cond_bg': _L3_cond_in['bg'], 'L3_cond_Wb': _L3_cond_in['Wb'], 'L3_cond_bb': _L3_cond_in['bb'], 'L3_cond_Wqkv': _L3_cond_in['Wqkv'], 'L3_cond_bqkv': _L3_cond_in['bqkv'], 'L3_cond_Wp': _L3_cond_in['Wp'], 'L3_cond_bp': _L3_cond_in['bp'], 'L3_cond_W1': _L3_cond_in['W1'], 'L3_cond_b1': _L3_cond_in['b1'], 'L3_cond_W2': _L3_cond_in['W2'], 'L3_cond_b2': _L3_cond_in['b2']}

def reference(x, cond_1024, L0_cond_Wm, L0_cond_bm, L0_cond_Lam_re, L0_cond_Lam_im, L0_cond_B_re, L0_cond_B_im, L0_cond_C_re, L0_cond_C_im, L0_cond_D_diag, L0_cond_log_step, L0_cond_Wc, L0_cond_bc, L0_cond_W1, L0_cond_b1, L0_cond_W2, L0_cond_b2, L1_cond_norm1_w, L1_cond_film1_w, L1_cond_film1_b, L1_cond_q_w, L1_cond_q_b, L1_cond_k_w, L1_cond_k_b, L1_cond_v_w, L1_cond_v_b, L1_cond_proj_w, L1_cond_proj_b, L1_cond_norm2_w, L1_cond_film2_w, L1_cond_film2_b, L1_cond_mlp_w1, L1_cond_mlp_b1, L1_cond_mlp_w2, L1_cond_mlp_b2, L2_cond_ln_g, L2_cond_ln_b, L2_cond_W1, L2_cond_b1, L2_cond_W2, L2_cond_b2, L3_cond_ln_g, L3_cond_ln_b, L3_cond_Wg, L3_cond_bg, L3_cond_Wb, L3_cond_bb, L3_cond_Wqkv, L3_cond_bqkv, L3_cond_Wp, L3_cond_bp, L3_cond_W1, L3_cond_b1, L3_cond_W2, L3_cond_b2):
    import jax
    import jax.numpy as jnp

    def _L0_cond_ref(y, t, Wm, bm, Lam_re, Lam_im, B_re, B_im, C_re, C_im, D_diag, log_step, Wc, bc, W1, b1, W2, b2):
        import jax, jax.numpy as jnp
        import numpy as np
        B, L, D, P = (8, 512, 256, 64)

        def _ln(x):
            m = x.mean(-1, keepdims=True)
            v = x.var(-1, keepdims=True)
            return (x - m) * jax.lax.rsqrt(v + 1e-05)

        def _s5(u, Lam_re, Lam_im, B_re, B_im, C_re, C_im, D_diag, log_step):
            Lam = Lam_re + 1j * Lam_im
            dt = jnp.exp(log_step)
            Lam_bar = jnp.exp(Lam * dt)
            Bc = B_re + 1j * B_im
            B_bar = ((Lam_bar - 1.0) / Lam)[:, None] * Bc
            Bu = jnp.einsum('bld,pd->blp', u.astype(B_bar.dtype), B_bar)
            A = jnp.broadcast_to(Lam_bar, Bu.shape)

            def binop(e1, e2):
                a1, b1 = e1
                a2, b2 = e2
                return (a1 * a2, a2 * b1 + b2)
            _, xs = jax.lax.associative_scan(binop, (A, Bu), axis=1)
            Cc = C_re + 1j * C_im
            return 2.0 * jnp.einsum('blp,dp->bld', xs, Cc).real + D_diag * u
        mod = t @ Wm + bm
        shift_a, scale_a, gate_a, shift_ff, scale_ff, gate_ff = jnp.split(mod, 6, axis=-1)
        y_mod = _ln(y) * (1 + scale_a[:, None]) + shift_a[:, None]
        a_y = _s5(y_mod, Lam_re, Lam_im, B_re, B_im, C_re, C_im, D_diag, log_step)
        y = y + gate_a[:, None] * a_y
        cond = t @ Wc + bc
        scale_c, shift_c = jnp.split(cond, 2, axis=-1)
        y_norm = _ln(y) * (1 + scale_c[:, None]) + shift_c[:, None]
        y_mod = y_norm * (1 + scale_ff[:, None]) + shift_ff[:, None]
        h = jax.nn.gelu(y_mod @ W1 + b1)
        ff_y = h @ W2 + b2
        return y + gate_ff[:, None] * ff_y

    def _L1_cond_ref(x, cond, norm1_w, film1_w, film1_b, q_w, q_b, k_w, k_b, v_w, v_b, proj_w, proj_b, norm2_w, film2_w, film2_b, mlp_w1, mlp_b1, mlp_w2, mlp_b2):
        import jax, jax.numpy as jnp
        import numpy as np
        DIM = 256
        MLP_RATIO = 4
        EPS = 1e-06

        def rmsnorm(x, w):
            return x * jax.lax.rsqrt(jnp.mean(x * x, axis=-1, keepdims=True) + EPS) * w

        def film(x, cond, w, b):
            ss = cond @ w + b
            scale, shift = jnp.split(ss, 2, axis=-1)
            return x * (1.0 + scale[:, None, :]) + shift[:, None, :]
        B, N, D = x.shape
        x_in = x
        h = film(rmsnorm(x, norm1_w), cond, film1_w, film1_b)
        Q = h @ q_w + q_b
        K = h @ k_w + k_b
        V = h @ v_w + v_b
        scores = jnp.einsum('bnd,bmd->bnm', Q, K) * D ** (-0.5)
        attn = jax.nn.softmax(scores, axis=-1)
        out = jnp.einsum('bnm,bmd->bnd', attn, V)
        x = x_in + (out @ proj_w + proj_b)
        x_in = x
        h = film(rmsnorm(x, norm2_w), cond, film2_w, film2_b)
        h = jax.nn.gelu(h @ mlp_w1 + mlp_b1, approximate=False) @ mlp_w2 + mlp_b2
        return x_in + h

    def _L2_cond_ref(x, ada_emb, ln_g, ln_b, W1, b1, W2, b2):
        import jax, jax.numpy as jnp
        import numpy as np
        FEAT = 256
        ADA = 256
        INTER = 256
        RANK = 8
        EPS = 1e-05

        def _layernorm(a, g, b):
            mu = jnp.mean(a, axis=-1, keepdims=True)
            var = jnp.mean(jnp.square(a - mu), axis=-1, keepdims=True)
            return (a - mu) * jax.lax.rsqrt(var + EPS) * g + b
        B, T, D = x.shape
        h = jax.nn.gelu(_layernorm(ada_emb, ln_g, ln_b) @ W1 + b1, approximate=False)
        w = h @ W2 + b2
        a1, bb1, a2, bb2 = jnp.split(w, 4, axis=-1)
        a1 = a1.reshape(B, D, RANK)
        bb1 = bb1.reshape(B, D, RANK)
        a2 = a2.reshape(B, D, RANK)
        bb2 = bb2.reshape(B, D, RANK)
        y = jnp.einsum('btd,bdr->btr', x, a1)
        y = jnp.einsum('btr,bdr->btd', y, bb1)
        y = jax.nn.gelu(y, approximate=False)
        y = jnp.einsum('btd,bdr->btr', y, a2)
        y = jnp.einsum('btr,bdr->btd', y, bb2)
        return y + x

    def _L3_cond_ref(hidden, w, ln_g, ln_b, Wg, bg, Wb, bb, Wqkv, bqkv, Wp, bp, W1, b1, W2, b2, num_heads):
        import jax, jax.numpy as jnp
        import numpy as np
        EPS = 1e-05

        def _sln(h, w, ln_g, ln_b, Wg, bg, Wb, bb):
            mu = jnp.mean(h, axis=-1, keepdims=True)
            var = jnp.mean((h - mu) ** 2, axis=-1, keepdims=True)
            ln = (h - mu) / jnp.sqrt(var + EPS) * ln_g + ln_b
            gamma = (w @ Wg.T + bg)[:, None, :]
            beta = (w @ Wb.T + bb)[:, None, :]
            return gamma * ln + beta
        B, N, D = hidden.shape
        hd = D // num_heads
        h = _sln(hidden, w, ln_g, ln_b, Wg, bg, Wb, bb)
        qkv = (h @ Wqkv.T + bqkv).reshape(B, N, num_heads, hd, 3)
        q = jnp.moveaxis(qkv[..., 0], 2, 1)
        k = jnp.moveaxis(qkv[..., 1], 2, 1)
        v = jnp.moveaxis(qkv[..., 2], 2, 1)
        energy = jnp.einsum('bhqd,bhkd->bhqk', q, k)
        att = jax.nn.softmax(energy, axis=-1) / D ** 0.5
        out = jnp.einsum('bhqk,bhkd->bhqd', att, v)
        out = jnp.moveaxis(out, 1, 2).reshape(B, N, D)
        out = out @ Wp.T + bp
        h1 = out + hidden
        h2 = _sln(h1, w, ln_g, ln_b, Wg, bg, Wb, bb)
        return h2 + h1
    x = _L0_cond_ref(x, cond_1024, L0_cond_Wm, L0_cond_bm, L0_cond_Lam_re, L0_cond_Lam_im, L0_cond_B_re, L0_cond_B_im, L0_cond_C_re, L0_cond_C_im, L0_cond_D_diag, L0_cond_log_step, L0_cond_Wc, L0_cond_bc, L0_cond_W1, L0_cond_b1, L0_cond_W2, L0_cond_b2)
    x = _L1_cond_ref(x, cond_1024, L1_cond_norm1_w, L1_cond_film1_w, L1_cond_film1_b, L1_cond_q_w, L1_cond_q_b, L1_cond_k_w, L1_cond_k_b, L1_cond_v_w, L1_cond_v_b, L1_cond_proj_w, L1_cond_proj_b, L1_cond_norm2_w, L1_cond_film2_w, L1_cond_film2_b, L1_cond_mlp_w1, L1_cond_mlp_b1, L1_cond_mlp_w2, L1_cond_mlp_b2)
    x = _L2_cond_ref(x, cond_1024, L2_cond_ln_g, L2_cond_ln_b, L2_cond_W1, L2_cond_b1, L2_cond_W2, L2_cond_b2)
    x = _L3_cond_ref(x, cond_1024, L3_cond_ln_g, L3_cond_ln_b, L3_cond_Wg, L3_cond_bg, L3_cond_Wb, L3_cond_bb, L3_cond_Wqkv, L3_cond_bqkv, L3_cond_Wp, L3_cond_bp, L3_cond_W1, L3_cond_b1, L3_cond_W2, L3_cond_b2, 16)
    return x

_drawn_inputs = setup_inputs


def setup_inputs(seed=0):
    import zlib

    import numpy as np

    out = dict(_drawn_inputs(seed))
    spreads = {'L0_cond_Lam_re': (-0.5, 0.6),
     'L0_cond_b1': (0.0, 0.8),
     'L0_cond_b2': (0.0, 0.295),
     'L1_cond_norm1_w': (1.0, 0.2),
     'L1_cond_film1_b': (0.0, 0.1),
     'L1_cond_q_b': (0.0, 0.401),
     'L1_cond_k_b': (0.0, 2.0),
     'L1_cond_v_b': (0.0, 0.1),
     'L1_cond_proj_b': (0.0, 0.1),
     'L1_cond_norm2_w': (1.0, 0.2),
     'L1_cond_film2_b': (0.0, 0.1),
     'L1_cond_mlp_b1': (0.0, 0.272),
     'L1_cond_mlp_b2': (0.0, 0.1),
     'L2_cond_ln_g': (1.0, 0.2),
     'L2_cond_ln_b': (0.0, 0.272),
     'L2_cond_b1': (0.0, 0.275),
     'L2_cond_b2': (0.0, 0.1),
     'L3_cond_ln_g': (1.0, 0.2),
     'L3_cond_ln_b': (0.0, 0.1),
     'L3_cond_bg': (0.0, 0.1),
     'L3_cond_bb': (0.0, 0.1),
     'L3_cond_bqkv': (0.0, 2.0),
     'L3_cond_bp': (0.0, 0.1),
     'L3_cond_b1': (0.0, 0.1),
     'L3_cond_b2': (0.0, 0.1)}
    factors = {'L0_cond_bm': 2.907,
     'L0_cond_Wc': 6.985,
     'L0_cond_bc': 8.0,
     'L0_cond_W1': 3.369,
     'L0_cond_W2': 2.845}
    for name, (base, spread) in spreads.items():
        noise = np.random.default_rng([zlib.crc32(name.encode()), seed]).standard_normal(out[name].shape)
        drawn = base * np.exp(spread * noise) if base else spread * noise
        out[name] = jnp.asarray(drawn.astype(out[name].dtype))
    for name, factor in factors.items():
        out[name] = (out[name] * factor).astype(out[name].dtype)
    return out
```

```python
from contextlib import ExitStack

import numpy as np
import concourse.bass as bass
from concourse import mybir

F32 = mybir.dt.float32
BF16 = mybir.dt.bfloat16
I32 = mybir.dt.int32
ALU = mybir.AluOpType
ACT = mybir.ActivationFunctionType
AX_X = mybir.AxisListType.X

P = 128
B, T, D = 2, 1024, 256
KB = D // P
NT = T // P
HALF = 512
NC = T // HALF
TPC = HALF // P
FF = 4 * D
NF = FF // P
S5 = 64
HEADS, HD = 16, 16
GH = 4
NG = HEADS // GH
RANK = 8
LR = 4 * RANK * D
PAIRS = [(0, 0), (0, 1), (1, 0), (1, 1), (0, 2), (2, 0)]
NPAIR = len(PAIRS)
UNIT = GH * TPC
NUNIT = NG * NC
LEAD = UNIT + 8
KSTK = NPAIR * HD
NPART = 3
KFULL = KSTK + NPART

CW = dict(shift_a=0, scale_a=2, gate_a=4, shift_ff=6, scale_ff=8, gate_ff=10, scale_c=12, shift_c=14,
          f1_scale=16, f1_shift=18, f2_scale=20, f2_shift=22, gamma=24, beta=26)
NCB = 28
NCOND = NCB * P
PU, PM, P1, P2, P3 = range(0, 10, 2)
NPAR = 10
VC = dict(norm1=0, norm2=2, ln3_g=4, ln3_b=6, q_b=8, k_b=10, q3_b=12, k3_b=14, D=16, b1=18, mb1=26,
          lam_re=34, lam_im=35, log_step=36)
NVC = 37
BV, BP, MB2, BV3, BP3, B20 = range(6)
GA, GF, S3, B3 = range(4)


def norm_jobs(tag):
    return [(tag, h, k) for h in range(NC) for k in range(KB)]


def act_jobs():
    jobs = norm_jobs("u") + norm_jobs("m")
    jobs += [("h0", c, f) for c in range(NC) for f in range(NF)]
    jobs += norm_jobs("n1") + [(w, c, k) for w in "qk" for c in range(NC) for k in range(KB)]
    for c in range(NC):
        jobs += [("p", c * TPC + t, s) for t in range(TPC) for s in range(2)]
        jobs += [("o", c, k) for k in range(KB)]
    jobs += norm_jobs("n2") + [("h1", c, f) for c in range(NC) for f in range(NF)]
    jobs += norm_jobs("x2") + [("g", c, k) for c in range(NC) for k in range(KB)]
    jobs += norm_jobs("n3") + [(w, c, k) for k in range(KB) for w in ("q3", "k3") for c in range(NC)]
    jobs += norm_jobs("ot")
    return {j: n for n, j in enumerate(jobs)}


def dve_jobs():
    two = NT // 2
    jobs = [("bu", c, s) for c in range(NC) for s in range(2)]
    jobs += [("y0", j) for j in range(two)] + [("w20", j) for j in range(two)]
    jobs += [("v1", j) for j in range(two)] + [("pr", j) for j in range(two)] + [("w21", j) for j in range(two)]
    jobs += [("a1", c) for c in range(NC)] + [("a2", c) for c in range(NC)] + [("f2", j) for j in range(two)]
    jobs += [("v3", j) for j in range(two)] + [("p3", j) for j in range(two)]
    return {j: n for n, j in enumerate(jobs)}


def build(nc, I, out):
    AJ, DJ = act_jobs(), dve_jobs()
    ctx = ExitStack()
    with ctx:
        def sb(name, shape, dt=F32):
            return ctx.enter_context(nc.sbuf_tensor(name, shape, dt))

        def sem(name):
            return ctx.enter_context(nc.semaphore(name))

        X = sb("X", [P, NT, D])
        XN = sb("XN", [P, NT, D])
        XT = sb("XT", [P, KB, T])
        W1 = sb("W1", [P, KB, FF])
        W2 = sb("W2", [P, NF, D])
        WA = sb("WA", [P, 4, KB, D])
        WQ3 = sb("WQ3", [P, 3, KB, D])
        WP3 = sb("WP3", [P, KB, D])
        C2 = sb("C2", [P, T])
        S2 = sb("S2", [P, T])
        BA = sb("BA", [P, 2, KB, P])
        CT = sb("CT", [P, 2, D])
        CG = sb("CG", [P, 2, D])
        DG = sb("DG", [P, KB, P])
        BC = sb("BC", [P, 6, D])
        GB = sb("GB", [P, B, 4, D])
        VEC = sb("VEC", [P, NVC])
        PAR = sb("PAR", [P, B, NPAR * KB])
        CUR = sb("CUR", [P, NPAR * KB])
        LA = sb("LA", [P, B, 2, KB, RANK])
        LB = sb("LB", [RANK, B, 2, D])
        LAC = sb("LAC", [P, 2, KB, RANK])
        LBC = sb("LBC", [RANK, 2, D])
        ident = sb("ident", [P, P])
        identb = sb("identb", [P, P], BF16)
        SEL = sb("SEL", [B, B, P])
        BG = sb("BG", [P, D])
        ST = sb("ST", [P, NT, 6])
        MV = sb("MV", [P, NT, 2])
        VE = sb("VE", [P, NT])
        RST = sb("RST", [P, NT])
        MHALF = sb("MHALF", [P, NT])
        NM = sb("NM", [P, NT])
        NMS = sb("NMS", [P, NT])
        SM = sb("SM", [P, NT])
        RSM = sb("RSM", [P, NT])
        RVEC = sb("RVEC", [P, 1])
        SG = sb("SG", [P, 2])
        TM = sb("TM", [P, 24])
        TI = sb("TI", [P, 1], I32)
        NMX = sb("NMX", [P, 2, UNIT])
        NMR = sb("NMR", [P, UNIT])
        NMP = sb("NMP", [P, NPART, UNIT], BF16)
        NMT = sb("NMT", [NPART * UNIT, P], BF16)
        RC = sb("RC", [P, TPC * GH])
        UO = sb("UO", [P, HALF])
        R1 = sb("R1", [P, 16384])
        R2 = sb("R2", [P, 11264])

        HT = R1[:, 0:8192].rearrange("p (f t) -> p f t", f=NF)
        PT = R1[:, 0:4096].rearrange("p (k q) -> p k q", k=NT)
        QT = R1[:, 8192:10240].rearrange("p (k t) -> p k t", k=KB)
        KT = R1[:, 10240:12288].rearrange("p (k t) -> p k t", k=KB)
        V = R1[:, 12288:14336].rearrange("p (t d) -> p t d", t=NT)
        Y8 = R1[0:RANK, 14336:16384].rearrange("p (s t) -> p s t", s=2)
        OT = XN[:, :, :].rearrange("p t d -> p (t d)").rearrange("p (k t) -> p k t", k=KB)
        PX = XT[:, :, :]
        QS = R1[0:KFULL, 0:8192].bitcast(BF16).rearrange("p (c h q) -> p c h q", c=NC, h=HEADS)
        KS = R1[0:KFULL, 8192:16384].bitcast(BF16).rearrange("p (h t) -> p h t", h=HEADS)
        T1 = R2[:, 0:1024]
        T2 = R2[:, 1024:2048]
        Z = R2[:, 2048:3072]
        ZC = R2[:, 3072:4096]
        ZS = R2[:, 4096:5120]
        PQ = R2[:, 0:3072].bitcast(BF16).rearrange("p (s k t) -> p s k t", s=NPART, k=KB)
        PK = R2[:, 3072:6144].bitcast(BF16).rearrange("p (s k t) -> p s k t", s=NPART, k=KB)
        PB = R2[:, 0:4096].rearrange("p (s j q) -> p s j q", s=2, j=GH)
        O = R2[:, 4096:6144].rearrange("p (t d) -> p t d", t=NT)
        VP = R2[:, 6144:10240].rearrange("p (t h c) -> p t h c", t=NT, h=HEADS)
        QF = XN[:, :, :].rearrange("p t d -> p (t d)").rearrange("p (s q) -> p s q", s=4)
        RP = R2[:, 10240:11264].rearrange("p (s q) -> p s q", s=2)
        WC = R2[:, 0:KB * NCOND].rearrange("p (k n) -> p k n", k=KB)
        W2L = R2[:, KB * NCOND:KB * NCOND + 4096].rearrange("p (s k n) -> p s k n", s=2, k=KB)
        L2W1 = R1[:, 15360:15872].rearrange("p (k n) -> p k n", k=KB)
        ROWS = R1[0:B, 0:NCOND]
        WR = R1[0:B, 3584:3584 + LR]
        LNR = R1[0:B, 11776:11776 + 5 * D].rearrange("p (s d) -> p s d", s=5)
        TR = R1[0:B, 13056:13056 + 6 * D].rearrange("p (s d) -> p s d", s=6)
        BX = XN[:, 0:4, :]
        COLR = XT[:, 0, 0:NCB * B].rearrange("p (n b) -> p n b", b=B)
        CTX = XT[:, 1, 0:3 * KB * B].rearrange("p (s k b) -> p s k b", s=3, b=B)

        PA = ctx.enter_context(nc.psum_tensor("PA", [P, 4, HALF], F32))
        PD = ctx.enter_context(nc.psum_tensor("PD", [P, 4, HALF], F32))
        PDF = PD[:, :, :].rearrange("p s q -> p (s q)").rearrange("p (s q) -> p s q", s=2)
        PTB = PA[:, 3, 0:64].bitcast(BF16)

        DR = nc.dram_tensor("qk_parts", [2, NPART, KB, P, T], BF16, kind="Internal").ap()

        s_in_a = sem("setup_in_a")
        s_in_b = sem("setup_in_b")
        s_l2in = [sem("l2w_in0"), sem("l2w_in1")]
        s_const = sem("constants_ready")
        s_cfull = sem("row_bank_full")
        s_cev = sem("row_bank_evacuated")
        s_ada_st = sem("ada_stats")
        s_ada_rs = sem("ada_rstd")
        s_ada = sem("ada_rows_ready")
        s_small = sem("small_bank_full")
        s_ctx = sem("small_bank_copied")
        s_hid = sem("hidden_row_ready")
        s_gelu = sem("hidden_gelu_ready")
        s_ang = sem("angles_ready")
        s_trig = sem("trig_ready")
        s_sb = sem("film_rows_ready")
        s_bx = sem("state_maps_ready")
        s_gb = sem("row_broadcasts_ready")
        s_spread = sem("lowrank_spread")
        s_vp = sem("v_padding_ready")
        s_link0 = sem("setup_dve_step")
        s_xin = [sem(f"x_in{c}") for c in range(NC)]
        s_w1in = [sem("w1_layer0_in"), sem("w1_layer1_in")]
        s_w2in = [sem("w2_layer0_in"), sem("w2_layer1_in")]
        s_afull = sem("act_bank_full")
        s_aev = sem("act_bank_evacuated")
        s_dfull = sem("dve_bank_full")
        s_dev = sem("dve_bank_evacuated")
        s_dstep = sem("dve_step")
        s_gstep = sem("pool_step")
        s_stats = sem("stats_ready")
        s_rstd = sem("rstd_ready")
        s_xn = sem("xn_ready")
        s_pre = sem("bias_added")
        s_par = sem("batch_params_ready")
        s_w2g = sem("gated_w2_ready")
        s_z = sem("states_ready")
        s_zc = sem("states_cos_ready")
        s_zs = sem("states_sin_ready")
        s_up = sem("mlp_up_done")
        s_down = sem("mlp_down_done")
        s_sfull = sem("scores_full")
        s_max1 = sem("scores_max")
        s_nmax = sem("negmax_ready")
        s_exp1 = sem("probs1_ready")
        s_qk = sem("qk_float32_ready")
        s_parts = sem("qk_parts_ready")
        s_ones = sem("ones_rows_ready")
        s_spill = [sem(f"parts_stored{n}") for n in range(4)]
        s_stack = [sem(f"group_stack_in{g}") for g in range(NG)]
        s_mfull = sem("maxpass_full")
        s_mred = sem("maxpass_reduced")
        s_nmp = sem("negmax_parts")
        s_nmtf = sem("negmax_t_full")
        s_nmt = sem("negmax_t_ready")
        s_nmrow = [sem(f"negmax_rows{m}") for m in range(NUNIT)]
        s_efull = sem("energy_full")
        s_exp3 = sem("probs3_ready")
        s_pv = sem("pv_done")
        s_uo = sem("heads_out_copied")
        s_ut = sem("heads_out_t_full")
        s_on = sem("heads_out_normed")
        s_scaled = sem("out_scaled")
        s_fin = sem("out_ready")
        s_out = sem("out_stored")
        s_end = sem("batch_ended")
        s_go = {e: sem(f"go_{e}") for e in ("pe", "act", "dve", "pool")}
        per_batch = [*s_xin, *s_w1in, *s_w2in, s_afull, s_aev, s_dfull, s_dev, s_dstep, s_gstep, s_stats, s_rstd,
                     s_xn, s_pre, s_par, s_w2g, s_z, s_zc, s_zs, s_up, s_down, s_sfull, s_max1, s_nmax, s_exp1, s_qk,
                     s_parts, s_ones, *s_spill, *s_stack, s_mfull, s_mred, s_nmp, s_nmtf, s_nmt, *s_nmrow,
                     s_efull, s_exp3, s_pv, s_uo, s_ut, s_on, s_scaled, s_fin, s_out, s_end]

        N_IN_A, N_IN_B = 9, 6
        LCH = 1024
        NLCH = LR // LCH
        NROWJ = NCOND // HALF
        NLJ = LR // HALF
        NSTEP = NUNIT * NT

        def turn_step(m):
            return (UNIT * (m + 1) - LEAD) // 2

        block = ctx.enter_context(nc.Block())

        def begin(e, name):
            e.wait_ge(s_go[name], 1)
            e.sem_clear(s_go[name])

        @block.sync
        def _(sp):
            def kp(a):
                return a.rearrange("(k p) n -> p k n", p=P)

            sp.dma_start(TR[:, 0, :], I["t"]).then_inc(s_in_a, 16)
            sp.dma_start(LNR[:, :, :], I["lnrow"].partition_broadcast(B)).then_inc(s_in_a, 16)
            sp.dma_start(CTX[:, 0, :, :], I["tT"]).then_inc(s_in_a, 16)
            sp.dma_start(VEC[:, :], I["vec"]).then_inc(s_in_a, 16)
            sp.dma_start(WC, kp(I["wcond"])).then_inc(s_in_a, 16)
            sp.dma_start(ROWS, I["bcond"].partition_broadcast(B)).then_inc(s_in_a, 16)
            sp.dma_start(WR, I["l2_b2"].partition_broadcast(B)).then_inc(s_in_a, 16)
            sp.dma_start(L2W1, kp(I["l2_w1"])).then_inc(s_in_a, 16)
            sp.dma_start(BX[:, 0:2, :], I["b2x"]).then_inc(s_in_a, 16)
            for n in range(NLCH):
                if n >= 2:
                    sp.wait_ge(s_cfull, NROWJ + 2 * (n - 1))
                sp.dma_start(W2L[:, n % 2], kp(I["l2_w2"])[:, :, n * LCH:(n + 1) * LCH]).then_inc(s_l2in[n % 2], 16)
            sp.dma_start(CT[:, :, :], I["ct"]).then_inc(s_in_b, 16)
            sp.dma_start(BC[:, :, :], I["bc"].partition_broadcast(P)).then_inc(s_in_b, 16)
            for w in range(2):
                sp.dma_start(WA[:, 2 * w:2 * w + 2], I["wa"][:, 2 * w:2 * w + 2]).then_inc(s_in_b, 16)
            sp.dma_start(WQ3[:, :, :, :], I["wqkv3"]).then_inc(s_in_b, 16)
            sp.dma_start(WP3[:, :, :], kp(I["wp3"])).then_inc(s_in_b, 16)
            sp.wait_ge(s_cev, NROWJ + NLJ)
            for b in range(B):
                for s in range(2):
                    for k in range(KB):
                        o = s * RANK * D + k * P * RANK
                        sp.dma_start(LA[:, b, s, k, :],
                                     WR[b:b + 1, o:o + P * RANK].rearrange("a (p r) -> a p r", r=RANK)).then_inc(s_spread, 16)
                    o = (2 + s) * RANK * D
                    sp.dma_start(LB[:, b, s, :],
                                 WR[b:b + 1, o:o + D * RANK].rearrange("a (r d) -> a r d", d=D)).then_inc(s_spread, 16)
            sp.wait_ge(s_spread, 16 * 2 * B * (KB + 1))
            sp.wait_ge(s_in_b, 16 * N_IN_B)
            sp.wait_ge(s_vp, 2)
            for e in s_go:
                sp.sem_inc(s_go[e], 1)
            with sp.Fori(0, B) as b:
                for c in range(NC):
                    sp.dma_start(X[:, c * TPC:(c + 1) * TPC, :],
                                 I["x"][b, c * HALF:(c + 1) * HALF, :].rearrange("(t p) d -> p t d", p=P)).then_inc(s_xin[c], 16)
                sp.dma_start(W1[:, :, :], kp(I["w1_0"])).then_inc(s_w1in[0], 16)
                sp.dma_start(W2[:, :, :], kp(I["w2_0"])).then_inc(s_w2in[0], 16)
                sp.wait_ge(s_up, 1)
                sp.dma_start(W1[:, :, :], kp(I["w1_1"])).then_inc(s_w1in[1], 16)
                sp.wait_ge(s_down, 1)
                sp.dma_start(W2[:, :, :], kp(I["w2_1"])).then_inc(s_w2in[1], 16)
                for k in range(KB):
                    for side, src in enumerate((PQ, PK)):
                        n = 2 * k + side
                        sp.wait_ge(s_parts, NC * (n + 1))
                        sp.dma_start(DR[side, :, k, :, :].rearrange("s p t -> p s t"), src[:, :, k, :]).then_inc(s_spill[n], 16)
                    for g in range(NG // KB * k, NG // KB * (k + 1)):
                        for side in range(2):
                            sp.wait_ge(s_spill[2 * k + side], 16)
                            for n, pair in enumerate(PAIRS):
                                r = (g * GH * HD) % P
                                src = DR[side, pair[side], k, r:r + GH * HD, :].rearrange("(h d) t -> d h t", d=HD)
                                rows, heads = slice(n * HD, (n + 1) * HD), slice(g * GH, (g + 1) * GH)
                                if side:
                                    sp.dma_start(KS[rows, heads, :], src).then_inc(s_stack[g], 16)
                                else:
                                    for c in range(NC):
                                        sp.dma_start(QS[rows, c, heads, :],
                                                     src[:, :, c * HALF:(c + 1) * HALF]).then_inc(s_stack[g], 16)
                for m in range(NUNIT):
                    g, c = divmod(m, NC)
                    sp.wait_ge(s_nmt, m + 1)
                    for s in range(NPART):
                        sp.dma_start(QS[KSTK + s:KSTK + s + 1, c, g * GH:(g + 1) * GH, :],
                                     NMT[s * UNIT:(s + 1) * UNIT, :]).then_inc(s_nmrow[m], 16)
                for c in range(NC):
                    sp.wait_ge(s_fin, c + 1)
                    sp.dma_start(out[b, c * HALF:(c + 1) * HALF, :].rearrange("(t p) d -> p t d", p=P),
                                 XN[:, c * TPC:(c + 1) * TPC, :]).then_inc(s_out, 16)
                sp.wait_ge(s_out, 16 * NC)
                sp.wait_ge(s_end, 4)
                for s in per_batch:
                    sp.sem_clear(s)
                for e in s_go:
                    sp.sem_inc(s_go[e], 1)

        @block.gpsimd
        def _(po):
            po.memset(ident[:, :], 0.0).then_inc(s_const, 1)
            po.memset(SEL[:, :, :], 0.0).then_inc(s_const, 1)
            po.memset(MHALF[:, :], -0.5).then_inc(s_const, 1)
            po.wait_ge(s_const, 3)
            po.affine_select(out=ident[:, :], in_=ident[:, :], compare_op=ALU.not_equal, fill=1.0, base=0,
                             pattern=[[-1, P]], channel_multiplier=1).then_inc(s_const, 1)
            po.affine_select(out=SEL[:, :, :], in_=SEL[:, :, :], compare_op=ALU.not_equal, fill=1.0, base=0,
                             pattern=[[-1, B], [0, P]], channel_multiplier=1).then_inc(s_const, 1)
            po.wait_ge(s_const, 5)
            po.tensor_copy(identb[:, :], ident[:, :]).then_inc(s_const, 1)
            po.wait_ge(s_ada_st, 1)
            po.tensor_scalar(VE[0:B, 0:1], MV[0:B, 0, 1:2], 1e-5, None, ALU.add).then_inc(s_ada_rs, 1)
            po.wait_ge(s_ada_rs, 1)
            po.tensor_tensor(RST[0:B, 0:1], VE[0:B, 0:1], MHALF[0:B, 0:1], ALU.pow).then_inc(s_ada_rs, 1)
            po.wait_ge(s_cfull, NROWJ + NLJ)
            po.memset(VP[:, :, :, HD:2 * HD], 0.0).then_inc(s_vp, 1)
            po.wait_ge(s_vp, 1)
            po.memset(VP[:, :, :, HD:HD + 1], float(D) ** 0.5).then_inc(s_vp, 1)
            with po.Fori(0, B) as b:
                begin(po, "pool")
                cnt = dict(g=0, st=0, xn=0)

                def link(i):
                    cnt["g"] += 1
                    i.then_inc(s_gstep, 1)
                    po.wait_ge(s_gstep, cnt["g"])

                def rstd(eps, rms=False):
                    for h in range(NC):
                        cnt["st"] += 1
                        po.wait_ge(s_stats, cnt["st"])
                        t = slice(h * TPC, (h + 1) * TPC)
                        if rms:
                            link(po.tensor_tensor(VE[:, t], MV[:, t, 0], MV[:, t, 0], ALU.mult))
                            link(po.tensor_tensor(VE[:, t], VE[:, t], MV[:, t, 1], ALU.add))
                            link(po.tensor_scalar(VE[:, t], VE[:, t], eps, None, ALU.add))
                        else:
                            link(po.tensor_scalar(VE[:, t], MV[:, t, 1], eps, None, ALU.add))
                        po.tensor_tensor(RST[:, t], VE[:, t], MHALF[:, t], ALU.pow).then_inc(s_rstd, 1)

                def prebias(row):
                    for h in range(NC):
                        cnt["xn"] += 1
                        po.wait_ge(s_xn, cnt["xn"])
                        t = slice(h * TPC, (h + 1) * TPC)
                        po.tensor_tensor(X[:, t, :], X[:, t, :], row.unsqueeze(1).to_broadcast([P, TPC, D]),
                                         ALU.add).then_inc(s_pre, 1)

                rstd(1e-5)
                cnt["xn"] += NC
                po.wait_ge(s_w2in[0], 16)
                po.tensor_tensor(W2[:, :, :], W2[:, :, :], GB[:, b, GF, :].unsqueeze(1).to_broadcast([P, NF, D]),
                                 ALU.mult).then_inc(s_w2g, 1)
                for c in range(NC):
                    po.wait_ge(s_z, c + 1)
                    q = slice(c * HALF, (c + 1) * HALF)
                    po.tensor_tensor(ZS[:, q], Z[:, q], S2[:, q], ALU.mult).then_inc(s_zs, 1)
                rstd(1e-5)
                po.wait_ge(s_par, 2)
                prebias(BG[:, :])
                rstd(1e-6, rms=True)
                prebias(BC[:, BP, :])
                rstd(1e-6, rms=True)
                prebias(BC[:, MB2, :])
                rstd(1e-5)
                po.wait_ge(s_aev, AJ[("n3", 1, 1)] + 1)
                po.memset(KS[KSTK:KFULL, :, :], 1.0).then_inc(s_ones, 1)
                po.wait_ge(s_ones, 1)
                prebias(BC[:, BP3, :])
                rstd(1e-5)
                for h in range(NC):
                    po.wait_ge(s_scaled, h + 1)
                    t = slice(h * TPC, (h + 1) * TPC)
                    po.tensor_tensor(X[:, t, :], X[:, t, :], GB[:, b, B3, :].unsqueeze(1).to_broadcast([P, TPC, D]),
                                     ALU.add).then_inc(s_pre, 1)
                po.wait_ge(s_pre, 5 * NC)
                po.sem_inc(s_end, 1)
            begin(po, "pool")

        @block.scalar
        def _(act):
            act.wait_ge(s_hid, 1)
            act.activation(TR[:, 3, :], TR[:, 2, :], ACT.Gelu).then_inc(s_gelu, 1)
            act.wait_ge(s_ang, 1)
            act.activation(TM[:, 8:10], TM[:, 6:8], ACT.Sin).then_inc(s_trig, 1)
            with act.Fori(0, B) as b:
                begin(act, "act")
                seen = [0]

                def bank(job):
                    n = AJ[job]
                    assert n == seen[0], (job, n, seen)
                    seen[0] += 1
                    act.wait_ge(s_afull, n + 1)
                    return PA[:, n % 4, :]

                def par(p, k):
                    return CUR[:, p * KB + k:p * KB + k + 1]

                def vec(name, k=0):
                    return VEC[:, VC[name] + k:VC[name] + k + 1]

                def modulated(tag, p):
                    for h in range(NC):
                        for k in range(KB):
                            act.activation(XT[:, k, h * HALF:(h + 1) * HALF], bank((tag, h, k)), ACT.Identity,
                                           bias=par(p + 1, k), scale=par(p, k)).then_inc(s_aev, 1)

                def hidden(tag, func, bias):
                    for c in range(NC):
                        for f in range(NF):
                            act.activation(HT[:, f, c * HALF:(c + 1) * HALF], bank((tag, c, f)), func,
                                           bias=vec(bias, f)).then_inc(s_aev, 1)

                act.wait_ge(s_par, 1)
                modulated("u", PU)
                modulated("m", PM)
                hidden("h0", ACT.Gelu_apprx_tanh, "b1")
                modulated("n1", P1)
                for name, dst, bias in (("q", QT, "q_b"), ("k", KT, "k_b")):
                    for c in range(NC):
                        for k in range(KB):
                            act.activation(dst[:, k, c * HALF:(c + 1) * HALF], bank((name, c, k)), ACT.Identity,
                                           bias=vec(bias, k)).then_inc(s_aev, 1)

                def probs_turn(t):
                    for s in range(2):
                        act.activation(PT[:, 4 * s:4 * s + 4, (t % TPC) * P:(t % TPC + 1) * P],
                                       bank(("p", t, s)).rearrange("p (k q) -> p k q", k=4),
                                       ACT.Copy).then_inc(s_aev, 1)
                    if t % TPC == TPC - 1:
                        c = t // TPC
                        for k in range(KB):
                            act.activation(OT[:, k, c * HALF:(c + 1) * HALF], bank(("o", c, k)),
                                           ACT.Copy).then_inc(s_aev, 1)

                for t in range(NT):
                    act.wait_ge(s_nmax, t + 1)
                    act.activation(PX[:, t % 2, :], PDF[:, t % 2, :], ACT.Exp, bias=NMS[:, t:t + 1],
                                   scale=float(D) ** -0.5, accum_out=SM[:, t:t + 1]).then_inc(s_exp1, 1)
                    if t >= 1:
                        probs_turn(t - 1)
                probs_turn(NT - 1)
                modulated("n2", P2)
                hidden("h1", ACT.Gelu, "mb1")
                for h in range(NC):
                    for k in range(KB):
                        act.activation(XT[:, k, h * HALF:(h + 1) * HALF], bank(("x2", h, k)), ACT.Copy).then_inc(s_aev, 1)
                for c in range(NC):
                    for k in range(KB):
                        act.activation(QT[:, k, c * HALF:(c + 1) * HALF], bank(("g", c, k)), ACT.Gelu).then_inc(s_aev, 1)
                modulated("n3", P3)
                n = 0
                for k in range(KB):
                    for name in ("q3", "k3"):
                        for c in range(NC):
                            if n >= 4:
                                act.wait_ge(s_parts, n - 3)
                            act.activation(QF[:, n % 4, :], bank((name, c, k)), ACT.Identity,
                                           bias=vec(name + "_b", k)).then_inc(s_aev, 1)
                            n += 1

                def turn_max(m):
                    act.wait_ge(s_nmtf, m + 1)
                    if m >= 1:
                        act.wait_ge(s_nmrow[m - 1], 16 * NPART)
                    act.activation(NMT[:, :], PTB[0:NPART * UNIT, :], ACT.Copy).then_inc(s_nmt, 1)

                def copy_heads_out(m):
                    act.wait_ge(s_pv, (m + 1) * NT)
                    if m >= 1:
                        act.wait_ge(s_ut, m)
                    act.activation(UO[:, :], PA[:, 2, :], ACT.Copy).then_inc(s_uo, 1)

                turn_max(0)
                for k in range(2 * KB):
                    act.wait_ge(s_spill[k], 16)
                for step in range(NSTEP):
                    m, kt = divmod(step, NT)
                    if step >= 2:
                        act.wait_ge(s_pv, step - 1)
                    for j in range(GH):
                        e = step * GH + j
                        act.wait_ge(s_efull, e + 1)
                        act.activation(PB[:, step % 2, j, :], PA[:, e % 2, :], ACT.Exp).then_inc(s_exp3, 1)
                    if kt == 0 and m >= 1:
                        copy_heads_out(m - 1)
                    for u in range(1, NUNIT):
                        if step == turn_step(u):
                            turn_max(u)
                copy_heads_out(NUNIT - 1)
                for h in range(NC):
                    for k in range(KB):
                        act.activation(XT[:, k, h * HALF:(h + 1) * HALF], bank(("ot", h, k)), ACT.Copy).then_inc(s_aev, 1)
                assert seen[0] == len(AJ)
                act.wait_ge(s_aev, len(AJ))
                act.sem_inc(s_end, 1)
            begin(act, "act")

        @block.tensor
        def _(pe):
            def rows(n, lhs, w, c0):
                if n >= 4:
                    pe.wait_ge(s_cev, n - 3)
                for k in range(KB):
                    m = pe.matmul(PD[0:B, n % 4, :], CTX[:, lhs, k, :], w[:, k, c0:c0 + HALF],
                                  start=(k == 0), stop=(k == KB - 1))
                m.then_inc(s_cfull, 1)

            def row_columns(bank, row):
                for k in range(KB):
                    m = pe.transpose(PA[:, bank, k * B:(k + 1) * B], row[:, k * P:(k + 1) * P], ident[0:B, 0:B])
                m.then_inc(s_small, 1)

            pe.wait_ge(s_const, 6)
            pe.wait_ge(s_in_a, 16 * N_IN_A)
            for n in range(NROWJ):
                rows(n, 0, WC, n * HALF)
            pe.wait_ge(s_ada, 1)
            row_columns(0, TR[:, 1, :])
            pe.wait_ge(s_cev, NROWJ)
            for n in range(NCB):
                m = pe.transpose(PA[:, 3, n * B:(n + 1) * B], ROWS[:, n * P:(n + 1) * P], ident[0:B, 0:B])
            m.then_inc(s_small, 1)
            pe.wait_ge(s_ctx, 1)
            for k in range(KB):
                m = pe.matmul(PA[0:B, 1, 0:D], CTX[:, 1, k, :], L2W1[:, k, :], start=(k == 0), stop=(k == KB - 1))
            m.then_inc(s_small, 1)
            pe.wait_ge(s_gelu, 1)
            row_columns(2, TR[:, 3, :])
            pe.wait_ge(s_bx, 1)
            pe.wait_ge(s_ctx, 3)
            for s in range(2):
                for k in range(KB):
                    m = pe.transpose(PA[:, 0, (2 * s + k) * P:(2 * s + k + 1) * P], BX[:, 2 + s, k * P:(k + 1) * P],
                                     ident[:, :])
            m.then_inc(s_small, 1)
            pe.wait_ge(s_sb, 1)
            for b in range(B):
                pe.wait_ge(s_ctx, 4 if b == 0 else 5)
                for s, row in enumerate((ROWS[:, CW["gate_a"] * P:CW["gate_a"] * P + D],
                                         ROWS[:, CW["gate_ff"] * P:CW["gate_ff"] * P + D], TR[:, 4, :], TR[:, 5, :])):
                    m = pe.matmul(PA[:, 1 + s // 2, (s % 2) * D:(s % 2 + 1) * D], SEL[:, b, :], row, start=True, stop=True)
                m.then_inc(s_small, 1)
            for n in range(NLCH):
                pe.wait_ge(s_l2in[n % 2], 16 * (n // 2 + 1))
                for q in range(2):
                    rows(NROWJ + 2 * n + q, 2, W2L[:, n % 2], q * HALF)

            with pe.Fori(0, B) as b:
                begin(pe, "pe")
                sa, sd = [0], [0]

                def abank(job, rows_=P):
                    n = AJ[job]
                    assert n == sa[0], (job, n, sa)
                    sa[0] += 1
                    if n >= 4:
                        pe.wait_ge(s_aev, n - 3)
                    return PA[0:rows_, n % 4, :]

                def dbank(job, rows_=P):
                    n = DJ[job]
                    assert n == sd[0], (job, n, sd)
                    sd[0] += 1
                    if n >= 4:
                        pe.wait_ge(s_dev, n - 3)
                    return PD[0:rows_, n % 4, :]

                def turn(tag, src, nready):
                    for h in range(NC):
                        if nready is not None:
                            pe.wait_ge(s_xn, nready + h + 1)
                        for k in range(KB):
                            o = abank((tag, h, k))
                            for t in range(TPC):
                                m = pe.transpose(o[:, t * P:(t + 1) * P], src[:, h * TPC + t, k * P:(k + 1) * P], ident[:, :])
                            m.then_inc(s_afull, 1)

                def project(job, w, col, h, bank=abank):
                    o = bank(job)
                    for k in range(KB):
                        m = pe.matmul(o, w[:, k, col:col + P], XT[:, k, h * HALF:(h + 1) * HALF],
                                      start=(k == 0), stop=(k == KB - 1))
                    m.then_inc(s_afull if bank is abank else s_dfull, 1)

                def tokens_out(tag, lhs, rhs, nk, ready, rows_=P):
                    for j in range(NT // 2):
                        if ready is not None:
                            ready(j)
                        o = dbank((tag, j))
                        for u in range(2):
                            t = 2 * j + u
                            for k in range(nk):
                                m = pe.matmul(o[:, u * D:(u + 1) * D], lhs(k)[:, t * P:(t + 1) * P], rhs(k),
                                              start=(k == 0), stop=(k == nk - 1))
                        m.then_inc(s_dfull, 1)

                def mlp(tag, out_tag, layer):
                    pe.wait_ge(s_w1in[layer], 16)
                    for c in range(NC):
                        pe.wait_ge(s_aev, AJ[(("m", "n2")[layer], c, KB - 1)] + 1)
                        for f in range(NF):
                            project((tag, c, f), W1, f * P, c)
                    pe.wait_ge(s_afull, sa[0])
                    pe.sem_inc(s_up, 1)
                    if layer == 0:
                        pe.wait_ge(s_w2g, 1)
                    else:
                        pe.wait_ge(s_w2in[1], 16)

                    def ready(j):
                        pe.wait_ge(s_aev, AJ[(tag, j // 2, NF - 1)] + 1)

                    tokens_out(out_tag, lambda k: HT[:, k, :], lambda k: W2[:, k, :], NF, ready)
                    pe.wait_ge(s_dfull, sd[0])
                    pe.sem_inc(s_down, 1)

                turn("u", XN, 0)
                pe.wait_ge(s_par, 1)
                for c in range(NC):
                    pe.wait_ge(s_aev, AJ[("u", c, KB - 1)] + 1)
                    for s in range(2):
                        o = dbank(("bu", c, s))
                        for k in range(KB):
                            m = pe.matmul(o, BA[:, s, k, :], XT[:, k, c * HALF:(c + 1) * HALF],
                                          start=(k == 0), stop=(k == KB - 1))
                        m.then_inc(s_dfull, 1)
                for j in range(NT // 2):
                    pe.wait_ge(s_zc, j // 2 + 1)
                    pe.wait_ge(s_zs, j // 2 + 1)
                    o = dbank(("y0", j))
                    for u in range(2):
                        t = 2 * j + u
                        tt = slice(t * P, (t + 1) * P)
                        pe.matmul(o[:, u * D:(u + 1) * D], ZC[:, tt], CG[:, 0, :], start=True, stop=False)
                        for k in range(KB):
                            pe.matmul(o[:, u * D + k * P:u * D + (k + 1) * P], XT[:, k, tt], DG[:, k, :],
                                      start=False, stop=False)
                        m = pe.matmul(o[:, u * D:(u + 1) * D], ZS[:, tt], CG[:, 1, :], start=False, stop=True)
                    m.then_inc(s_dfull, 1)
                turn("m", XN, NC)
                mlp("h0", "w20", 0)

                turn("n1", XN, 2 * NC)
                for name, w in (("q", 0), ("k", 1)):
                    for c in range(NC):
                        pe.wait_ge(s_aev, AJ[("n1", c, KB - 1)] + 1)
                        for k in range(KB):
                            project((name, c, k), WA[:, w], k * P, c)
                tokens_out("v1", lambda k: XT[:, k, :], lambda k: WA[:, 2, k, :], KB, None)

                def scores(t):
                    if t >= 2:
                        pe.wait_ge(s_exp1, t - 1)
                    for c in range(NC):
                        for k in range(KB):
                            m = pe.matmul(PDF[:, t % 2, c * HALF:(c + 1) * HALF], QT[:, k, t * P:(t + 1) * P],
                                          KT[:, k, c * HALF:(c + 1) * HALF], start=(k == 0), stop=(k == KB - 1))
                    m.then_inc(s_sfull, 1)

                def probs_turn(t):
                    pe.wait_ge(s_exp1, t + 1)
                    for s in range(2):
                        o = abank(("p", t, s))
                        for k in range(4):
                            m = pe.transpose(o[:, k * P:(k + 1) * P], PX[:, t % 2, (4 * s + k) * P:(4 * s + k + 1) * P],
                                             ident[:, :])
                        m.then_inc(s_afull, 1)

                pe.wait_ge(s_dev, DJ[("v1", NT // 2 - 1)] + 1)
                pe.wait_ge(s_aev, AJ[("k", NC - 1, KB - 1)] + 1)
                scores(0)
                scores(1)
                for t in range(NT):
                    probs_turn(t)
                    if t + 2 < NT:
                        scores(t + 2)
                    if t % TPC == TPC - 1:
                        c = t // TPC
                        pe.wait_ge(s_aev, AJ[("p", t, 1)] + 1)
                        for k in range(KB):
                            o = abank(("o", c, k))
                            for kt in range(NT):
                                m = pe.matmul(o, V[:, kt, k * P:(k + 1) * P], PT[:, kt, :], start=(kt == 0), stop=(kt == NT - 1))
                            m.then_inc(s_afull, 1)
                tokens_out("pr", lambda k: OT[:, k, :], lambda k: WA[:, 3, k, :], KB,
                           lambda j: pe.wait_ge(s_aev, AJ[("o", j // 2, KB - 1)] + 1))
                turn("n2", XN, 3 * NC)
                mlp("h1", "w21", 1)

                for h in range(NC):
                    pe.wait_ge(s_dev, DJ[("w21", 2 * h + 1)] + 1)
                    for k in range(KB):
                        o = abank(("x2", h, k))
                        for t in range(TPC):
                            m = pe.transpose(o[:, t * P:(t + 1) * P], X[:, h * TPC + t, k * P:(k + 1) * P], ident[:, :])
                        m.then_inc(s_afull, 1)

                def down(tag, src, s, c):
                    o = dbank((tag, c), RANK)
                    for k in range(KB):
                        m = pe.matmul(o, LAC[:, s, k, :], src[:, k, c * HALF:(c + 1) * HALF], start=(k == 0), stop=(k == KB - 1))
                    m.then_inc(s_dfull, 1)

                for c in range(NC):
                    pe.wait_ge(s_aev, AJ[("x2", c, KB - 1)] + 1)
                    down("a1", XT, 0, c)
                for c in range(NC):
                    pe.wait_ge(s_dev, DJ[("a1", c)] + 1)
                    for k in range(KB):
                        o = abank(("g", c, k))
                        pe.matmul(o, LBC[:, 0, k * P:(k + 1) * P], Y8[:, 0, c * HALF:(c + 1) * HALF], start=True,
                                  stop=True).then_inc(s_afull, 1)
                for c in range(NC):
                    pe.wait_ge(s_aev, AJ[("g", c, KB - 1)] + 1)
                    down("a2", QT, 1, c)
                tokens_out("f2", lambda k: Y8[:, 1, :], lambda k: LBC[:, 1, :], 1,
                           lambda j: pe.wait_ge(s_dev, DJ[("a2", j // 2)] + 1))

                turn("n3", XN, 4 * NC)
                tokens_out("v3", lambda k: XT[:, k, :], lambda k: WQ3[:, 2, k, :], KB,
                           lambda j: pe.wait_ge(s_aev, AJ[("n3", j // 2, KB - 1)] + 1))
                for k in range(KB):
                    for w, name in enumerate(("q3", "k3")):
                        for c in range(NC):
                            project((name, c, k), WQ3[:, w], k * P, c)

                def maxpass(n):
                    m, r = divmod(n, UNIT)
                    h, t = m // NC * GH + r // TPC, m % NC * TPC + r % TPC
                    if n >= 2:
                        pe.wait_ge(s_mred, n - 1)
                    if n % (NC * UNIT) == 0:
                        pe.wait_ge(s_stack[m // NC], 16 * (NC + 1) * NPAIR)
                    for c in range(NC):
                        i = pe.matmul(PDF[:, n % 2, c * HALF:(c + 1) * HALF], QS[0:KSTK, t // TPC, h, (t % TPC) * P:(t % TPC + 1) * P],
                                      KS[0:KSTK, h, c * HALF:(c + 1) * HALF], start=True, stop=True)
                    i.then_inc(s_mfull, 1)

                def turn_max(m):
                    pe.wait_ge(s_nmp, m + 1)
                    if m >= 2:
                        pe.wait_ge(s_on, m - 1)
                    if m >= 1:
                        pe.wait_ge(s_nmt, m)
                    pe.transpose(PTB[0:NPART * UNIT, :], NMP[:, :, :].rearrange("p s n -> p (s n)"),
                                 identb[:, :]).then_inc(s_nmtf, 1)

                def turn_heads_out(m):
                    pe.wait_ge(s_uo, m + 1)
                    if m >= 1:
                        pe.wait_ge(s_on, m)
                    pe.wait_ge(s_nmt, min(m + 2, NUNIT))
                    for t in range(TPC):
                        i = pe.transpose(PA[:, 3, t * P:(t + 1) * P], UO[:, t * P:(t + 1) * P], ident[:, :])
                    i.then_inc(s_ut, 1)

                def energy(step, j):
                    m, kt = divmod(step, NT)
                    g, c = divmod(m, NC)
                    e = step * GH + j
                    if e >= 2:
                        pe.wait_ge(s_exp3, e - 1)
                    pe.matmul(PA[:, e % 2, :], KS[:, g * GH + j, kt * P:(kt + 1) * P],
                              QS[:, c, g * GH + j, :], start=True, stop=True).then_inc(s_efull, 1)

                def times_v(step):
                    m, kt = divmod(step, NT)
                    g, c = divmod(m, NC)
                    pe.wait_ge(s_exp3, (step + 1) * GH)
                    if kt == 0 and m >= 1:
                        pe.wait_ge(s_uo, m)
                    for j in range(GH):
                        i = pe.matmul(PA[32 * j:32 * j + 32, 2, :], VP[:, kt, g * GH + j, :], PB[:, step % 2, j, :],
                                      start=(kt == 0), stop=(kt == NT - 1))
                    i.then_inc(s_pv, 1)

                pe.wait_ge(s_ones, 1)
                pe.wait_ge(s_dev, DJ[("v3", NT // 2 - 1)] + 1)
                pe.wait_ge(s_aev, AJ[("k3", NC - 1, KB - 1)] + 1)
                for n in range(LEAD):
                    maxpass(n)
                    if n == UNIT + 1:
                        turn_max(0)
                pe.wait_ge(s_nmrow[0], 16 * NPART)
                energy(0, 0)
                energy(0, 1)
                for step in range(NSTEP):
                    m, kt = divmod(step, NT)
                    n = LEAD + 2 * step
                    if step >= 1:
                        times_v(step - 1)
                    energy(step, 2)
                    if n < NUNIT * UNIT:
                        maxpass(n)
                    energy(step, 3)
                    if n < NUNIT * UNIT:
                        maxpass(n + 1)
                    for u in range(1, NUNIT):
                        if step == turn_step(u):
                            turn_max(u)
                    if kt == 1 and m >= 1:
                        turn_heads_out(m - 1)
                    if step + 1 < NSTEP:
                        if kt == NT - 1:
                            pe.wait_ge(s_nmrow[m + 1], 16 * NPART)
                        energy(step + 1, 0)
                        energy(step + 1, 1)
                times_v(NSTEP - 1)
                turn_heads_out(NUNIT - 1)
                pe.wait_ge(s_on, NUNIT)
                turn("ot", O, None)
                tokens_out("p3", lambda k: XT[:, k, :], lambda k: WP3[:, k, :], KB,
                           lambda j: pe.wait_ge(s_aev, AJ[("ot", j // 2, KB - 1)] + 1))
                assert sa[0] == len(AJ) and sd[0] == len(DJ)
                pe.wait_ge(s_dfull, len(DJ))
                pe.sem_inc(s_end, 1)
            begin(pe, "pe")

        @block.vector
        def _(ve):
            n0 = [0]

            def l0(i):
                n0[0] += 1
                i.then_inc(s_link0, 1)
                ve.wait_ge(s_link0, n0[0])

            ve.wait_ge(s_in_a, 16 * N_IN_A)
            l0(ve.bn_stats(ST[0:B, 0, :], TR[:, 0, :]))
            ve.bn_aggr(MV[0:B, 0, :], ST[0:B, 0, :]).then_inc(s_ada_st, 1)
            for n in range(NROWJ):
                ve.wait_ge(s_cfull, n + 1)
                q = slice(n * HALF, (n + 1) * HALF)
                ve.tensor_tensor(ROWS[:, q], PD[0:B, n % 4, :], ROWS[:, q], ALU.add).then_inc(s_cev, 1)
            ve.wait_ge(s_ada_rs, 2)
            l0(ve.tensor_scalar(TR[:, 1, :], TR[:, 0, :], MV[0:B, 0, 0:1], RST[0:B, 0:1], ALU.subtract, ALU.mult))
            l0(ve.tensor_tensor(TR[:, 1, :], TR[:, 1, :], LNR[:, 0, :], ALU.mult))
            ve.tensor_tensor(TR[:, 1, :], TR[:, 1, :], LNR[:, 1, :], ALU.add).then_inc(s_ada, 1)
            ve.wait_ge(s_small, 1)
            ve.tensor_copy(CTX[:, 1, :, :].rearrange("p k b -> p (k b)"), PA[:, 0, 0:KB * B]).then_inc(s_ctx, 1)
            ve.wait_ge(s_small, 2)
            ve.tensor_copy(COLR.rearrange("p n b -> p (n b)"), PA[:, 3, 0:NCB * B]).then_inc(s_ctx, 1)
            ve.wait_ge(s_small, 3)
            ve.tensor_tensor(TR[:, 2, :], PA[0:B, 1, 0:D], LNR[:, 2, :], ALU.add).then_inc(s_hid, 1)
            ve.wait_ge(s_ctx, 2)
            ve.wait_ge(s_cev, NROWJ)
            for b in range(B):
                def c(name):
                    return COLR[:, CW[name]:CW[name] + KB, b]

                def v(name):
                    return VEC[:, VC[name]:VC[name] + KB]

                def p(n):
                    return PAR[:, b, n * KB:(n + 1) * KB]

                l0(ve.tensor_scalar(p(PU), c("scale_a"), 1.0, None, ALU.add))
                l0(ve.tensor_copy(p(PU + 1), c("shift_a")))
                l0(ve.tensor_scalar(TM[:, 20:22], c("scale_ff"), 1.0, None, ALU.add))
                l0(ve.scalar_tensor_tensor(p(PM), c("scale_c"), 1.0, TM[:, 20:22], ALU.add, ALU.mult))
                l0(ve.tensor_tensor(TM[:, 22:24], c("shift_c"), TM[:, 20:22], ALU.mult))
                l0(ve.tensor_tensor(p(PM + 1), TM[:, 22:24], c("shift_ff"), ALU.add))
                l0(ve.scalar_tensor_tensor(p(P1), c("f1_scale"), 1.0, v("norm1"), ALU.add, ALU.mult))
                l0(ve.tensor_copy(p(P1 + 1), c("f1_shift")))
                l0(ve.scalar_tensor_tensor(p(P2), c("f2_scale"), 1.0, v("norm2"), ALU.add, ALU.mult))
                l0(ve.tensor_copy(p(P2 + 1), c("f2_shift")))
                l0(ve.tensor_tensor(p(P3), c("gamma"), v("ln3_g"), ALU.mult))
                l0(ve.tensor_tensor(TM[:, 22:24], c("gamma"), v("ln3_b"), ALU.mult))
                l0(ve.tensor_tensor(p(P3 + 1), TM[:, 22:24], c("beta"), ALU.add))
            gamma = ROWS[:, CW["gamma"] * P:CW["gamma"] * P + D]
            beta = ROWS[:, CW["beta"] * P:CW["beta"] * P + D]
            l0(ve.tensor_tensor(TR[:, 4, :], gamma, LNR[:, 3, :], ALU.mult))
            l0(ve.tensor_tensor(TR[:, 5, :], gamma, LNR[:, 4, :], ALU.mult))
            ve.tensor_tensor(TR[:, 5, :], TR[:, 5, :], beta, ALU.add).then_inc(s_sb, 1)

            def tm(n):
                return TM[:, n:n + 1]

            ROUND = 1.5 * 2.0 ** 23
            DT, LR_, TH, RR, COS, SIN, A0, A1, A2, A3 = 0, 1, 2, 3, 8, 9, 10, 11, 12, 13

            def exp(o, x):
                l0(ve.tensor_scalar(tm(A0), tm(x), -87.0, 88.0, ALU.max, ALU.min))
                l0(ve.tensor_scalar(tm(A1), tm(A0), 1.4426950408889634, ROUND, ALU.mult, ALU.add))
                l0(ve.tensor_scalar(tm(A1), tm(A1), -ROUND, None, ALU.add))
                l0(ve.scalar_tensor_tensor(tm(A0), tm(A1), -0.693359375, tm(A0), ALU.mult, ALU.add))
                l0(ve.scalar_tensor_tensor(tm(A0), tm(A1), 2.12194440e-4, tm(A0), ALU.mult, ALU.add))
                coef = [1 / 5040, 1 / 720, 1 / 120, 1 / 24, 1 / 6, 0.5, 1.0]
                l0(ve.tensor_scalar(tm(A2), tm(A0), coef[0], coef[1], ALU.mult, ALU.add))
                for q in coef[2:] + [1.0]:
                    l0(ve.tensor_scalar(tm(A2), tm(A2), tm(A0), q, ALU.mult, ALU.add))
                l0(ve.tensor_scalar(tm(A1), tm(A1), 127.0, 2.0 ** 23, ALU.add, ALU.mult))
                l0(ve.tensor_copy(TI[:, :], tm(A1)))
                l0(ve.tensor_tensor(tm(o), tm(A2), TI[:, :].bitcast(F32), ALU.mult))

            lam_re, lam_im = (VEC[:, VC[n]:VC[n] + 1] for n in ("lam_re", "lam_im"))
            l0(ve.tensor_copy(tm(LR_), VEC[:, VC["log_step"]:VC["log_step"] + 1]))
            exp(DT, LR_)
            l0(ve.tensor_tensor(tm(LR_), lam_re, tm(DT), ALU.mult))
            l0(ve.tensor_tensor(tm(TH), lam_im, tm(DT), ALU.mult))
            exp(RR, LR_)
            PI1, PI2, PI3 = 6.28125, 1.93500518798828125e-3, 3.0199159819e-7
            l0(ve.tensor_scalar(tm(A1), tm(TH), 1.0 / (2 * np.pi), ROUND, ALU.mult, ALU.add))
            l0(ve.tensor_scalar(tm(A1), tm(A1), -ROUND, None, ALU.add))
            l0(ve.scalar_tensor_tensor(tm(A0), tm(A1), -PI1, tm(TH), ALU.mult, ALU.add))
            l0(ve.scalar_tensor_tensor(tm(A0), tm(A1), -PI2, tm(A0), ALU.mult, ALU.add))
            l0(ve.scalar_tensor_tensor(tm(A0), tm(A1), -PI3, tm(A0), ALU.mult, ALU.add))
            l0(ve.tensor_scalar(tm(A2), tm(A0), float(np.pi / 2), None, ALU.add))
            l0(ve.tensor_scalar(tm(A3), tm(A2), float(np.pi), float(-2 * np.pi), ALU.is_gt, ALU.mult))
            l0(ve.tensor_tensor(tm(A2), tm(A2), tm(A3), ALU.add))
            l0(ve.tensor_scalar(tm(6), tm(A2), -3.1415925, 3.1415925, ALU.max, ALU.min))
            ve.tensor_scalar(tm(7), tm(A0), -3.1415925, 3.1415925, ALU.max, ALU.min).then_inc(s_ang, 1)
            ve.wait_ge(s_trig, 1)
            NR, NI, DEN, FR, FI, UU, WW = 14, 15, 16, 17, 18, 4, 5
            l0(ve.tensor_scalar(tm(NR), tm(COS), tm(RR), -1.0, ALU.mult, ALU.add))
            l0(ve.tensor_tensor(tm(NI), tm(SIN), tm(RR), ALU.mult))
            l0(ve.tensor_tensor(tm(A0), lam_im, lam_im, ALU.mult))
            l0(ve.scalar_tensor_tensor(tm(DEN), lam_re, lam_re, tm(A0), ALU.mult, ALU.add))
            l0(ve.reciprocal(tm(DEN), tm(DEN)))
            l0(ve.tensor_tensor(tm(A0), tm(NI), lam_im, ALU.mult))
            l0(ve.scalar_tensor_tensor(tm(FR), tm(NR), lam_re, tm(A0), ALU.mult, ALU.add))
            l0(ve.tensor_tensor(tm(FR), tm(FR), tm(DEN), ALU.mult))
            l0(ve.tensor_tensor(tm(A0), tm(NR), lam_im, ALU.mult))
            l0(ve.scalar_tensor_tensor(tm(FI), tm(NI), lam_re, tm(A0), ALU.mult, ALU.subtract))
            l0(ve.tensor_tensor(tm(FI), tm(FI), tm(DEN), ALU.mult))
            lo, hi = slice(0, S5), slice(S5, 2 * S5)
            l0(ve.tensor_copy(TM[lo, UU:UU + 1], TM[lo, FR:FR + 1]))
            l0(ve.tensor_copy(TM[hi, UU:UU + 1], TM[hi, FI:FI + 1]))
            l0(ve.tensor_scalar(TM[lo, WW:WW + 1], TM[lo, FI:FI + 1], -1.0, None, ALU.mult))
            l0(ve.tensor_copy(TM[hi, WW:WW + 1], TM[hi, FR:FR + 1]))
            l0(ve.tensor_scalar(BX[:, 2, :], BX[:, 1, :], tm(WW), None, ALU.mult))
            l0(ve.scalar_tensor_tensor(BX[:, 2, :], BX[:, 0, :], tm(UU), BX[:, 2, :], ALU.mult, ALU.add))
            l0(ve.tensor_scalar(BX[:, 3, :], BX[:, 0, :], tm(WW), None, ALU.mult))
            ve.scalar_tensor_tensor(BX[:, 3, :], BX[:, 1, :], tm(UU), BX[:, 3, :], ALU.mult, ALU.subtract).then_inc(s_bx, 1)
            l0(ve.tensor_copy(RVEC[:, :], tm(RR)))
            l0(ve.memset(SG[lo, 0:1], 2.0))
            l0(ve.memset(SG[hi, 0:1], -2.0))
            l0(ve.memset(SG[:, 1:2], -2.0))
            ve.wait_ge(s_small, 4)
            ve.tensor_copy(CTX[:, 2, :, :].rearrange("p k b -> p (k b)"), PA[:, 2, 0:KB * B]).then_inc(s_ctx, 1)
            ve.wait_ge(s_small, 5)
            ve.tensor_copy(BA[:, :, :, :].rearrange("p s k n -> p (s k n)"), PA[:, 0, :]).then_inc(s_ctx, 1)
            for b in range(B):
                ve.wait_ge(s_small, 6 + b)
                ve.tensor_copy(GB[:, b].rearrange("p (s u) d -> p s (u d)", s=2), PA[:, 1:3, :]).then_inc(s_ctx, 1)
            l0(ve.memset(C2[:, 0:1], 1.0))
            l0(ve.memset(S2[:, 0:1], 0.0))
            n = 1
            while n < T:
                a, q = slice(0, n), slice(n, 2 * n)
                l0(ve.tensor_scalar(T1[:, a], S2[:, a], tm(SIN), None, ALU.mult))
                l0(ve.scalar_tensor_tensor(C2[:, q], C2[:, a], tm(COS), T1[:, a], ALU.mult, ALU.subtract))
                l0(ve.tensor_scalar(T2[:, a], C2[:, a], tm(SIN), None, ALU.mult))
                l0(ve.scalar_tensor_tensor(S2[:, q], S2[:, a], tm(COS), T2[:, a], ALU.mult, ALU.add))
                l0(ve.tensor_tensor(tm(A0), tm(SIN), tm(SIN), ALU.mult))
                l0(ve.tensor_tensor(tm(A1), tm(SIN), tm(COS), ALU.mult))
                l0(ve.scalar_tensor_tensor(tm(COS), tm(COS), tm(COS), tm(A0), ALU.mult, ALU.subtract))
                l0(ve.tensor_scalar(tm(SIN), tm(A1), 2.0, None, ALU.mult))
                n *= 2
            for n in range(NLJ):
                ve.wait_ge(s_cfull, NROWJ + n + 1)
                q = slice(n * HALF, (n + 1) * HALF)
                ve.tensor_tensor(WR[:, q], PD[0:B, (NROWJ + n) % 4, :], WR[:, q], ALU.add).then_inc(s_cev, 1)

            with ve.Fori(0, B) as b:
                begin(ve, "dve")
                cnt = dict(l=0, rs=0)
                sd = [0]

                def link(i):
                    cnt["l"] += 1
                    i.then_inc(s_dstep, 1)
                    ve.wait_ge(s_dstep, cnt["l"])

                def bank(job, rows_=P):
                    n = DJ[job]
                    assert n == sd[0], (job, n, sd)
                    sd[0] += 1
                    ve.wait_ge(s_dfull, n + 1)
                    return PD[0:rows_, n % 4, :]

                def two(j):
                    return slice(2 * j, 2 * j + 2)

                def pair(a):
                    return a.rearrange("p (u d) -> p u d", u=2)

                def row2(a):
                    return a.unsqueeze(1).to_broadcast([P, 2, D])

                def stats(ready):
                    for h in range(NC):
                        ready(h)
                        for t in range(h * TPC, (h + 1) * TPC):
                            i = ve.bn_stats(ST[:, t, :], X[:, t, :])
                        link(i)
                        for t in range(h * TPC, (h + 1) * TPC):
                            i = ve.bn_aggr(MV[:, t, :], ST[:, t, :])
                        i.then_inc(s_stats, 1)

                def normalise(mean, sem_=s_xn):
                    for h in range(NC):
                        cnt["rs"] += 1
                        ve.wait_ge(s_rstd, cnt["rs"])
                        for t in range(h * TPC, (h + 1) * TPC):
                            if mean:
                                i = ve.tensor_scalar(XN[:, t, :], X[:, t, :], MV[:, t, 0:1], RST[:, t:t + 1],
                                                     ALU.subtract, ALU.mult)
                            else:
                                i = ve.tensor_scalar(XN[:, t, :], X[:, t, :], RST[:, t:t + 1], None, ALU.mult)
                        i.then_inc(sem_, 1)

                def add_out(tag, npre):
                    for j in range(NT // 2):
                        if npre:
                            ve.wait_ge(s_pre, npre + j // 2 + 1 - NC)
                        ve.tensor_tensor(X[:, two(j), :], pair(bank((tag, j))), X[:, two(j), :], ALU.add).then_inc(s_dev, 1)

                def after(tag):
                    return lambda h: ve.wait_ge(s_dev, DJ[(tag, 2 * h + 1)] + 1)

                link(ve.tensor_copy(CUR[:, :], PAR[:, b, :]))
                link(ve.tensor_copy(LAC[:, :, :, :], LA[:, b]))
                link(ve.tensor_copy(LBC[:, :, :], LB[:, b]))
                for s in range(2):
                    link(ve.scalar_tensor_tensor(CG[:, s, :], CT[:, s, :], SG[:, s:s + 1], GB[:, b, GA, :], ALU.mult, ALU.mult))
                for k in range(KB):
                    i = ve.scalar_tensor_tensor(DG[:, k, :], ident[:, :], VEC[:, VC["D"] + k:VC["D"] + k + 1],
                                                GB[:, b, GA, k * P:(k + 1) * P], ALU.mult, ALU.mult)
                i.then_inc(s_par, 1)
                ve.tensor_tensor(BG[:, :], BC[:, B20, :], GB[:, b, GF, :], ALU.mult).then_inc(s_par, 1)

                stats(lambda h: ve.wait_ge(s_xin[h], 16))
                normalise(True)
                for c in range(NC):
                    q = slice(c * HALF, (c + 1) * HALF)
                    ve.tensor_tensor(T1[:, q], bank(("bu", c, 0)), C2[:, q], ALU.mult).then_inc(s_dev, 1)
                    ve.tensor_tensor(T2[:, q], bank(("bu", c, 1)), S2[:, q], ALU.mult).then_inc(s_dev, 1)
                    ve.wait_ge(s_dev, sd[0])
                    link(ve.tensor_tensor(T1[:, q], T1[:, q], T2[:, q], ALU.add))
                    ve.tensor_tensor_scan(Z[:, q], RVEC[:, 0:1].to_broadcast([P, HALF]), T1[:, q],
                                          0.0 if c == 0 else Z[:, c * HALF - 1:c * HALF], ALU.mult, ALU.add).then_inc(s_z, 1)
                    ve.wait_ge(s_z, c + 1)
                    ve.tensor_tensor(ZC[:, q], Z[:, q], C2[:, q], ALU.mult).then_inc(s_zc, 1)
                add_out("y0", 0)
                stats(after("y0"))
                normalise(True)
                add_out("w20", 1 * NC)

                stats(after("w20"))
                normalise(False)
                for j in range(NT // 2):
                    ve.tensor_tensor(V[:, two(j), :], pair(bank(("v1", j))), row2(BC[:, BV, :]), ALU.add).then_inc(s_dev, 1)
                for t in range(NT):
                    ve.wait_ge(s_sfull, t + 1)
                    ve.tensor_reduce(NM[:, t:t + 1], PDF[:, t % 2, :], axis=AX_X, op=ALU.max, negate=True).then_inc(s_max1, 1)
                    ve.wait_ge(s_max1, t + 1)
                    ve.tensor_scalar(NMS[:, t:t + 1], NM[:, t:t + 1], float(D) ** -0.5, None, ALU.mult).then_inc(s_nmax, 1)
                ve.wait_ge(s_exp1, NT)
                link(ve.reciprocal(RSM[:, :], SM[:, :]))
                for j in range(NT // 2):
                    ve.wait_ge(s_pre, 1 * NC + j // 2 + 1)
                    o = bank(("pr", j))
                    for u in range(2):
                        t = 2 * j + u
                        i = ve.scalar_tensor_tensor(X[:, t, :], o[:, u * D:(u + 1) * D], RSM[:, t:t + 1], X[:, t, :],
                                                    ALU.mult, ALU.add)
                    i.then_inc(s_dev, 1)
                stats(after("pr"))
                normalise(False)
                add_out("w21", 3 * NC)

                for c in range(NC):
                    ve.tensor_copy(Y8[:, 0, c * HALF:(c + 1) * HALF], bank(("a1", c), RANK)).then_inc(s_dev, 1)
                for c in range(NC):
                    ve.tensor_copy(Y8[:, 1, c * HALF:(c + 1) * HALF], bank(("a2", c), RANK)).then_inc(s_dev, 1)
                add_out("f2", 0)

                stats(after("f2"))
                normalise(True)
                for j in range(NT // 2):
                    o = bank(("v3", j))
                    for u in range(2):
                        i = ve.tensor_tensor(VP[:, 2 * j + u, :, 0:HD],
                                             o[:, u * D:(u + 1) * D].rearrange("p (h d) -> p h d", h=HEADS),
                                             BC[:, BV3, :].rearrange("p (h d) -> p h d", h=HEADS), ALU.add)
                    i.then_inc(s_dev, 1)
                n = 0
                for k in range(KB):
                    for name, dst in (("q3", PQ), ("k3", PK)):
                        for c in range(NC):
                            ve.wait_ge(s_aev, AJ[(name, c, k)] + 1)
                            f, r = QF[:, n % 4, :], RP[:, n % 2, :]
                            q = slice(c * HALF, (c + 1) * HALF)
                            link(ve.tensor_copy(dst[:, 0, k, q], f))
                            link(ve.tensor_tensor(r, f, dst[:, 0, k, q], ALU.subtract))
                            link(ve.tensor_copy(dst[:, 1, k, q], r))
                            ve.tensor_tensor(dst[:, 2, k, q], r, dst[:, 1, k, q], ALU.subtract).then_inc(s_parts, 1)
                            n += 1

                def reduce_max(n):
                    ve.wait_ge(s_mfull, n + 1)
                    m, r = divmod(n, UNIT)
                    ve.tensor_reduce(NMX[:, m % 2, r:r + 1], PDF[:, n % 2, :], axis=AX_X, op=ALU.max,
                                     negate=True).then_inc(s_mred, 1)
                    if r == UNIT - 1:
                        split_max(m)

                def split_max(m):
                    ve.wait_ge(s_mred, (m + 1) * UNIT)
                    if m >= 1:
                        ve.wait_ge(s_nmtf, m)
                    f = NMX[:, m % 2, :]
                    link(ve.tensor_copy(NMP[:, 0, :], f))
                    link(ve.tensor_tensor(NMR[:, :], f, NMP[:, 0, :], ALU.subtract))
                    link(ve.tensor_copy(NMP[:, 1, :], NMR[:, :]))
                    ve.tensor_tensor(NMP[:, 2, :], NMR[:, :], NMP[:, 1, :], ALU.subtract).then_inc(s_nmp, 1)

                def norm_heads_out(m):
                    g, c = divmod(m, NC)
                    ve.wait_ge(s_ut, m + 1)
                    o = PA[:, 3, :].rearrange("p (n c) -> p n c", c=32)
                    link(ve.reciprocal(RC[:, :], o[:, :, HD]))
                    ve.tensor_tensor(
                        O[:, c * TPC:(c + 1) * TPC, g * GH * HD:(g + 1) * GH * HD].rearrange("p t (h d) -> p t h d", h=GH),
                        PA[:, 3, :].rearrange("p (t h c) -> p t h c", t=TPC, h=GH)[:, :, :, 0:HD],
                        RC[:, :].rearrange("p (t h) -> p t h", t=TPC).unsqueeze(3).to_broadcast([P, TPC, GH, HD]),
                        ALU.mult).then_inc(s_on, 1)

                for n in range(LEAD):
                    reduce_max(n)
                for k in range(2 * KB):
                    ve.wait_ge(s_spill[k], 16)
                for step in range(NSTEP):
                    m, kt = divmod(step, NT)
                    n = LEAD + 2 * step
                    if n < NUNIT * UNIT:
                        reduce_max(n)
                        reduce_max(n + 1)
                    if kt == 2 and m >= 1:
                        norm_heads_out(m - 1)
                norm_heads_out(NUNIT - 1)
                add_out("p3", 4 * NC)
                stats(after("p3"))
                normalise(True, s_scaled)
                for h in range(NC):
                    t = slice(h * TPC, (h + 1) * TPC)
                    ve.wait_ge(s_scaled, h + 1)
                    link(ve.tensor_tensor(XN[:, t, :], XN[:, t, :], GB[:, b, S3, :].unsqueeze(1).to_broadcast([P, TPC, D]),
                                          ALU.mult))
                    ve.wait_ge(s_pre, 4 * NC + h + 1)
                    ve.tensor_tensor(XN[:, t, :], XN[:, t, :], X[:, t, :], ALU.add).then_inc(s_fin, 1)
                assert sd[0] == len(DJ)
                ve.wait_ge(s_fin, NC)
                ve.sem_inc(s_end, 1)
            begin(ve, "dve")


def kernel(**inputs):
    import concourse.bacc as _bacc
    from concourse.bass_utils import run_bass_kernel_spmd as _run

    g = {k: np.asarray(v) for k, v in inputs.items()}

    def blocks(a):
        return a.reshape(-1, P).T

    def twice(a, b):
        return np.concatenate([a, b], axis=0)

    def kpn(w):
        return w.reshape(KB, P, -1).transpose(1, 0, 2)

    t = g["cond_1024"]
    wq3 = g["L3_cond_Wqkv"].reshape(D, 3, D)
    bq3 = g["L3_cond_bqkv"].reshape(D, 3)
    w2 = g["L2_cond_W2"].reshape(D, 4, D, RANK)
    b2 = g["L2_cond_b2"].reshape(4, D, RANK)
    l2_w2 = np.concatenate([w2[:, 0].reshape(D, -1), w2[:, 2].reshape(D, -1),
                            w2[:, 1].transpose(0, 2, 1).reshape(D, -1), w2[:, 3].transpose(0, 2, 1).reshape(D, -1)], axis=1)
    l2_b2 = np.concatenate([b2[0].reshape(-1), b2[2].reshape(-1), b2[1].T.reshape(-1), b2[3].T.reshape(-1)])
    col = lambda n: np.concatenate([g[n], g[n]])[:, None]
    arrays = {
        "x": g["x"], "t": t, "tT": t.T.reshape(KB, P, B).transpose(1, 0, 2),
        "lnrow": np.stack([g["L2_cond_ln_g"], g["L2_cond_ln_b"], g["L2_cond_b1"], g["L3_cond_ln_g"], g["L3_cond_ln_b"]]),
        "vec": np.concatenate(
            [blocks(g[n]) for n in ("L1_cond_norm1_w", "L1_cond_norm2_w", "L3_cond_ln_g", "L3_cond_ln_b", "L1_cond_q_b",
                                    "L1_cond_k_b")] + [blocks(bq3[:, 0]), blocks(bq3[:, 1])]
            + [blocks(g[n]) for n in ("L0_cond_D_diag", "L0_cond_b1", "L1_cond_mlp_b1")]
            + [col(n) for n in ("L0_cond_Lam_re", "L0_cond_Lam_im", "L0_cond_log_step")], axis=1),
        "wcond": np.concatenate([g["L0_cond_Wm"], g["L0_cond_Wc"], g["L1_cond_film1_w"], g["L1_cond_film2_w"],
                                 g["L3_cond_Wg"].T, g["L3_cond_Wb"].T], axis=1),
        "bcond": np.concatenate([g["L0_cond_bm"], g["L0_cond_bc"], g["L1_cond_film1_b"], g["L1_cond_film2_b"],
                                 g["L3_cond_bg"], g["L3_cond_bb"]]),
        "l2_w1": g["L2_cond_W1"], "l2_w2": l2_w2, "l2_b2": l2_b2,
        "b2x": np.stack([twice(g["L0_cond_B_re"], g["L0_cond_B_re"]), twice(g["L0_cond_B_im"], g["L0_cond_B_im"])], axis=1),
        "ct": np.stack([twice(g["L0_cond_C_re"].T, g["L0_cond_C_im"].T), twice(g["L0_cond_C_im"].T, g["L0_cond_C_re"].T)],
                       axis=1),
        "bc": np.stack([g["L1_cond_v_b"], g["L1_cond_proj_b"], g["L1_cond_mlp_b2"], bq3[:, 2], g["L3_cond_bp"],
                        g["L0_cond_b2"]]),
        "wa": np.stack([kpn(g[f"L1_cond_{n}_w"]) for n in ("q", "k", "v", "proj")], axis=1),
        "wqkv3": np.stack([kpn(wq3[:, j].T) for j in range(3)], axis=1),
        "wp3": g["L3_cond_Wp"].T,
        "w1_0": g["L0_cond_W1"], "w2_0": g["L0_cond_W2"], "w1_1": g["L1_cond_mlp_w1"], "w2_1": g["L1_cond_mlp_w2"],
    }
    arrays = {k: np.ascontiguousarray(v) for k, v in arrays.items()}
    nc = _bacc.Bacc("TRN2", target_bir_lowering=False, num_devices=1)
    ins = {k: nc.dram_tensor(f"in_{k}", v.shape, mybir.dt.from_np(v.dtype), kind="ExternalInput").ap()
           for k, v in arrays.items()}
    out = nc.dram_tensor("out_0", (B, T, D), F32, kind="ExternalOutput").ap()
    build(nc, ins, out)
    r = _run(nc, [{f"in_{k}": v for k, v in arrays.items()}], core_ids=[0])
    return r.results[0]["out_0"]
```

```python
from contextlib import ExitStack

import numpy as np
import concourse.bass as bass
from concourse import mybir

F32 = mybir.dt.float32
BF16 = mybir.dt.bfloat16
I32 = mybir.dt.int32
ALU = mybir.AluOpType
ACT = mybir.ActivationFunctionType
AX_X = mybir.AxisListType.X

P = 128
B, T, D = 2, 1024, 256
KB = D // P
NT = T // P
HALF = 512
NC = T // HALF
TPC = HALF // P
TWO = NT // 2
FF = 4 * D
NF = FF // P
S5 = 64
HEADS, HD = 16, 16
GH = 4
NG = HEADS // GH
RANK = 8
LR = 4 * RANK * D
LCH = 1024
NLCH = LR // LCH
GCOL = 32
LG = LCH // (P // GCOL)
PAIRS = [(0, 0), (0, 1), (1, 0), (1, 1), (0, 2), (2, 0)]
NPAIR = len(PAIRS)
KSTK = NPAIR * HD
NPART = 3
KFULL = KSTK + NPART
UNIT = GH * TPC
NUNIT = B * NG * NC
NMAX = NUNIT * UNIT
NSTEP = NUNIT * NT
LEAD = UNIT + 14
SOLO = (NMAX - LEAD) // 2
NSLOT = 3

CW = dict(shift_a=0, scale_a=2, gate_a=4, shift_ff=6, scale_ff=8, gate_ff=10, scale_c=12, shift_c=14,
          f1_scale=16, f1_shift=18, f2_scale=20, f2_shift=22, gamma=24, beta=26)
NCB = 28
NCOND = NCB * P
LEVELS = T.bit_length() - 1
NROWJ = NCOND // HALF
PU, PM, P1, P2, P3 = range(0, 10, 2)
NPAR = 10
VC = dict(norm1=0, norm2=2, ln3_g=4, ln3_b=6, q_b=8, k_b=10, q3_b=12, k3_b=14, D=16, b1=18, mb1=26,
          lam_re=34, lam_im=35, log_step=36)
NVC = 37
BV, BP, MB2, BV3, BP3, B20 = range(6)
GA, GF, S3, B3 = range(4)

MLPP = 4
NLEAD = 5


def parts_of(stage, b, parts=MLPP):
    return [(stage, b * MLPP + p) for p in range(parts)]


def weave(*lists):
    return [x for n in range(max(map(len, lists))) for one in lists for x in one[n:n + 1]]


SCHED = [("n0", 0), ("n0", 1), ("tab", 0), ("lr", 0), ("lr", 1), ("bu", 0), ("lr", 2), ("bu", 1), ("lr", 3),
         ("y0", 0), ("lr", 4), ("lr", 5), ("y0", 1), ("lr", 6), ("lr", 7)]
assert NLCH == 8
SCHED += [("m", 0)] + parts_of("u0", 0) + parts_of("d0", 0) + [("h0", 0)]
SCHED += [("m", 1)] + parts_of("u0", 1) + parts_of("d0", 1) + [("h0", 1), ("lb", 0)]
SCHED += [("n1", 0), ("qkv", 0), ("att", 0), ("n1", 1), ("qkv", 1), ("pr", 0), ("att", 1), ("pr", 1)]
SCHED += [("n2", 0)] + parts_of("u1", 0) + parts_of("d1", 0) + [("n2", 1)]
SCHED += weave(parts_of("u1", 1) + parts_of("d1", 1),
               [("x2", 0), ("a1", 0), ("g", 0), ("a2", 0), ("f2", 0), None, ("n3", 0), ("qk3", 0)])
SCHED = [x for x in SCHED if x]
SCHED += [("x2", 1), ("a1", 1), ("g", 1), ("a2", 1), ("f2", 1), ("lead", 0), ("n3", 1), ("lead", 1), ("qk3", 1)]
SCHED += [("lead", n) for n in range(2, NLEAD)] + [("step", n) for n in range(SOLO)]
SCHED += weave([("step", n) for n in range(SOLO, NSTEP)],
               [("oa", 0), ("oa", 1)] + parts_of("p3", 0, TWO) + [("end", 0)])
SCHED += [("ot", 1)] + parts_of("p3", 1, TWO) + [("end", 1)]


def turned(b, stage):
    return [(b, stage, h, k) for h in range(NC) for k in range(KB)]


def act_jobs(stage, b):
    if stage in ("n0", "m", "n1", "n2", "x2", "n3", "ot"):
        return turned(b, stage)
    if stage in ("u0", "u1"):
        b, part = divmod(b, MLPP)
        c, h = divmod(part, MLPP // NC)
        n = NF * NC // MLPP
        return [(b, "h" + stage[1], c, f) for f in range(h * n, (h + 1) * n)]
    if stage == "qkv":
        return [(b, w, c, k) for w in "qk" for c in range(NC) for k in range(KB)]
    if stage == "att":
        jobs = []
        for c in range(NC):
            jobs += [(b, "p", c * TPC + t, s) for t in range(TPC) for s in range(2)] + [(b, "o", c, k) for k in range(KB)]
        return jobs
    if stage == "g":
        return [(b, "g", c, k) for c in range(NC) for k in range(KB)]
    if stage == "qk3":
        return [(b, w, c, k) for k in range(KB) for w in ("q3", "k3") for c in range(NC)]
    return []


def dve_jobs(stage, b):
    if stage == "lr":
        return [(b, "lr")]
    if stage == "bu":
        return [(b, "bu", c, s) for c in range(NC) for s in range(2)]
    if stage in ("a1", "a2"):
        return [(b, stage, c) for c in range(NC)]
    if stage in ("d0", "d1", "p3"):
        b, j = divmod(b, TWO)
        return [(b, {"d0": "w20", "d1": "w21", "p3": "p3"}[stage], j)]
    if stage == "oa":
        return [(0, "ot", b, k) for k in range(KB)]
    out = {"y0": "y0", "qkv": "v1", "pr": "pr", "f2": "f2", "qk3": "v3"}.get(stage)
    return [(b, out, j) for j in range(TWO)] if out else []


def number(jobs_of):
    jobs = [j for stage, b in SCHED for j in jobs_of(stage, b)]
    return {j: n for n, j in enumerate(jobs)}


def order(*stages):
    return {x: n for n, x in enumerate(x for x in SCHED if x[0] in stages)}


def build(nc, I, out):
    AJ, DJ = number(act_jobs), number(dve_jobs)
    NORM = order("n0", "y0", "h0", "pr", "f2", "end")
    PRE = order("y0", "h0", "pr", "f2", "end")
    ctx = ExitStack()
    with ctx:
        def sb(name, shape, dt=F32):
            return ctx.enter_context(nc.sbuf_tensor(name, shape, dt))

        def sem(name):
            return ctx.enter_context(nc.semaphore(name))

        X = sb("X", [P, B, NT, D])
        XN = sb("XN", [P, B, NT, D])
        XT = sb("XT", [P, B, KB, T])
        W12 = sb("W12", [P, 2, KB * FF])
        W1 = W12[:, 0].rearrange("p (k n) -> p k n", k=KB)
        W2 = W12[:, 1].rearrange("p (f d) -> p f d", f=NF)
        WA = sb("WA", [P, 4, KB, D])
        WQ3 = sb("WQ3", [P, 3, KB, D])
        WP3 = sb("WP3", [P, KB, D])
        C2 = sb("C2", [P, T])
        S2 = sb("S2", [P, T])
        BA = sb("BA", [P, 2, KB, P])
        CT = sb("CT", [P, 2, D])
        CG = sb("CG", [P, B, 2, D])
        DG = sb("DG", [P, B, KB, P])
        BC = sb("BC", [P, 6, D])
        GB = sb("GB", [P, B, 4, D])
        BG = sb("BG", [P, B, D])
        VEC = sb("VEC", [P, NVC])
        PAR = sb("PAR", [P, B, NPAR * KB])
        LA = sb("LA", [P, B, 2, KB, RANK])
        LB = sb("LB", [RANK, B, 2, D])
        ident = sb("ident", [P, P])
        identb = sb("identb", [P, P], BF16)
        SEL = sb("SEL", [B, B, P])
        ST = sb("ST", [P, B, NT, 6])
        MV = sb("MV", [P, B, NT, 2])
        VE = sb("VE", [P, B, NT])
        RST = sb("RST", [P, B, NT])
        MHALF = sb("MHALF", [P, NT])
        NM = sb("NM", [P, NT])
        NMS = sb("NMS", [P, B, NT])
        SM = sb("SM", [P, B, NT])
        RSM = sb("RSM", [P, B, NT])
        RVEC = sb("RVEC", [P, 1])
        SG = sb("SG", [P, 2])
        TM = sb("TM", [P, 28])
        TI = sb("TI", [P, 1], I32)
        CTX = sb("CTX", [P, 2, KB, B])
        HIDC = sb("HIDC", [P, KB, GCOL])
        LAB = sb("LAB", [P, 2, KB, RANK])
        COLR = sb("COLR", [P, NCB, B])
        NMX = sb("NMX", [P, 2, UNIT])
        NMR = sb("NMR", [P, UNIT])
        NMP = sb("NMP", [P, NPART, UNIT], BF16)
        NMT = sb("NMT", [NPART * UNIT, P], BF16)
        RC = sb("RC", [P, UNIT])
        UO = sb("UO", [P, HALF])
        TG = sb("TG", [P, HALF])
        R = sb("R", [P, 20736])

        def flat(a):
            return a.rearrange("p t d -> p (t d)")

        WAF = WA[:, :, :, :].rearrange("p a k d -> p (a k d)")
        WQF = WQ3[:, :, :, :].rearrange("p a k d -> p (a k d)")
        HT = R[:, 0:8192].rearrange("p (f t) -> p f t", f=NF)
        WC = R[:, 0:KB * NCOND].rearrange("p (k n) -> p k n", k=KB)
        ROWS = R[0:B, 8192:8192 + NCOND]
        LNR = R[0:B, 11776:11776 + 5 * D].rearrange("p (s d) -> p s d", s=5)
        TR = R[0:B, 13056:13056 + 6 * D].rearrange("p (s d) -> p s d", s=6)
        BX = R[:, 14592:14592 + 4 * D].rearrange("p (s d) -> p s d", s=4)
        T1 = R[:, 15616:15616 + HALF]
        T2 = R[:, 16128:16128 + HALF]
        ANG = R[:, 7168:7168 + 4 * 2 * LEVELS].rearrange("p (a s n) -> p a s n", a=4, s=2)
        TURNS = ANG[:, 0, 0, :]
        ARG = ANG[:, 1]
        WRAP = ANG[:, 2, 0, :]
        TRIG = ANG[:, 3]
        ZB = [[R[:, 8192 + (3 * b + i) * T:8192 + (3 * b + i + 1) * T] for i in range(3)] for b in range(B)]
        W2L = R[:, 16640:16640 + 4096].rearrange("p (s k n) -> p s k n", s=2, k=KB)
        LRO = WQF[:, 512:512 + 2 * LG].rearrange("p (s n) -> p s n", s=2)
        LBB = T1[0:RANK].rearrange("p (s d) -> p s d", s=2)
        L2W1 = WQF[:, 0:512].rearrange("p (k n) -> p k n", k=KB)
        QT = R[:, 8192:10240].rearrange("p (k t) -> p k t", k=KB)
        KT = R[:, 10240:12288].rearrange("p (k t) -> p k t", k=KB)
        V = R[:, 12288:14336].rearrange("p (t d) -> p t d", t=NT)
        PT = R[:, 16384:20480].rearrange("p (k q) -> p k q", k=NT)
        OT = [flat(XN[:, b]).rearrange("p (k t) -> p k t", k=KB) for b in range(B)]
        GT = R[:, 8192:12288].rearrange("p (b k t) -> p b k t", b=B, k=KB)
        Y8 = R[0:RANK, 12288:16384].rearrange("p (b s t) -> p b s t", b=B, s=2)
        STK = R[0:KFULL, 0:NSLOT * 4096].bitcast(BF16).rearrange("p (s w n) -> p s w n", s=NSLOT, w=2)
        QS = STK[:, :, 0, :].rearrange("p s (c h q) -> p s c h q", c=NC, h=GH)
        KS = STK[:, :, 1, :].rearrange("p s (h t) -> p s h t", h=GH)
        PB = R[:, 12288:16384].rearrange("p (s j q) -> p s j q", s=2, j=GH)
        VP = [a.rearrange("p (t h c) -> p t h c", t=NT, h=HEADS)
              for a in (R[:, 16384:20480], W12[:, :, :].rearrange("p w n -> p (w n)"))]
        O = [XN[:, b] for b in range(B)]
        QF = [[flat(XN[:, b])[:, n * HALF:(n + 1) * HALF] for n in range(4)] for b in range(B)]
        QF[0] += QF[0]
        QF[1] += [R[:, 8192 + n * HALF:8192 + (n + 1) * HALF] for n in range(4)]
        PARTS = WAF[:, 0:1536].bitcast(BF16).rearrange("p (s n q) -> p s n q", s=2, n=NPART)
        RP = WAF[:, 1536:2048]

        PA = ctx.enter_context(nc.psum_tensor("PA", [P, 4, HALF], F32))
        PD = ctx.enter_context(nc.psum_tensor("PD", [P, 4, HALF], F32))
        PDF = PD[:, :, :].rearrange("p s q -> p (s q)").rearrange("p (s q) -> p s q", s=2)
        PTB = PA[:, 3, 0:64].bitcast(BF16)
        DR = nc.dram_tensor("qk_parts", [B, 2, KB, NPART, P, T], BF16, kind="Internal").ap()

        s_vin = sem("vectors_in")
        s_rin = sem("rows_in")
        s_cin = sem("cond_weights_in")
        s_bin = sem("broadcast_rows_in")
        s_xin = [[sem(f"x_in{b}{c}") for c in range(NC)] for b in range(B)]
        s_w1in = [sem("w1_layer0_in"), sem("w1_layer1_in")]
        s_w2in = [sem("w2_layer0_in"), sem("w2_layer1_in")]
        s_wain = sem("attention_weights_in")
        s_w3in = sem("last_attention_weights_in")
        s_l2in = [sem("adapter_weights_in0"), sem("adapter_weights_in1")]
        s_const = sem("constants_ready")
        s_cfull = sem("cond_bank_full")
        s_cev = sem("cond_bank_evacuated")
        s_ada_st = sem("ada_stats")
        s_ada_rs = sem("ada_rstd")
        s_ada = sem("ada_rows_ready")
        s_small = sem("small_bank_full")
        s_ctx = sem("small_bank_copied")
        s_hid = sem("hidden_row_ready")
        s_gelu = sem("hidden_gelu_ready")
        s_ang = sem("angles_ready")
        s_trig = sem("trig_ready")
        s_sb = sem("film_rows_ready")
        s_bx = sem("state_maps_ready")
        s_par = sem("params_ready")
        s_hidz = sem("hidden_columns_zeroed")
        s_lbin = sem("adapter_bias_in")
        s_lowrank = sem("adapter_maps_ready")
        s_lrst = [sem("adapter_rows_spread0"), sem("adapter_rows_spread1")]
        s_vp = sem("v_padding_ready")
        s_afull = sem("act_bank_full")
        s_aev = sem("act_bank_evacuated")
        s_dfull = sem("dve_bank_full")
        s_dev = sem("dve_bank_evacuated")
        s_dstep = sem("dve_step")
        s_gstep = sem("pool_step")
        s_stats = sem("stats_ready")
        s_rstd = sem("rstd_ready")
        s_xn = sem("xn_ready")
        s_pre = sem("bias_added")
        s_z = sem("states_ready")
        s_zc = sem("states_cos_ready")
        s_zs = sem("states_sin_ready")
        s_sfull = sem("scores_full")
        s_max1 = sem("scores_max")
        s_nmax = sem("negmax_ready")
        s_exp1 = sem("probs1_ready")
        s_hi = sem("qk_high_ready")
        s_rest = sem("qk_rest_ready")
        s_mid = sem("qk_mid_ready")
        s_parts = sem("qk_parts_ready")
        s_ones = sem("ones_rows_ready")
        s_spill = [[sem(f"parts{b}_stored{u}") for u in range(2)] for b in range(B)]
        s_stack = [sem(f"group_stack_in{g}") for g in range(B * NG)]
        s_mfull = sem("maxpass_full")
        s_mred = sem("maxpass_reduced")
        s_nmp = sem("negmax_parts")
        s_nmtf = sem("negmax_t_full")
        s_nmt = sem("negmax_t_ready")
        s_nmrow = [sem(f"negmax_rows{m % 4}") for m in range(4)]
        s_efull = sem("energy_full")
        s_exp3 = sem("probs3_ready")
        s_pv = sem("pv_done")
        s_uo = sem("heads_out_copied")
        s_ut = sem("heads_out_t_full")
        s_on = sem("heads_out_normed")
        s_scaled = sem("out_scaled")
        s_fin = sem("out_ready")
        s_out = sem("out_stored")

        STACKED = 16 * (NC + 1) * NPAIR

        def nmrow_in(e, m):
            e.wait_ge(s_nmrow[m % 4], 16 * NPART * (m // 4 + 1))

        def store_parts(e, j):
            b, r = divmod(j, 2 * KB * NC)
            k, r = divmod(r, 2 * NC)
            side, c = divmod(r, NC)
            e.dma_start(DR[b, side, k, :, :, c * HALF:(c + 1) * HALF].rearrange("s p q -> p s q"),
                        PARTS[:, j % 2]).then_inc(s_spill[b][j % 2], 16)

        def parts_stored(e, j):
            b, r = divmod(j - 2, 2 * KB * NC)
            e.wait_ge(s_spill[b][j % 2], 16 * (r // 2 + 1))

        def turn_step(m):
            return (UNIT * (m + 1) - LEAD) // 2 + 1

        def run(engine_stages):
            for stage, b in SCHED:
                if stage in engine_stages:
                    engine_stages[stage](b)

        QK3_JOBS = [(name, c, k) for k in range(KB) for name in ("q3", "k3") for c in range(NC)]

        block = ctx.enter_context(nc.Block())

        @block.sync
        def _(sp):
            def kp(a):
                return a.rearrange("(k p) n -> p k n", p=P)

            sp.dma_start(VEC[:, :], I["vec"]).then_inc(s_vin, 16)
            sp.dma_start(BX[:, 0:2, :], I["b2x"]).then_inc(s_vin, 16)
            sp.dma_start(TR[:, 0, :], I["t"]).then_inc(s_rin, 16)
            sp.dma_start(LNR[:, :, :], I["lnrow"].partition_broadcast(B)).then_inc(s_rin, 16)
            sp.dma_start(CTX[:, 0, :, :], I["tT"]).then_inc(s_rin, 16)
            sp.dma_start(ROWS, I["bcond"].partition_broadcast(B)).then_inc(s_rin, 16)
            sp.dma_start(WC, kp(I["wcond"])).then_inc(s_cin, 16)
            sp.dma_start(L2W1, kp(I["l2_w1"])).then_inc(s_cin, 16)
            for b in range(B):
                for c in range(NC):
                    sp.dma_start(X[:, b, c * TPC:(c + 1) * TPC, :],
                                 I["x"][b, c * HALF:(c + 1) * HALF, :].rearrange("(t p) d -> p t d", p=P)
                                 ).then_inc(s_xin[b][c], 16)
            sp.dma_start(CT[:, :, :], I["ct"]).then_inc(s_bin, 16)
            sp.dma_start(BC[:, :, :], I["bc"].partition_broadcast(P)).then_inc(s_bin, 16)
            for n in range(NLCH + 2):
                if n < NLCH:
                    if n >= 2:
                        sp.wait_ge(s_dfull, DJ[(n - 2, "lr")] + 1)
                    cols = slice(n * LCH, (n + 1) * LCH)
                    sp.dma_start(W2L[:, n % 2], kp(I["l2_w2"])[:, :, cols]).then_inc(s_l2in[n % 2], 16)
                if n == 1:
                    sp.dma_start(W1[:, :, :], kp(I["w1_0"])).then_inc(s_w1in[0], 16)
                    sp.dma_start(W2[:, :, :], kp(I["w2_0"])).then_inc(s_w2in[0], 16)
                if n >= 2:
                    i = n - 2
                    sp.wait_ge(s_dev, DJ[(i, "lr")] + 1)
                    which, part = divmod(i * LCH, RANK * D)
                    for b in range(B):
                        src = LRO[b:P:GCOL, i % 2, :]
                        if which < 2:
                            k, p0 = divmod(part // RANK, P)
                            dst = LA[p0:p0 + LCH // RANK, b, which, k, :]
                            src = src.rearrange("a (p r) -> a p r", r=RANK)
                        else:
                            r0 = part // D
                            dst = LB[r0:r0 + LCH // D, b, which - 2, :]
                        sp.dma_start(dst, src).then_inc(s_lrst[i % 2], 16)
            sp.dma_start(LAB[:, :, :, :], I["l2_b2"][0:2 * RANK * D].rearrange("(s k p r) -> p s k r", s=2, k=KB, r=RANK)
                         ).then_inc(s_lbin, 16)
            sp.wait_ge(s_z, B * NC)
            sp.dma_start(LBB, I["l2_b2"][2 * RANK * D:].rearrange("(s r d) -> r s d", s=2, d=D)).then_inc(s_lbin, 16)
            for w in range(2):
                sp.dma_start(WA[:, 2 * w:2 * w + 2], I["wa"][:, 2 * w:2 * w + 2]).then_inc(s_wain, 16)
            for u in range(2):
                sp.wait_ge(s_lrst[u], 16 * B * NLCH // 2)
            sp.dma_start(WQ3[:, :, :, :], I["wqkv3"]).then_inc(s_w3in, 16)
            sp.dma_start(WP3[:, :, :], kp(I["wp3"])).then_inc(s_w3in, 16)
            sp.wait_ge(s_afull, AJ[(1, "h0", NC - 1, NF - 1)] + 1)
            sp.dma_start(W1[:, :, :], kp(I["w1_1"])).then_inc(s_w1in[1], 16)
            sp.wait_ge(s_dfull, DJ[(1, "w20", TWO - 1)] + 1)
            sp.dma_start(W2[:, :, :], kp(I["w2_1"])).then_inc(s_w2in[1], 16)
            loaded = 0

            def stack(upto):
                nonlocal loaded
                while loaded < upto:
                    gg = loaded
                    b, g = divmod(gg, NG)
                    k, r = g // (NG // KB), (g * GH * HD) % P
                    if gg >= NSLOT:
                        sp.wait_ge(s_pv, (gg - NSLOT + 1) * NC * NT)
                    for u in range(2):
                        sp.wait_ge(s_spill[b][u], 16 * 2 * (k + 1))
                    heads = DR[b, :, k, :, r:r + GH * HD, :]
                    for n, pair in enumerate(PAIRS):
                        rows = slice(n * HD, (n + 1) * HD)
                        sp.dma_start(KS[rows, gg % NSLOT], heads[1, pair[1]].rearrange("(h d) t -> d h t", d=HD)
                                     ).then_inc(s_stack[gg], 16)
                        for c in range(NC):
                            sp.dma_start(QS[rows, gg % NSLOT, c],
                                         heads[0, pair[0], :, c * HALF:(c + 1) * HALF].rearrange("(h d) t -> d h t", d=HD)
                                         ).then_inc(s_stack[gg], 16)
                    loaded += 1

            for j in range(2 * KB * NC):
                sp.wait_ge(s_parts, j + 1)
                store_parts(sp, j)
            sp.wait_ge(s_dfull, DJ[(1, "w21", TWO - 1)] + 1)
            stack(2)
            for m in range(NUNIT):
                gg, c = divmod(m, NC)
                sp.wait_ge(s_nmt, m + 1)
                for s in range(NPART):
                    sp.dma_start(QS[KSTK + s:KSTK + s + 1, gg % NSLOT, c],
                                 NMT[s * UNIT:(s + 1) * UNIT, :]).then_inc(s_nmrow[m % 4], 16)
                if m == 1:
                    sp.wait_ge(s_parts, B * 2 * KB * NC)
                    stack(NSLOT)
                if c == 0 and gg >= 1 and gg + 2 < B * NG:
                    stack(gg + 3)
            for b in range(B):
                for c in range(NC):
                    sp.wait_ge(s_fin, b * NC + c + 1)
                    sp.dma_start(out[b, c * HALF:(c + 1) * HALF, :].rearrange("(t p) d -> p t d", p=P),
                                 XN[:, b, c * TPC:(c + 1) * TPC, :]).then_inc(s_out, 16)
            sp.wait_ge(s_out, 16 * B * NC)

        @block.gpsimd
        def _(po):
            po.memset(ident[:, :], 0.0).then_inc(s_const, 1)
            po.memset(SEL[:, :, :], 0.0).then_inc(s_const, 1)
            po.memset(MHALF[:, :], -0.5).then_inc(s_const, 1)
            po.memset(HIDC[:, :, :], 0.0).then_inc(s_hidz, 1)
            po.wait_ge(s_const, 3)
            po.affine_select(out=ident[:, :], in_=ident[:, :], compare_op=ALU.not_equal, fill=1.0, base=0,
                             pattern=[[-1, P]], channel_multiplier=1).then_inc(s_const, 1)
            po.affine_select(out=SEL[:, :, :], in_=SEL[:, :, :], compare_op=ALU.not_equal, fill=1.0, base=0,
                             pattern=[[-1, B], [0, P]], channel_multiplier=1).then_inc(s_const, 1)
            po.wait_ge(s_const, 5)
            po.tensor_copy(identb[:, :], ident[:, :]).then_inc(s_const, 1)
            po.wait_ge(s_ada_st, 1)
            po.tensor_scalar(VE[0:B, 0, 0:1], MV[0:B, 0, 0, 1:2], 1e-5, None, ALU.add).then_inc(s_ada_rs, 1)
            po.wait_ge(s_ada_rs, 1)
            po.tensor_tensor(RST[0:B, 0, 0:1], VE[0:B, 0, 0:1], MHALF[0:B, 0:1], ALU.pow).then_inc(s_ada_rs, 1)
            cnt = [0]

            def link(i):
                cnt[0] += 1
                i.then_inc(s_gstep, 1)
                po.wait_ge(s_gstep, cnt[0])

            def rstd(stage, b, eps, rms=False):
                for h in range(NC):
                    po.wait_ge(s_stats, NORM[(stage, b)] * NC + h + 1)
                    t = slice(h * TPC, (h + 1) * TPC)
                    ve_ = VE[:, b, t]
                    if rms:
                        link(po.tensor_tensor(ve_, MV[:, b, t, 0], MV[:, b, t, 0], ALU.mult))
                        link(po.tensor_tensor(ve_, ve_, MV[:, b, t, 1], ALU.add))
                        link(po.tensor_scalar(ve_, ve_, eps, None, ALU.add))
                    else:
                        link(po.tensor_scalar(ve_, MV[:, b, t, 1], eps, None, ALU.add))
                    po.tensor_tensor(RST[:, b, t], ve_, MHALF[:, t], ALU.pow).then_inc(s_rstd, 1)

            def prebias(stage, b, row, sem_, n):
                for h in range(NC):
                    po.wait_ge(sem_, n * NC + h + 1)
                    x = X[:, b, h * TPC:(h + 1) * TPC, :]
                    po.tensor_tensor(x, x, row.unsqueeze(1).to_broadcast([P, TPC, D]), ALU.add).then_inc(s_pre, 1)

            def normed(stage, eps, row=None, rms=False):
                def f(b):
                    rstd(stage, b, eps, rms)
                    if row is not None:
                        prebias(stage, b, row(b), s_xn, NORM[(stage, b)])
                return f

            def bu(b):
                for c in range(NC):
                    po.wait_ge(s_z, b * NC + c + 1)
                    q = slice(c * HALF, (c + 1) * HALF)
                    po.tensor_tensor(ZB[b][2][:, q], ZB[b][0][:, q], S2[:, q], ALU.mult).then_inc(s_zs, 1)

            def x2(b):
                if b == 0:
                    po.wait_ge(s_afull, AJ[(1, "o", NC - 1, KB - 1)] + 1)
                else:
                    po.wait_ge(s_dfull, DJ[(1, "w21", TWO - 1)] + 1)
                    po.wait_ge(s_gstep, cnt[0])
                    po.memset(KS[KSTK:KFULL, 0:2], 1.0).then_inc(s_ones, 1)
                    po.wait_ge(s_ones, 1)
                po.memset(VP[b][:, :, :, HD:2 * HD], 0.0).then_inc(s_vp, 1)
                po.wait_ge(s_vp, 2 * b + 1)
                po.memset(VP[b][:, :, :, HD:HD + 1], float(D) ** 0.5).then_inc(s_vp, 1)

            def qk3(b):
                for n in range(2 * KB * NC):
                    j = b * 2 * KB * NC + n
                    src = QF[b][n]
                    hi, mid, low = (PARTS[:, j % 2, i, :] for i in range(NPART))
                    if b == 0:
                        po.wait_ge(s_hi, j + 1)
                    else:
                        po.wait_ge(s_aev, AJ[(b, *QK3_JOBS[n])] + 1)
                        parts_stored(po, j)
                        po.tensor_copy(hi, src).then_inc(s_hi, 1)
                        po.wait_ge(s_hi, j + 1)
                    po.tensor_tensor(RP, src, hi, ALU.subtract).then_inc(s_rest, 1)
                    if b == 1:
                        po.wait_ge(s_rest, j + 1)
                        po.tensor_copy(mid, RP).then_inc(s_mid, 1)
                    po.wait_ge(s_mid, j + 1)
                    po.tensor_tensor(low, RP, mid, ALU.subtract).then_inc(s_parts, 1)
                    po.wait_ge(s_parts, j + 1)
                    if b == 1:
                        store_parts(po, j)
                if b == 1:
                    po.memset(KS[KSTK:KFULL, 2:3], 1.0).then_inc(s_ones, 1)
                    for u in range(2):
                        po.wait_ge(s_spill[1][u], 16 * KB * NC)

            def end(b):
                rstd("end", b, 1e-5)
                prebias("end", b, GB[:, b, B3, :], s_scaled, b)

            run({"n0": normed("n0", 1e-5), "bu": bu, "y0": normed("y0", 1e-5, lambda b: BG[:, b, :]),
                 "h0": normed("h0", 1e-6, lambda b: BC[:, BP, :], rms=True),
                 "pr": normed("pr", 1e-6, lambda b: BC[:, MB2, :], rms=True), "x2": x2,
                 "f2": normed("f2", 1e-5, lambda b: BC[:, BP3, :]), "qk3": qk3, "end": end})

        @block.scalar
        def _(act):
            act.wait_ge(s_ang, 1)
            act.activation(TRIG, ARG, ACT.Sin).then_inc(s_trig, 1)
            act.wait_ge(s_hid, 1)
            act.activation(TR[:, 3, :], TR[:, 2, :], ACT.Gelu).then_inc(s_gelu, 1)
            act.wait_ge(s_par, 1)
            seen = [0]

            def bank(*job):
                n = AJ[job]
                assert n == seen[0], (job, n, seen)
                seen[0] += 1
                act.wait_ge(s_afull, n + 1)
                return PA[:, n % 4, :]

            def vec(name, k=0):
                return VEC[:, VC[name] + k:VC[name] + k + 1]

            def modulated(stage, p):
                def f(b):
                    for h in range(NC):
                        for k in range(KB):
                            q = p * KB + k
                            act.activation(XT[:, b, k, h * HALF:(h + 1) * HALF], bank(b, stage, h, k), ACT.Identity,
                                           bias=PAR[:, b, q + KB:q + KB + 1], scale=PAR[:, b, q:q + 1]).then_inc(s_aev, 1)
                return f

            def copied(stage, dst, func=ACT.Copy):
                def f(b):
                    for h in range(NC):
                        for k in range(KB):
                            act.activation(dst(b)[:, k, h * HALF:(h + 1) * HALF], bank(b, stage, h, k), func).then_inc(s_aev, 1)
                return f

            def hidden(stage, func, bias, before):
                def f(part):
                    for b, tag, c, f_ in act_jobs(stage, part):
                        prev = before(b, c)
                        if prev is not None and f_ == 0:
                            act.wait_ge(s_dfull, DJ[prev] + 1)
                        act.activation(HT[:, f_, c * HALF:(c + 1) * HALF], bank(b, tag, c, f_), func,
                                       bias=vec(bias, f_)).then_inc(s_aev, 1)
                return f

            def qkv(b):
                for name, dst in (("q", QT), ("k", KT)):
                    for c in range(NC):
                        for k in range(KB):
                            act.activation(dst[:, k, c * HALF:(c + 1) * HALF], bank(b, name, c, k), ACT.Identity,
                                           bias=vec(name + "_b", k)).then_inc(s_aev, 1)

            def att(b):
                def probs_turn(t):
                    for s in range(2):
                        act.activation(PT[:, 4 * s:4 * s + 4, (t % TPC) * P:(t % TPC + 1) * P],
                                       bank(b, "p", t, s).rearrange("p (k q) -> p k q", k=4), ACT.Copy).then_inc(s_aev, 1)
                    if t % TPC == TPC - 1:
                        c = t // TPC
                        for k in range(KB):
                            act.activation(OT[b][:, k, c * HALF:(c + 1) * HALF], bank(b, "o", c, k),
                                           ACT.Copy).then_inc(s_aev, 1)

                for t in range(NT):
                    act.wait_ge(s_nmax, b * NT + t + 1)
                    act.activation(XT[:, b, t % 2, :], PDF[:, t % 2, :], ACT.Exp, bias=NMS[:, b, t:t + 1],
                                   scale=float(D) ** -0.5, accum_out=SM[:, b, t:t + 1]).then_inc(s_exp1, 1)
                    if t >= 1:
                        probs_turn(t - 1)
                probs_turn(NT - 1)

            def qk3(b):
                n = 0
                for k in range(KB):
                    for name in ("q3", "k3"):
                        for c in range(NC):
                            if b == 0 and n >= 4:
                                act.wait_ge(s_parts, n - 3)
                            act.activation(QF[b][n], bank(b, name, c, k), ACT.Identity,
                                           bias=vec(name + "_b", k)).then_inc(s_aev, 1)
                            n += 1

            def turn_max(m):
                act.wait_ge(s_nmtf, m + 1)
                if m >= 1:
                    nmrow_in(act, m - 1)
                act.activation(NMT[:, :], PTB[0:NPART * UNIT, :], ACT.Copy).then_inc(s_nmt, 1)

            def copy_heads_out(m):
                act.wait_ge(s_pv, (m + 1) * NT)
                if m >= 1:
                    act.wait_ge(s_ut, m)
                act.activation(UO[:, :], PA[:, 2, :], ACT.Copy).then_inc(s_uo, 1)

            def lead(part):
                if part == NLEAD - 1:
                    turn_max(0)

            def step(n):
                m, kt = divmod(n, NT)
                if n == 0:
                    act.wait_ge(s_dfull, DJ[(1, "f2", TWO - 1)] + 1)
                if n >= 2:
                    act.wait_ge(s_pv, n - 1)
                for j in range(GH):
                    if j == 2 and kt == 0 and m >= 1:
                        copy_heads_out(m - 1)
                    e = n * GH + j
                    act.wait_ge(s_efull, e + 1)
                    act.activation(PB[:, n % 2, j, :], PA[:, e % 2, :], ACT.Exp).then_inc(s_exp3, 1)
                for u in range(1, NUNIT):
                    if n == turn_step(u):
                        turn_max(u)
                if n == NSTEP - 1:
                    copy_heads_out(NUNIT - 1)

            def none(b, c):
                return None

            run({"n0": modulated("n0", PU), "m": modulated("m", PM), "n1": modulated("n1", P1),
                 "n2": modulated("n2", P2), "n3": modulated("n3", P3),
                 "u0": hidden("u0", ACT.Gelu_apprx_tanh, "b1", lambda b, c: (0, "w20", 2 * c + 1) if b else None),
                 "u1": hidden("u1", ACT.Gelu, "mb1", lambda b, c: (0, "w21", 2 * c + 1) if b else (1, "w20", 2 * c + 1)),
                 "qkv": qkv, "att": att, "x2": copied("x2", lambda b: XT[:, b]),
                 "g": copied("g", lambda b: GT[:, b], ACT.Gelu), "qk3": qk3, "lead": lead, "step": step,
                 "ot": copied("ot", lambda b: XT[:, b])})
            assert seen[0] == len(AJ)

        @block.tensor
        def _(pe):
            def row_bank(o, lhs, w, c0, full):
                for k in range(KB):
                    m = pe.matmul(o, CTX[:, lhs, k, :], w[:, k, c0:c0 + HALF], start=(k == 0), stop=(k == KB - 1))
                m.then_inc(full, 1)

            def row_columns(bank, row):
                for k in range(KB):
                    m = pe.transpose(PA[:, bank, k * B:(k + 1) * B], row[:, k * P:(k + 1) * P], ident[0:B, 0:B])
                m.then_inc(s_small, 1)

            pe.wait_ge(s_const, 6)
            pe.wait_ge(s_rin, 16 * 4)
            pe.wait_ge(s_cin, 16 * 2)
            for n in range(NROWJ):
                if n == 4:
                    pe.wait_ge(s_bx, 1)
                    for s in range(2):
                        for k in range(KB):
                            m = pe.transpose(PA[:, 0, (2 * s + k) * P:(2 * s + k + 1) * P],
                                             BX[:, 2 + s, k * P:(k + 1) * P], ident[:, :])
                    m.then_inc(s_small, 1)
                if n >= 4:
                    pe.wait_ge(s_cev, n - 3)
                row_bank(PD[0:B, n % 4, :], 0, WC, n * HALF, s_cfull)
            pe.wait_ge(s_ada, 1)
            row_columns(1, TR[:, 1, :])
            pe.wait_ge(s_cev, NROWJ)
            for n in range(NCB):
                m = pe.transpose(PA[:, 3, n * B:(n + 1) * B], ROWS[:, n * P:(n + 1) * P], ident[0:B, 0:B])
            m.then_inc(s_small, 1)
            pe.wait_ge(s_ctx, 2)
            for k in range(KB):
                m = pe.matmul(PA[0:B, 2, 0:D], CTX[:, 1, k, :], L2W1[:, k, :], start=(k == 0), stop=(k == KB - 1))
            m.then_inc(s_small, 1)
            pe.wait_ge(s_sb, 1)
            for b in range(B):
                pe.wait_ge(s_ctx, 3 if b == 0 else 4)
                for s, row in enumerate((ROWS[:, CW["gate_a"] * P:CW["gate_a"] * P + D],
                                         ROWS[:, CW["gate_ff"] * P:CW["gate_ff"] * P + D], TR[:, 4, :], TR[:, 5, :])):
                    m = pe.matmul(PA[:, s // 2, (s % 2) * D:(s % 2 + 1) * D], SEL[:, b, :], row, start=True, stop=True)
                m.then_inc(s_small, 1)
            pe.wait_ge(s_gelu, 1)
            row_columns(3, TR[:, 3, :])

            sa, sd = [0], [0]
            hold = {"a": lambda: pe.wait_ge(s_ctx, 6), "d": None}

            def bank(kind, jobs, seen, ps, ev, job, rows_):
                n = jobs[job]
                assert n == seen[0], (job, n, seen)
                seen[0] += 1
                if hold[kind]:
                    hold[kind]()
                    hold[kind] = None
                if n >= 4:
                    pe.wait_ge(ev, n - 3)
                return ps[0:rows_, n % 4, :]

            def abank(*job):
                return bank("a", AJ, sa, PA, s_aev, job, P)

            def dbank(*job, rows_=P):
                return bank("d", DJ, sd, PD, s_dev, job, rows_)

            def turn(stage, src, norm=None):
                def f(b):
                    for h in range(NC):
                        if norm:
                            pe.wait_ge(s_xn, NORM[(norm, b)] * NC + h + 1)
                        elif stage == "x2":
                            pe.wait_ge(s_dev, DJ[(b, "w21", 2 * h + 1)] + 1)
                        for k in range(KB):
                            o = abank(b, stage, h, k)
                            for t in range(TPC):
                                m = pe.transpose(o[:, t * P:(t + 1) * P], src(b)[:, h * TPC + t, k * P:(k + 1) * P],
                                                 ident[:, :])
                            m.then_inc(s_afull, 1)
                return f

            def project(o, w, col, b, h, full):
                for k in range(KB):
                    m = pe.matmul(o, w[:, k, col:col + P], XT[:, b, k, h * HALF:(h + 1) * HALF],
                                  start=(k == 0), stop=(k == KB - 1))
                m.then_inc(full, 1)

            def tokens_bank(b, tag, j, lhs, rhs, nk):
                o = dbank(b, tag, j)
                for u in range(2):
                    t = 2 * j + u
                    for k in range(nk):
                        m = pe.matmul(o[:, u * D:(u + 1) * D], lhs(k)[:, t * P:(t + 1) * P], rhs(k),
                                      start=(k == 0), stop=(k == nk - 1))
                m.then_inc(s_dfull, 1)

            def tokens_out(b, tag, lhs, rhs, nk, ready):
                for j in range(TWO):
                    if ready:
                        ready(j)
                    tokens_bank(b, tag, j, lhs, rhs, nk)

            def xt_ready(b, stage, h):
                pe.wait_ge(s_aev, AJ[(b, stage, h, KB - 1)] + 1)

            def lr(n):
                pe.wait_ge(s_ctx, 6)
                pe.wait_ge(s_l2in[n % 2], 16 * (n // 2 + 1))
                o = dbank(n, "lr")
                for k in range(KB):
                    for j in range(P // GCOL):
                        m = pe.matmul(o[GCOL * j:GCOL * (j + 1), 0:LG], HIDC[:, k, :],
                                      W2L[:, n % 2, k, j * LG:(j + 1) * LG], start=(k == 0), stop=(k == KB - 1))
                m.then_inc(s_dfull, 1)

            def bu(b):
                for c in range(NC):
                    xt_ready(b, "n0", c)
                    for s in range(2):
                        project(dbank(b, "bu", c, s), BA[:, s], 0, b, c, s_dfull)

            def y0(b):
                pe.wait_ge(s_par, 2)
                for j in range(TWO):
                    pe.wait_ge(s_zc, b * NC + j // 2 + 1)
                    pe.wait_ge(s_zs, b * NC + j // 2 + 1)
                    o = dbank(b, "y0", j)
                    for u in range(2):
                        tt = slice((2 * j + u) * P, (2 * j + u + 1) * P)
                        pe.matmul(o[:, u * D:(u + 1) * D], ZB[b][1][:, tt], CG[:, b, 0, :], start=True, stop=False)
                        for k in range(KB):
                            pe.matmul(o[:, u * D + k * P:u * D + (k + 1) * P], XT[:, b, k, tt], DG[:, b, k, :],
                                      start=False, stop=False)
                        m = pe.matmul(o[:, u * D:(u + 1) * D], ZB[b][2][:, tt], CG[:, b, 1, :], start=False, stop=True)
                    m.then_inc(s_dfull, 1)

            def up(stage, layer, src):
                def f(part):
                    pe.wait_ge(s_w1in[layer], 16)
                    for b, tag, c, f_ in act_jobs(stage, part):
                        xt_ready(b, src, c)
                        project(abank(b, tag, c, f_), W1, f_ * P, b, c, s_afull)
                return f

            def mlp_down(stage, hidden, layer):
                def f(part):
                    pe.wait_ge(s_w2in[layer], 16)
                    (b, tag, j), = dve_jobs(stage, part)
                    pe.wait_ge(s_aev, AJ[(b, hidden, j // 2, NF - 1)] + 1)
                    tokens_bank(b, tag, j, lambda k: HT[:, k, :], lambda k: W2[:, k, :], NF)
                return f

            def qkv(b):
                pe.wait_ge(s_wain, 32)
                for name, w in (("q", 0), ("k", 1)):
                    for c in range(NC):
                        xt_ready(b, "n1", c)
                        for k in range(KB):
                            project(abank(b, name, c, k), WA[:, w], k * P, b, c, s_afull)
                tokens_out(b, "v1", lambda k: XT[:, b, k, :], lambda k: WA[:, 2, k, :], KB, None)

            def att(b):
                def scores(t):
                    if t >= 2:
                        pe.wait_ge(s_exp1, b * NT + t - 1)
                    for c in range(NC):
                        for k in range(KB):
                            m = pe.matmul(PDF[:, t % 2, c * HALF:(c + 1) * HALF], QT[:, k, t * P:(t + 1) * P],
                                          KT[:, k, c * HALF:(c + 1) * HALF], start=(k == 0), stop=(k == KB - 1))
                    m.then_inc(s_sfull, 1)

                def probs_turn(t):
                    pe.wait_ge(s_exp1, b * NT + t + 1)
                    for s in range(2):
                        o = abank(b, "p", t, s)
                        for k in range(4):
                            m = pe.transpose(o[:, k * P:(k + 1) * P], XT[:, b, t % 2, (4 * s + k) * P:(4 * s + k + 1) * P],
                                             ident[:, :])
                        m.then_inc(s_afull, 1)

                pe.wait_ge(s_dev, sd[0])
                pe.wait_ge(s_aev, AJ[(b, "k", NC - 1, KB - 1)] + 1)
                scores(0)
                scores(1)
                for t in range(NT):
                    probs_turn(t)
                    if t + 2 < NT:
                        scores(t + 2)
                    if t % TPC == TPC - 1:
                        c = t // TPC
                        pe.wait_ge(s_aev, AJ[(b, "p", t, 1)] + 1)
                        for k in range(KB):
                            o = abank(b, "o", c, k)
                            for kt in range(NT):
                                m = pe.matmul(o, V[:, kt, k * P:(k + 1) * P], PT[:, kt, :], start=(kt == 0),
                                              stop=(kt == NT - 1))
                            m.then_inc(s_afull, 1)
                hold["d"] = lambda: pe.wait_ge(s_exp1, (b + 1) * NT)

            def pr(b):
                tokens_out(b, "pr", lambda k: OT[b][:, k, :], lambda k: WA[:, 3, k, :], KB,
                           lambda j: pe.wait_ge(s_aev, AJ[(b, "o", j // 2, KB - 1)] + 1))

            def down(tag, src_tag, src, s):
                def f(b):
                    pe.wait_ge(s_lowrank, 1)
                    for c in range(NC):
                        xt_ready(b, src_tag, c)
                        o = dbank(b, tag, c, rows_=RANK)
                        for k in range(KB):
                            m = pe.matmul(o, LA[:, b, s, k, :], src(b)[:, k, c * HALF:(c + 1) * HALF], start=(k == 0),
                                          stop=(k == KB - 1))
                        m.then_inc(s_dfull, 1)
                return f

            def g(b):
                for c in range(NC):
                    pe.wait_ge(s_dev, DJ[(b, "a1", c)] + 1)
                    for k in range(KB):
                        pe.matmul(abank(b, "g", c, k), LB[:, b, 0, k * P:(k + 1) * P], Y8[:, b, 0, c * HALF:(c + 1) * HALF],
                                  start=True, stop=True).then_inc(s_afull, 1)

            def f2(b):
                tokens_out(b, "f2", lambda k: Y8[:, b, 1, :], lambda k: LB[:, b, 1, :], 1,
                           lambda j: pe.wait_ge(s_dev, DJ[(b, "a2", j // 2)] + 1))

            def qk3(b):
                pe.wait_ge(s_w3in, 32)
                for k in range(KB):
                    for w, name in enumerate(("q3", "k3")):
                        for c in range(NC):
                            xt_ready(b, "n3", c)
                            project(abank(b, name, c, k), WQ3[:, w], k * P, b, c, s_afull)
                tokens_out(b, "v3", lambda k: XT[:, b, k, :], lambda k: WQ3[:, 2, k, :], KB, None)

            def maxpass(n):
                m, r = divmod(n, UNIT)
                gg, c = divmod(m, NC)
                j, t = divmod(r, TPC)
                if n >= 2:
                    pe.wait_ge(s_mred, n - 1)
                if n % (NC * UNIT) == 0:
                    pe.wait_ge(s_stack[gg], STACKED)
                for kc in range(NC):
                    i = pe.matmul(PDF[:, n % 2, kc * HALF:(kc + 1) * HALF],
                                  QS[0:KSTK, gg % NSLOT, c, j, t * P:(t + 1) * P],
                                  KS[0:KSTK, gg % NSLOT, j, kc * HALF:(kc + 1) * HALF], start=True, stop=True)
                i.then_inc(s_mfull, 1)

            def turn_max(m):
                pe.wait_ge(s_nmp, m + 1)
                if m >= 2:
                    pe.wait_ge(s_on, m - 1)
                if m >= 1:
                    pe.wait_ge(s_nmt, m)
                pe.transpose(PTB[0:NPART * UNIT, :], NMP[:, :, :].rearrange("p s n -> p (s n)"),
                             identb[:, :]).then_inc(s_nmtf, 1)

            def turn_heads_out(m):
                pe.wait_ge(s_uo, m + 1)
                if m >= 1:
                    pe.wait_ge(s_on, m)
                pe.wait_ge(s_nmt, min(m + 2, NUNIT))
                for t in range(TPC):
                    i = pe.transpose(PA[:, 3, t * P:(t + 1) * P], UO[:, t * P:(t + 1) * P], ident[:, :])
                i.then_inc(s_ut, 1)

            def energy(step, j):
                m, kt = divmod(step, NT)
                gg, c = divmod(m, NC)
                e = step * GH + j
                if e >= 2:
                    pe.wait_ge(s_exp3, e - 1)
                pe.matmul(PA[:, e % 2, :], KS[:, gg % NSLOT, j, kt * P:(kt + 1) * P], QS[:, gg % NSLOT, c, j, :],
                          start=True, stop=True).then_inc(s_efull, 1)

            def times_v(step):
                m, kt = divmod(step, NT)
                gg, c = divmod(m, NC)
                b, g_ = divmod(gg, NG)
                pe.wait_ge(s_exp3, (step + 1) * GH)
                if kt == 0 and m >= 1:
                    pe.wait_ge(s_uo, m)
                for j in range(GH):
                    i = pe.matmul(PA[32 * j:32 * j + 32, 2, :], VP[b][:, kt, g_ * GH + j, :], PB[:, step % 2, j, :],
                                  start=(kt == 0), stop=(kt == NT - 1))
                i.then_inc(s_pv, 1)

            def lead(part):
                pe.wait_ge(s_dev, sd[0])
                per = LEAD // NLEAD
                for n in range(part * per, (part + 1) * per):
                    maxpass(n)
                if part == NLEAD - 1:
                    pe.wait_ge(s_aev, sa[0])
                    turn_max(0)
                hold["d"] = lambda: pe.wait_ge(s_mred, (part + 1) * per)

            def step(n):
                m, kt = divmod(n, NT)
                s = LEAD + 2 * n
                if n == 0:
                    pe.wait_ge(s_ones, 1)
                    pe.wait_ge(s_vp, 2 * B)
                    pe.wait_ge(s_dev, sd[0])
                    nmrow_in(pe, 0)
                    energy(0, 0)
                    energy(0, 1)
                energy(n, 2)
                energy(n, 3)
                if s < NMAX:
                    maxpass(s)
                    maxpass(s + 1)
                for u in range(1, NUNIT):
                    if n == turn_step(u):
                        turn_max(u)
                if kt == 1 and m >= 1:
                    turn_heads_out(m - 1)
                if n + 1 < NSTEP:
                    if kt == NT - 1:
                        nmrow_in(pe, m + 1)
                        if (m + 1) // NC == 2:
                            pe.wait_ge(s_ones, 2)
                    energy(n + 1, 0)
                    energy(n + 1, 1)
                times_v(n)
                if n == SOLO - 1:
                    hold["d"] = lambda: pe.wait_ge(s_mred, NMAX)
                if n == NSTEP - 1:
                    turn_heads_out(NUNIT - 1)
                    pe.wait_ge(s_on, NUNIT)

            def turn_first(h):
                for k in range(KB):
                    o = dbank(0, "ot", h, k)
                    for t in range(TPC):
                        m = pe.transpose(o[:, t * P:(t + 1) * P], O[0][:, h * TPC + t, k * P:(k + 1) * P], ident[:, :])
                    m.then_inc(s_dfull, 1)

            def p3(part):
                b, j = divmod(part, TWO)
                if b:
                    xt_ready(b, "ot", j // 2)
                else:
                    pe.wait_ge(s_dev, DJ[(b, "ot", j // 2, KB - 1)] + 1)
                tokens_bank(b, "p3", j, lambda k: XT[:, b, k, :], lambda k: WP3[:, k, :], KB)

            run({"n0": turn("n0", lambda b: XN[:, b], "n0"), "lr": lr, "bu": bu, "y0": y0,
                 "m": turn("m", lambda b: XN[:, b], "y0"), "u0": up("u0", 0, "m"), "d0": mlp_down("d0", "h0", 0),
                 "n1": turn("n1", lambda b: XN[:, b], "h0"), "qkv": qkv, "att": att, "pr": pr,
                 "n2": turn("n2", lambda b: XN[:, b], "pr"), "u1": up("u1", 1, "n2"), "d1": mlp_down("d1", "h1", 1),
                 "x2": turn("x2", lambda b: X[:, b]), "a1": down("a1", "x2", lambda b: XT[:, b], 0), "g": g,
                 "a2": down("a2", "g", lambda b: GT[:, b], 1), "f2": f2,
                 "n3": turn("n3", lambda b: XN[:, b], "f2"), "qk3": qk3, "lead": lead, "step": step,
                 "oa": turn_first, "ot": turn("ot", lambda b: O[b]), "p3": p3})
            assert sa[0] == len(AJ) and sd[0] == len(DJ)

        @block.vector
        def _(ve):
            cnt = [0]

            def link(i):
                cnt[0] += 1
                i.then_inc(s_dstep, 1)
                ve.wait_ge(s_dstep, cnt[0])

            l0 = link
            ve.wait_ge(s_vin, 32)
            def tm(n):
                return TM[:, n:n + 1]

            ROUND = 1.5 * 2.0 ** 23
            DT, LR_, TH, RR, A0, A1, A2 = 0, 1, 2, 3, 10, 11, 12

            def exp(o, x):
                l0(ve.tensor_scalar(tm(A0), tm(x), -87.0, 88.0, ALU.max, ALU.min))
                l0(ve.tensor_scalar(tm(A1), tm(A0), 1.4426950408889634, ROUND, ALU.mult, ALU.add))
                l0(ve.tensor_scalar(tm(A1), tm(A1), -ROUND, None, ALU.add))
                l0(ve.scalar_tensor_tensor(tm(A0), tm(A1), -0.693359375, tm(A0), ALU.mult, ALU.add))
                l0(ve.scalar_tensor_tensor(tm(A0), tm(A1), 2.12194440e-4, tm(A0), ALU.mult, ALU.add))
                coef = [1 / 5040, 1 / 720, 1 / 120, 1 / 24, 1 / 6, 0.5, 1.0]
                l0(ve.tensor_scalar(tm(A2), tm(A0), coef[0], coef[1], ALU.mult, ALU.add))
                for q in coef[2:] + [1.0]:
                    l0(ve.tensor_scalar(tm(A2), tm(A2), tm(A0), q, ALU.mult, ALU.add))
                l0(ve.tensor_scalar(tm(A1), tm(A1), 127.0, 2.0 ** 23, ALU.add, ALU.mult))
                l0(ve.tensor_copy(TI[:, :], tm(A1)))
                l0(ve.tensor_tensor(tm(o), tm(A2), TI[:, :].bitcast(F32), ALU.mult))

            lam_re, lam_im = (VEC[:, VC[n]:VC[n] + 1] for n in ("lam_re", "lam_im"))
            l0(ve.tensor_copy(tm(LR_), VEC[:, VC["log_step"]:VC["log_step"] + 1]))
            exp(DT, LR_)
            l0(ve.tensor_tensor(tm(LR_), lam_re, tm(DT), ALU.mult))
            l0(ve.tensor_tensor(tm(TH), lam_im, tm(DT), ALU.mult))
            exp(RR, LR_)
            PI1, PI2, PI3 = 6.28125, 1.93500518798828125e-3, 3.0199159819e-7
            angle = ARG[:, 1, :]
            l0(ve.tensor_copy(ARG[:, 1, 0:1], tm(TH)))
            n = 1
            while n < LEVELS:
                m = min(n, LEVELS - n)
                l0(ve.tensor_scalar(ARG[:, 1, n:n + m], ARG[:, 1, 0:m], 2.0 ** n, None, ALU.mult))
                n *= 2
            l0(ve.tensor_scalar(TURNS, angle, 1.0 / (2 * np.pi), ROUND, ALU.mult, ALU.add))
            l0(ve.tensor_scalar(TURNS, TURNS, -ROUND, None, ALU.add))
            for part in (PI1, PI2, PI3):
                l0(ve.scalar_tensor_tensor(angle, TURNS, -part, angle, ALU.mult, ALU.add))
            l0(ve.tensor_scalar(ARG[:, 0, :], angle, float(np.pi / 2), None, ALU.add))
            l0(ve.tensor_scalar(WRAP, ARG[:, 0, :], float(np.pi), float(-2 * np.pi), ALU.is_gt, ALU.mult))
            l0(ve.tensor_tensor(ARG[:, 0, :], ARG[:, 0, :], WRAP, ALU.add))
            ve.tensor_scalar(ARG, ARG, -3.1415925, 3.1415925, ALU.max, ALU.min).then_inc(s_ang, 1)
            ve.wait_ge(s_trig, 1)
            cos, sin = TRIG[:, 0, 0:1], TRIG[:, 1, 0:1]
            NR, NI, DEN, FR, FI, UU, WW = 14, 15, 16, 17, 18, 4, 5
            l0(ve.tensor_scalar(tm(NR), cos, tm(RR), -1.0, ALU.mult, ALU.add))
            l0(ve.tensor_tensor(tm(NI), sin, tm(RR), ALU.mult))
            l0(ve.tensor_tensor(tm(A0), lam_im, lam_im, ALU.mult))
            l0(ve.scalar_tensor_tensor(tm(DEN), lam_re, lam_re, tm(A0), ALU.mult, ALU.add))
            l0(ve.reciprocal(tm(DEN), tm(DEN)))
            l0(ve.tensor_tensor(tm(A0), tm(NI), lam_im, ALU.mult))
            l0(ve.scalar_tensor_tensor(tm(FR), tm(NR), lam_re, tm(A0), ALU.mult, ALU.add))
            l0(ve.tensor_tensor(tm(FR), tm(FR), tm(DEN), ALU.mult))
            l0(ve.tensor_tensor(tm(A0), tm(NR), lam_im, ALU.mult))
            l0(ve.scalar_tensor_tensor(tm(FI), tm(NI), lam_re, tm(A0), ALU.mult, ALU.subtract))
            l0(ve.tensor_tensor(tm(FI), tm(FI), tm(DEN), ALU.mult))
            lo, hi = slice(0, S5), slice(S5, 2 * S5)
            l0(ve.tensor_copy(TM[lo, UU:UU + 1], TM[lo, FR:FR + 1]))
            l0(ve.tensor_copy(TM[hi, UU:UU + 1], TM[hi, FI:FI + 1]))
            l0(ve.tensor_scalar(TM[lo, WW:WW + 1], TM[lo, FI:FI + 1], -1.0, None, ALU.mult))
            l0(ve.tensor_copy(TM[hi, WW:WW + 1], TM[hi, FR:FR + 1]))
            l0(ve.tensor_scalar(BX[:, 2, :], BX[:, 1, :], tm(WW), None, ALU.mult))
            l0(ve.scalar_tensor_tensor(BX[:, 2, :], BX[:, 0, :], tm(UU), BX[:, 2, :], ALU.mult, ALU.add))
            l0(ve.tensor_scalar(BX[:, 3, :], BX[:, 0, :], tm(WW), None, ALU.mult))
            ve.scalar_tensor_tensor(BX[:, 3, :], BX[:, 1, :], tm(UU), BX[:, 3, :], ALU.mult, ALU.subtract).then_inc(s_bx, 1)
            l0(ve.tensor_copy(RVEC[:, :], tm(RR)))
            l0(ve.memset(SG[lo, 0:1], 2.0))
            l0(ve.memset(SG[hi, 0:1], -2.0))
            l0(ve.memset(SG[:, 1:2], -2.0))
            ve.wait_ge(s_rin, 16 * 4)
            l0(ve.bn_stats(ST[0:B, 0, 0, :], TR[:, 0, :]))
            ve.bn_aggr(MV[0:B, 0, 0, :], ST[0:B, 0, 0, :]).then_inc(s_ada_st, 1)
            ve.wait_ge(s_ada_rs, 2)
            l0(ve.tensor_scalar(TR[:, 1, :], TR[:, 0, :], MV[0:B, 0, 0, 0:1], RST[0:B, 0, 0:1], ALU.subtract, ALU.mult))
            l0(ve.tensor_tensor(TR[:, 1, :], TR[:, 1, :], LNR[:, 0, :], ALU.mult))
            ve.tensor_tensor(TR[:, 1, :], TR[:, 1, :], LNR[:, 1, :], ALU.add).then_inc(s_ada, 1)

            def stats(b, ready, halves=range(NC)):
                for h in halves:
                    ready(h)
                    for t in range(h * TPC, (h + 1) * TPC):
                        i = ve.bn_stats(ST[:, b, t, :], X[:, b, t, :])
                    link(i)
                    for t in range(h * TPC, (h + 1) * TPC):
                        i = ve.bn_aggr(MV[:, b, t, :], ST[:, b, t, :])
                    i.then_inc(s_stats, 1)

            def normalise(stage, b, mean, sem_=s_xn):
                for h in range(NC):
                    ve.wait_ge(s_rstd, NORM[(stage, b)] * NC + h + 1)
                    for t in range(h * TPC, (h + 1) * TPC):
                        if mean:
                            i = ve.tensor_scalar(XN[:, b, t, :], X[:, b, t, :], MV[:, b, t, 0:1], RST[:, b, t:t + 1],
                                                 ALU.subtract, ALU.mult)
                        else:
                            i = ve.tensor_scalar(XN[:, b, t, :], X[:, b, t, :], RST[:, b, t:t + 1], None, ALU.mult)
                    i.then_inc(sem_, 1)

            for n in range(NROWJ):
                ve.wait_ge(s_cfull, n + 1)
                q = slice(n * HALF, (n + 1) * HALF)
                ve.tensor_tensor(ROWS[:, q], PD[0:B, n % 4, :], ROWS[:, q], ALU.add).then_inc(s_cev, 1)
                if n == 3:
                    ve.wait_ge(s_small, 1)
                    ve.tensor_copy(BA[:, :, :, :].rearrange("p s k n -> p (s k n)"), PA[:, 0, :]).then_inc(s_ctx, 1)
            ve.wait_ge(s_cev, NROWJ)
            gamma = ROWS[:, CW["gamma"] * P:CW["gamma"] * P + D]
            beta = ROWS[:, CW["beta"] * P:CW["beta"] * P + D]
            l0(ve.tensor_tensor(TR[:, 4, :], gamma, LNR[:, 3, :], ALU.mult))
            l0(ve.tensor_tensor(TR[:, 5, :], gamma, LNR[:, 4, :], ALU.mult))
            ve.tensor_tensor(TR[:, 5, :], TR[:, 5, :], beta, ALU.add).then_inc(s_sb, 1)
            ve.wait_ge(s_small, 2)
            ve.tensor_copy(CTX[:, 1, :, :].rearrange("p k b -> p (k b)"), PA[:, 1, 0:KB * B]).then_inc(s_ctx, 1)
            ve.wait_ge(s_small, 3)
            ve.tensor_copy(COLR[:, :, :].rearrange("p n b -> p (n b)"), PA[:, 3, 0:NCB * B]).then_inc(s_ctx, 1)
            ve.wait_ge(s_small, 4)
            ve.tensor_tensor(TR[:, 2, :], PA[0:B, 2, 0:D], LNR[:, 2, :], ALU.add).then_inc(s_hid, 1)
            for b in range(B):
                ve.wait_ge(s_small, 5 + b)
                ve.tensor_copy(GB[:, b].rearrange("p (s u) d -> p s (u d)", s=2), PA[:, 0:2, :]).then_inc(s_ctx, 1)
            ve.wait_ge(s_ctx, 5)

            def c(name):
                return COLR[:, CW[name]:CW[name] + KB, :]

            def v(name):
                return VEC[:, VC[name]:VC[name] + KB].unsqueeze(2).to_broadcast([P, KB, B])

            def p(n):
                return PAR[:, :, n * KB:(n + 1) * KB].rearrange("p b k -> p k b")

            sf, sc, gb = (TM[:, 16 + 4 * n:20 + 4 * n].rearrange("p (k b) -> p k b", k=KB) for n in range(3))
            ve.tensor_scalar(p(PU), c("scale_a"), 1.0, None, ALU.add)
            ve.tensor_copy(p(PU + 1), c("shift_a"))
            ve.tensor_scalar(sf, c("scale_ff"), 1.0, None, ALU.add)
            ve.tensor_tensor(gb, c("gamma"), v("ln3_b"), ALU.mult)
            ve.scalar_tensor_tensor(p(P1), c("f1_scale"), 1.0, v("norm1"), ALU.add, ALU.mult)
            ve.tensor_copy(p(P1 + 1), c("f1_shift"))
            ve.scalar_tensor_tensor(p(P2), c("f2_scale"), 1.0, v("norm2"), ALU.add, ALU.mult)
            ve.tensor_copy(p(P2 + 1), c("f2_shift"))
            l0(ve.tensor_tensor(p(P3), c("gamma"), v("ln3_g"), ALU.mult))
            ve.scalar_tensor_tensor(p(PM), c("scale_c"), 1.0, sf, ALU.add, ALU.mult)
            ve.tensor_tensor(p(P3 + 1), gb, c("beta"), ALU.add)
            l0(ve.tensor_tensor(sc, c("shift_c"), sf, ALU.mult))
            ve.tensor_tensor(p(PM + 1), sc, c("shift_ff"), ALU.add).then_inc(s_par, 1)
            ve.wait_ge(s_small, 7)
            ve.wait_ge(s_hidz, 1)
            ve.tensor_copy(HIDC[:, :, 0:B], PA[:, 3, 0:KB * B].rearrange("p (k b) -> p k b", b=B)).then_inc(s_ctx, 1)

            sd = [0]

            def bank(*job, rows_=P):
                n = DJ[job]
                assert n == sd[0], (job, n, sd)
                sd[0] += 1
                ve.wait_ge(s_dfull, n + 1)
                return PD[0:rows_, n % 4, :]

            def two(j):
                return slice(2 * j, 2 * j + 2)

            def pair(a):
                return a.rearrange("p (u d) -> p u d", u=2)

            def row2(a):
                return a.unsqueeze(1).to_broadcast([P, 2, D])

            def add_bank(b, tag, j, pre=None):
                if pre:
                    ve.wait_ge(s_pre, PRE[pre] * NC + j // 2 + 1)
                x = X[:, b, two(j), :]
                ve.tensor_tensor(x, pair(bank(b, tag, j)), x, ALU.add).then_inc(s_dev, 1)

            def add_out(b, tag):
                for j in range(TWO):
                    add_bank(b, tag, j)

            def after(b, tag):
                return lambda h: ve.wait_ge(s_dev, DJ[(b, tag, 2 * h + 1)] + 1)

            def n0(b):
                stats(b, lambda h: ve.wait_ge(s_xin[b][h], 16))
                normalise("n0", b, True)

            def table(_):
                ve.memset(C2[:, 0:1], 1.0)
                link(ve.memset(S2[:, 0:1], 0.0))
                for i in range(LEVELS):
                    n = 1 << i
                    a, q = slice(0, n), slice(n, 2 * n)
                    cos, sin = TRIG[:, 0, i:i + 1], TRIG[:, 1, i:i + 1]
                    ve.tensor_scalar(T1[:, a], S2[:, a], sin, None, ALU.mult)
                    link(ve.tensor_scalar(T2[:, a], C2[:, a], sin, None, ALU.mult))
                    ve.scalar_tensor_tensor(C2[:, q], C2[:, a], cos, T1[:, a], ALU.mult, ALU.subtract)
                    link(ve.scalar_tensor_tensor(S2[:, q], S2[:, a], cos, T2[:, a], ALU.mult, ALU.add))

            def lr(n):
                if n >= 2:
                    ve.wait_ge(s_lrst[n % 2], 16 * B * (n // 2))
                ve.tensor_copy(LRO[:, n % 2, :], bank(n, "lr")[:, 0:LG]).then_inc(s_dev, 1)

            def lb(_):
                for u in range(2):
                    ve.wait_ge(s_lrst[u], 16 * B * NLCH // 2)
                ve.wait_ge(s_lbin, 32)
                for b in range(B):
                    ve.tensor_tensor(LA[:, b], LA[:, b], LAB[:, :, :, :], ALU.add)
                    i = ve.tensor_tensor(LB[:, b], LB[:, b], LBB, ALU.add)
                i.then_inc(s_lowrank, 1)

            def bu(b):
                if b == 0:
                    ve.wait_ge(s_bin, 32)
                    for a in range(B):
                        for s in range(2):
                            ve.scalar_tensor_tensor(CG[:, a, s, :], CT[:, s, :], SG[:, s:s + 1], GB[:, a, GA, :],
                                                    ALU.mult, ALU.mult)
                        for k in range(KB):
                            ve.scalar_tensor_tensor(DG[:, a, k, :], ident[:, :], VEC[:, VC["D"] + k:VC["D"] + k + 1],
                                                    GB[:, a, GA, k * P:(k + 1) * P], ALU.mult, ALU.mult)
                        i = ve.tensor_tensor(BG[:, a, :], BC[:, B20, :], GB[:, a, GF, :], ALU.mult)
                    i.then_inc(s_par, 1)
                Z, ZC = ZB[b][0], ZB[b][1]
                for c in range(NC):
                    q = slice(c * HALF, (c + 1) * HALF)
                    ve.tensor_tensor(T1, bank(b, "bu", c, 0), C2[:, q], ALU.mult).then_inc(s_dev, 1)
                    ve.tensor_tensor(T2, bank(b, "bu", c, 1), S2[:, q], ALU.mult).then_inc(s_dev, 1)
                    ve.wait_ge(s_dev, sd[0])
                    link(ve.tensor_tensor(T1, T1, T2, ALU.add))
                    ve.tensor_tensor_scan(Z[:, q], RVEC[:, 0:1].to_broadcast([P, HALF]), T1,
                                          0.0 if c == 0 else Z[:, c * HALF - 1:c * HALF], ALU.mult, ALU.add).then_inc(s_z, 1)
                    ve.wait_ge(s_z, b * NC + c + 1)
                    ve.tensor_tensor(ZC[:, q], Z[:, q], C2[:, q], ALU.mult).then_inc(s_zc, 1)

            def y0(b):
                add_out(b, "y0")
                stats(b, after(b, "y0"))
                normalise("y0", b, True)

            def d0(part):
                b, j = divmod(part, TWO)
                ve.wait_ge(s_pre, PRE[("y0", b)] * NC + j // 2 + 1)
                ve.tensor_tensor(pair(TG[:, :]), pair(bank(b, "w20", j)), row2(GB[:, b, GF, :]), ALU.mult).then_inc(s_dev, 1)
                ve.wait_ge(s_dev, sd[0])
                x = X[:, b, two(j), :]
                link(ve.tensor_tensor(x, x, pair(TG[:, :]), ALU.add))
                if j % 2:
                    stats(b, lambda h: None, [j // 2])

            def d1(part):
                b, j = divmod(part, TWO)
                add_bank(b, "w21", j, ("pr", b))

            def h0(b):
                normalise("h0", b, False)

            def qkv(b):
                for j in range(TWO):
                    ve.tensor_tensor(V[:, two(j), :], pair(bank(b, "v1", j)), row2(BC[:, BV, :]), ALU.add).then_inc(s_dev, 1)

            def att(b):
                for t in range(NT):
                    ve.wait_ge(s_sfull, b * NT + t + 1)
                    ve.tensor_reduce(NM[:, t:t + 1], PDF[:, t % 2, :], axis=AX_X, op=ALU.max, negate=True).then_inc(s_max1, 1)
                    ve.wait_ge(s_max1, b * NT + t + 1)
                    ve.tensor_scalar(NMS[:, b, t:t + 1], NM[:, t:t + 1], float(D) ** -0.5, None, ALU.mult).then_inc(s_nmax, 1)

            def pr(b):
                ve.wait_ge(s_exp1, (b + 1) * NT)
                link(ve.reciprocal(RSM[:, b, :], SM[:, b, :]))
                for j in range(TWO):
                    ve.wait_ge(s_pre, PRE[("h0", b)] * NC + j // 2 + 1)
                    o = bank(b, "pr", j)
                    for u in range(2):
                        t = 2 * j + u
                        x = X[:, b, t, :]
                        i = ve.scalar_tensor_tensor(x, o[:, u * D:(u + 1) * D], RSM[:, b, t:t + 1], x, ALU.mult, ALU.add)
                    i.then_inc(s_dev, 1)
                stats(b, after(b, "pr"))
                normalise("pr", b, False)

            def rank_rows(tag, s):
                def f(b):
                    for c in range(NC):
                        ve.tensor_copy(Y8[:, b, s, c * HALF:(c + 1) * HALF], bank(b, tag, c, rows_=RANK)).then_inc(s_dev, 1)
                return f

            def f2(b):
                add_out(b, "f2")
                stats(b, after(b, "f2"))
                normalise("f2", b, True)

            def qk3(b):
                def mid(j):
                    ve.wait_ge(s_rest, j + 1)
                    ve.tensor_copy(PARTS[:, j % 2, 1, :], RP).then_inc(s_mid, 1)

                for j, (name, c, k) in enumerate(QK3_JOBS if b == 0 else []):
                    ve.wait_ge(s_aev, AJ[(b, name, c, k)] + 1)
                    if j >= 2:
                        parts_stored(ve, j)
                    ve.tensor_copy(PARTS[:, j % 2, 0, :], QF[b][j]).then_inc(s_hi, 1)
                    mid(j)
                ve.wait_ge(s_vp, 2 * b + 1)
                for j in range(TWO):
                    o = bank(b, "v3", j)
                    for u in range(2):
                        i = ve.tensor_tensor(VP[b][:, 2 * j + u, :, 0:HD],
                                             o[:, u * D:(u + 1) * D].rearrange("p (h d) -> p h d", h=HEADS),
                                             BC[:, BV3, :].rearrange("p (h d) -> p h d", h=HEADS), ALU.add)
                    i.then_inc(s_dev, 1)

            def reduce_max(n):
                ve.wait_ge(s_mfull, n + 1)
                m, r = divmod(n, UNIT)
                ve.tensor_reduce(NMX[:, m % 2, r:r + 1], PDF[:, n % 2, :], axis=AX_X, op=ALU.max,
                                 negate=True).then_inc(s_mred, 1)
                if r == UNIT - 1:
                    split_max(m)

            def split_max(m):
                ve.wait_ge(s_mred, (m + 1) * UNIT)
                if m >= 1:
                    ve.wait_ge(s_nmtf, m)
                f = NMX[:, m % 2, :]
                link(ve.tensor_copy(NMP[:, 0, :], f))
                link(ve.tensor_tensor(NMR[:, :], f, NMP[:, 0, :], ALU.subtract))
                link(ve.tensor_copy(NMP[:, 1, :], NMR[:, :]))
                ve.tensor_tensor(NMP[:, 2, :], NMR[:, :], NMP[:, 1, :], ALU.subtract).then_inc(s_nmp, 1)

            def norm_heads_out(m):
                gg, c = divmod(m, NC)
                b, g = divmod(gg, NG)
                if m == 0 or m == NUNIT // B:
                    ve.wait_ge(s_parts, (b + 1) * 2 * KB * NC)
                ve.wait_ge(s_ut, m + 1)
                o = PA[:, 3, :].rearrange("p (n c) -> p n c", c=32)
                link(ve.reciprocal(RC[:, :], o[:, :, HD]))
                ve.tensor_tensor(
                    O[b][:, c * TPC:(c + 1) * TPC, g * GH * HD:(g + 1) * GH * HD].rearrange("p t (h d) -> p t h d", h=GH),
                    PA[:, 3, :].rearrange("p (t h c) -> p t h c", t=TPC, h=GH)[:, :, :, 0:HD],
                    RC[:, :].rearrange("p (t h) -> p t h", t=TPC).unsqueeze(3).to_broadcast([P, TPC, GH, HD]),
                    ALU.mult).then_inc(s_on, 1)

            def lead(part):
                per = LEAD // NLEAD
                for n in range(part * per, (part + 1) * per):
                    reduce_max(n)

            def step(n):
                m, kt = divmod(n, NT)
                s = LEAD + 2 * n
                if s < NMAX:
                    reduce_max(s)
                    reduce_max(s + 1)
                if kt == 1 and m >= 1:
                    norm_heads_out(m - 1)
                if n == NSTEP - 1:
                    norm_heads_out(NUNIT - 1)

            def turned_first(h):
                for k in range(KB):
                    ve.tensor_copy(XT[:, 0, k, h * HALF:(h + 1) * HALF], bank(0, "ot", h, k)).then_inc(s_dev, 1)

            def p3(part):
                b, j = divmod(part, TWO)
                add_bank(b, "p3", j, ("f2", b))
                if j % 2:
                    ve.wait_ge(s_dev, sd[0])
                    stats(b, lambda h: None, [j // 2])

            def end(b):
                normalise("end", b, True, s_scaled)
                for h in range(NC):
                    y = XN[:, b, h * TPC:(h + 1) * TPC, :]
                    ve.wait_ge(s_scaled, b * NC + h + 1)
                    link(ve.tensor_tensor(y, y, GB[:, b, S3, :].unsqueeze(1).to_broadcast([P, TPC, D]), ALU.mult))
                    ve.wait_ge(s_pre, PRE[("end", b)] * NC + h + 1)
                    ve.tensor_tensor(y, y, X[:, b, h * TPC:(h + 1) * TPC, :], ALU.add).then_inc(s_fin, 1)

            run({"n0": n0, "tab": table, "lr": lr, "bu": bu, "y0": y0, "d0": d0, "h0": h0, "lb": lb, "qkv": qkv, "att": att, "pr": pr, "d1": d1,
                 "a1": rank_rows("a1", 0), "a2": rank_rows("a2", 1), "f2": f2, "qk3": qk3, "lead": lead, "step": step,
                 "oa": turned_first, "p3": p3, "end": end})
            assert sd[0] == len(DJ)


def kernel(**inputs):
    import concourse.bacc as _bacc
    from concourse.bass_utils import run_bass_kernel_spmd as _run

    g = {k: np.asarray(v) for k, v in inputs.items()}

    def blocks(a):
        return a.reshape(-1, P).T

    def twice(a, b):
        return np.concatenate([a, b], axis=0)

    def kpn(w):
        return w.reshape(KB, P, -1).transpose(1, 0, 2)

    t = g["cond_1024"]
    wq3 = g["L3_cond_Wqkv"].reshape(D, 3, D)
    bq3 = g["L3_cond_bqkv"].reshape(D, 3)
    w2 = g["L2_cond_W2"].reshape(D, 4, D, RANK)
    b2 = g["L2_cond_b2"].reshape(4, D, RANK)
    l2_w2 = np.concatenate([w2[:, 0].reshape(D, -1), w2[:, 2].reshape(D, -1),
                            w2[:, 1].transpose(0, 2, 1).reshape(D, -1), w2[:, 3].transpose(0, 2, 1).reshape(D, -1)], axis=1)
    l2_b2 = np.concatenate([b2[0].reshape(-1), b2[2].reshape(-1), b2[1].T.reshape(-1), b2[3].T.reshape(-1)])
    col = lambda n: np.concatenate([g[n], g[n]])[:, None]
    arrays = {
        "x": g["x"], "t": t, "tT": t.T.reshape(KB, P, B).transpose(1, 0, 2),
        "lnrow": np.stack([g["L2_cond_ln_g"], g["L2_cond_ln_b"], g["L2_cond_b1"], g["L3_cond_ln_g"], g["L3_cond_ln_b"]]),
        "vec": np.concatenate(
            [blocks(g[n]) for n in ("L1_cond_norm1_w", "L1_cond_norm2_w", "L3_cond_ln_g", "L3_cond_ln_b", "L1_cond_q_b",
                                    "L1_cond_k_b")] + [blocks(bq3[:, 0]), blocks(bq3[:, 1])]
            + [blocks(g[n]) for n in ("L0_cond_D_diag", "L0_cond_b1", "L1_cond_mlp_b1")]
            + [col(n) for n in ("L0_cond_Lam_re", "L0_cond_Lam_im", "L0_cond_log_step")], axis=1),
        "wcond": np.concatenate([g["L0_cond_Wm"], g["L0_cond_Wc"], g["L1_cond_film1_w"], g["L1_cond_film2_w"],
                                 g["L3_cond_Wg"].T, g["L3_cond_Wb"].T], axis=1),
        "bcond": np.concatenate([g["L0_cond_bm"], g["L0_cond_bc"], g["L1_cond_film1_b"], g["L1_cond_film2_b"],
                                 g["L3_cond_bg"], g["L3_cond_bb"]]),
        "l2_w1": g["L2_cond_W1"], "l2_w2": l2_w2, "l2_b2": l2_b2,
        "b2x": np.stack([twice(g["L0_cond_B_re"], g["L0_cond_B_re"]), twice(g["L0_cond_B_im"], g["L0_cond_B_im"])], axis=1),
        "ct": np.stack([twice(g["L0_cond_C_re"].T, g["L0_cond_C_im"].T), twice(g["L0_cond_C_im"].T, g["L0_cond_C_re"].T)],
                       axis=1),
        "bc": np.stack([g["L1_cond_v_b"], g["L1_cond_proj_b"], g["L1_cond_mlp_b2"], bq3[:, 2], g["L3_cond_bp"],
                        g["L0_cond_b2"]]),
        "wa": np.stack([kpn(g[f"L1_cond_{n}_w"]) for n in ("q", "k", "v", "proj")], axis=1),
        "wqkv3": np.stack([kpn(wq3[:, j].T) for j in range(3)], axis=1),
        "wp3": g["L3_cond_Wp"].T,
        "w1_0": g["L0_cond_W1"], "w2_0": g["L0_cond_W2"], "w1_1": g["L1_cond_mlp_w1"], "w2_1": g["L1_cond_mlp_w2"],
    }
    arrays = {k: np.ascontiguousarray(v) for k, v in arrays.items()}
    nc = _bacc.Bacc("TRN2", target_bir_lowering=False, num_devices=1)
    ins = {k: nc.dram_tensor(f"in_{k}", v.shape, mybir.dt.from_np(v.dtype), kind="ExternalInput").ap()
           for k, v in arrays.items()}
    out = nc.dram_tensor("out_0", (B, T, D), F32, kind="ExternalOutput").ap()
    build(nc, ins, out)
    r = _run(nc, [{f"in_{k}": v for k, v in arrays.items()}], core_ids=[0])
    return r.results[0]["out_0"]
```

```python
from contextlib import ExitStack

import numpy as np
import concourse.bass as bass
from concourse import mybir

F32 = mybir.dt.float32
BF16 = mybir.dt.bfloat16
F32R = mybir.dt.float32r
I32 = mybir.dt.int32
ALU = mybir.AluOpType
ACT = mybir.ActivationFunctionType
AX_X = mybir.AxisListType.X

P = 128
B, T, D = 2, 1024, 256
KB = D // P
NT = T // P
HALF = 512
NC = T // HALF
TPC = HALF // P
TWO = NT // 2
FF = 4 * D
NF = FF // P
S5 = 64
HEADS, HD = 16, 16
GH = 4
NG = HEADS // GH
RANK = 8
LR = 4 * RANK * D
LCH = 1024
NLCH = LR // LCH
GCOL = 32
LG = LCH // (P // GCOL)
PAIRS = [(0, 0), (0, 1), (1, 0), (1, 1), (0, 2), (2, 0)]
NPAIR = len(PAIRS)
KSTK = NPAIR * HD
NPART = 3
KFULL = KSTK + NPART
UNIT = GH * TPC
NUNIT = B * NG * NC
NMAX = NUNIT * UNIT
NSTEP = NUNIT * NT
LEAD = UNIT + 14
TERMS = [(0, 0), (0, 1), (1, 0)]
NRING = 3
SOLO = (NMAX - LEAD) // 2
NSLOT = 3

CW = dict(shift_a=0, scale_a=2, gate_a=4, shift_ff=6, scale_ff=8, gate_ff=10, scale_c=12, shift_c=14,
          f1_scale=16, f1_shift=18, f2_scale=20, f2_shift=22, gamma=24, beta=26)
NCB = 28
NCOND = NCB * P
LEVELS = T.bit_length() - 1
LATE = 4
NROWJ = NCOND // HALF
PU, PM, P1, P2, P3 = range(0, 10, 2)
NPAR = 10
VC = dict(norm1=0, norm2=2, ln3_g=4, ln3_b=6, q_b=8, k_b=10, q3_b=12, k3_b=14, D=16, b1=18, mb1=26,
          lam_re=34, lam_im=35, log_step=36)
NVC = 37
BV, BP, MB2, BV3, BP3, B20 = range(6)
GA, GF, S3, B3 = range(4)

NTILE = NC * NF
LAG = 4
NLEAD = 5


def mlps(layer, turn, between, after):
    order, ups = [(turn, 0)], 0
    for d in range(B * NTILE):
        more = list(between.get(d, []))
        while ups < min(B * NTILE, d + 1 + LAG + max(0, 2 - d % NF if d else 0)):
            order += more[:1] + [(f"u{layer}", ups)]
            more = more[1:]
            if ups == NTILE - 1:
                order.append((turn, 1))
            ups += 1
        order += more + [(f"d{layer}", d)] + after.get(d, [])
    return order


def weave(*lists):
    return [x for n in range(max(map(len, lists))) for one in lists for x in one[n:n + 1]]


SCHED = [("n0", 0), ("n0", 1), ("tab", 0), ("lr", 0), ("lr", 1), ("bu", 0), ("lr", 2), ("bu", 1), ("lr", 3),
         ("y0", 0), ("yn", 0), ("ws", 0), ("lr", 4), ("lr", 5), ("y0", 1), ("lr", 6), ("lr", 7)]
assert NLCH == 8
SCHED += mlps(0, "m", {0: [None, ("ws", 1), ("yn", 1)]}, {NTILE - 1: [("h0", 0)]}) + [("h0", 1), ("lb", 0)]
SCHED += [("n1", 0), ("qkv", 0), ("att", 0), ("n1", 1), ("qkv", 1), ("pr", 0), ("pn", 0), ("att", 1), ("ws", 2)]
SCHED += mlps(1, "n2", {0: [None, ("pr", 1), ("ws", 3), ("pn", 1)], NTILE: [("x2", 0), ("a1", 0)], NTILE + NF: [("a2", 0), ("f2", 0)]},
              {NTILE + 2: [("g", 0)], NTILE + NF + 4: [("n3", 0)]})
SCHED += [("qk3", 0)]
SCHED = [x for x in SCHED if x]
SCHED += [("x2", 1), ("a1", 1), ("g", 1), ("a2", 1), ("f2", 1), ("lead", 0), ("n3", 1), ("lead", 1), ("qk3", 1)]
SCHED += [("lead", n) for n in range(2, NLEAD)] + [("step", n) for n in range(SOLO)]
SCHED += weave([("step", n) for n in range(SOLO, NSTEP)],
               [("oa", 0), ("oa", 1)] + [("p3", j) for j in range(TWO)] + [("end", 0)])
SCHED += [("ot", 1)] + [("p3", TWO + j) for j in range(TWO)] + [("end", 1)]


def turned(b, stage):
    return [(b, stage, h, k) for h in range(NC) for k in range(KB)]


def act_jobs(stage, b):
    if stage in ("n0", "m", "n1", "n2", "x2", "n3", "ot"):
        return turned(b, stage)
    if stage in ("u0", "u1"):
        b, i = divmod(b, NTILE)
        return [(b, "h" + stage[1], i // NF, i % NF)]
    if stage == "qkv":
        return [(b, w, c, k) for w in "qk" for c in range(NC) for k in range(KB)]
    if stage == "att":
        jobs = []
        for c in range(NC):
            jobs += [(b, "p", c * TPC + t, s) for t in range(TPC) for s in range(2)] + [(b, "o", c, k) for k in range(KB)]
        return jobs
    if stage == "g":
        return [(b, "g", c, k) for c in range(NC) for k in range(KB)]
    if stage == "qk3":
        return [(b, w, c, k) for k in range(KB) for w in ("q3", "k3") for c in range(NC)]
    return []


def split_jobs(stage, b):
    return act_jobs(stage, b) if stage in ("m", "n2", "u0", "u1") else []


def dve_jobs(stage, b):
    if stage == "lr":
        return [(b, "lr")]
    if stage == "bu":
        return [(b, "bu", c, s) for c in range(NC) for s in range(2)]
    if stage in ("a1", "a2"):
        return [(b, stage, c) for c in range(NC)]
    if stage == "p3":
        return [(b // TWO, "p3", b % TWO)]
    if stage in ("d0", "d1"):
        b, i = divmod(b, NTILE)
        c, f = divmod(i, NF)
        return [(b, "w2" + stage[1], t) for t in range(c * TPC, (c + 1) * TPC)] if f == NF - 1 else []
    if stage == "oa":
        return [(0, "ot", b, k) for k in range(KB)]
    out = {"y0": "y0", "qkv": "v1", "pr": "pr", "f2": "f2", "qk3": "v3"}.get(stage)
    return [(b, out, j) for j in range(TWO)] if out else []


def number(jobs_of):
    jobs = [j for stage, b in SCHED for j in jobs_of(stage, b)]
    return {j: n for n, j in enumerate(jobs)}


def order(*stages):
    return {x: n for n, x in enumerate(x for x in SCHED if x[0] in stages)}


def build(nc, I, out):
    AJ, DJ, SJ = number(act_jobs), number(dve_jobs), number(split_jobs)
    NORM = order("n0", "y0", "h0", "pr", "f2", "end")
    PRE = order("y0", "h0", "pr", "f2", "end")
    ctx = ExitStack()
    with ctx:
        def sb(name, shape, dt=F32):
            return ctx.enter_context(nc.sbuf_tensor(name, shape, dt))

        def sem(name):
            return ctx.enter_context(nc.semaphore(name))

        with ExitStack() as halves:
            def half(name, n):
                return halves.enter_context(nc.sbuf_tensor(name, [P, n], F32R))

            XSR = half("XSR", B * KB * T)
            WLR = half("WLR", 2 * KB * FF)
            HSR = half("HSR", 2 * NF * HALF)
            WHR0 = half("WHR0", 2 * KB * FF)
            half("GAP", 16384 - 8192 - 2 * KB * FF)
            WHR1 = half("WHR1", 2 * KB * FF)
        XT = sb("XT", [P, B, KB, T])
        W12 = sb("W12", [P, 2, KB * FF])
        R = sb("R", [P, 20736])
        X = sb("X", [P, B, NT, D])
        XN = sb("XN", [P, B, NT, D])
        WA = sb("WA", [P, 4, KB, D])
        WQ3 = sb("WQ3", [P, 3, KB, D])
        WP3 = sb("WP3", [P, KB, D])
        C2 = sb("C2", [P, T])
        S2 = sb("S2", [P, T])
        BA = sb("BA", [P, 2, KB, P])
        CT = sb("CT", [P, 2, D])
        CG = sb("CG", [P, B, 2, D])
        DG = sb("DG", [P, B, KB, P])
        BC = sb("BC", [P, 6, D])
        GB = sb("GB", [P, B, 4, D])
        BG = sb("BG", [P, B, D])
        VEC = sb("VEC", [P, NVC])
        PAR = sb("PAR", [P, B, NPAR * KB])
        LA = sb("LA", [P, B, 2, KB, RANK])
        LB = sb("LB", [RANK, B, 2, D])
        ident = sb("ident", [P, P])
        identb = sb("identb", [P, P], BF16)
        SEL = sb("SEL", [B, B, P])
        ST = sb("ST", [P, B, NT, 6])
        MV = sb("MV", [P, B, NT, 2])
        VE = sb("VE", [P, B, NT])
        RST = sb("RST", [P, B, NT])
        MHALF = sb("MHALF", [P, NT])
        NM = sb("NM", [P, NT])
        NMS = sb("NMS", [P, B, NT])
        SM = sb("SM", [P, B, NT])
        RSM = sb("RSM", [P, B, NT])
        RVEC = sb("RVEC", [P, 1])
        SG = sb("SG", [P, 2])
        TM = sb("TM", [P, 28])
        TI = sb("TI", [P, 1], I32)
        CTX = sb("CTX", [P, 2, KB, B])
        HIDC = sb("HIDC", [P, KB, GCOL])
        LAB = sb("LAB", [P, 2, KB, RANK])
        COLR = sb("COLR", [P, NCB, B])
        NMX = sb("NMX", [P, 2, UNIT])
        NMR = sb("NMR", [P, UNIT])
        NMP = sb("NMP", [P, NPART, UNIT], BF16)
        NMT = sb("NMT", [NPART * UNIT, P], BF16)
        RC = sb("RC", [P, UNIT])
        UO = sb("UO", [P, HALF])
        TG = sb("TG", [P, HALF])

        def flat(a):
            return a.rearrange("p t d -> p (t d)")

        WAF = WA[:, :, :, :].rearrange("p a k d -> p (a k d)")
        WQF = WQ3[:, :, :, :].rearrange("p a k d -> p (a k d)")
        WH = [[a[:, w * KB * FF:(w + 1) * KB * FF] for w in range(2)] for a in (WHR0, WHR1)]
        WL = [WLR[:, w * KB * FF:(w + 1) * KB * FF] for w in range(2)]
        XS = XSR[:, :].rearrange("p (c s k q) -> p c s k q", c=NC, s=2, k=KB)
        HS = HSR[:, :].rearrange("p (s f q) -> p s f q", s=2, f=NF)
        FT = [[R[:, o + n * HALF:o + (n + 1) * HALF] for n in range(NRING)] for o in (14592, 10240)]
        FT[0][2] = R[:, 16128:16128 + HALF]
        WC = R[:, 0:KB * NCOND].rearrange("p (k n) -> p k n", k=KB)
        ROWS = R[0:B, 8192:8192 + NCOND]
        LNR = R[0:B, 11776:11776 + 5 * D].rearrange("p (s d) -> p s d", s=5)
        TR = R[0:B, 13056:13056 + 6 * D].rearrange("p (s d) -> p s d", s=6)
        BX = R[:, 14592:14592 + 4 * D].rearrange("p (s d) -> p s d", s=4)
        T1 = R[:, 15616:15616 + HALF]
        T2 = R[:, 16128:16128 + HALF]
        ANG = R[:, 7168:7168 + 4 * 2 * LEVELS].rearrange("p (a s n) -> p a s n", a=4, s=2)
        TURNS = ANG[:, 0, 0, :]
        ARG = ANG[:, 1]
        WRAP = ANG[:, 2, 0, :]
        TRIG = ANG[:, 3]
        ZB = [[R[:, 8192 + (3 * b + i) * T:8192 + (3 * b + i + 1) * T] for i in range(3)] for b in range(B)]
        W2L = R[:, 16640:16640 + 4096].rearrange("p (s k n) -> p s k n", s=2, k=KB)
        LRO = WQF[:, 512:512 + 2 * LG].rearrange("p (s n) -> p s n", s=2)
        LBB = T1[0:RANK].rearrange("p (s d) -> p s d", s=2)
        L2W1 = WQF[:, 0:512].rearrange("p (k n) -> p k n", k=KB)
        QT = R[:, 8192:10240].rearrange("p (k t) -> p k t", k=KB)
        KT = R[:, 10240:12288].rearrange("p (k t) -> p k t", k=KB)
        V = R[:, 12288:14336].rearrange("p (t d) -> p t d", t=NT)
        PT = R[:, 16384:20480].rearrange("p (k q) -> p k q", k=NT)
        OT = [flat(XN[:, b]).rearrange("p (k t) -> p k t", k=KB) for b in range(B)]
        X2T = [OT[1], XT[:, 1]]
        GT = R[:, 8192:12288].rearrange("p (b k t) -> p b k t", b=B, k=KB)
        Y8 = R[0:RANK, 12288:16384].rearrange("p (b s t) -> p b s t", b=B, s=2)
        STK = R[0:KFULL, 0:NSLOT * 4096].bitcast(BF16).rearrange("p (s w n) -> p s w n", s=NSLOT, w=2)
        QS = STK[:, :, 0, :].rearrange("p s (c h q) -> p s c h q", c=NC, h=GH)
        KS = STK[:, :, 1, :].rearrange("p s (h t) -> p s h t", h=GH)
        PB = R[:, 12288:16384].rearrange("p (s j q) -> p s j q", s=2, j=GH)
        VP = [a.rearrange("p (t h c) -> p t h c", t=NT, h=HEADS)
              for a in (R[:, 16384:20480], W12[:, :, :].rearrange("p w n -> p (w n)"))]
        O = [XN[:, b] for b in range(B)]
        QF = [[flat(XN[:, b])[:, n * HALF:(n + 1) * HALF] for n in range(4)] for b in range(B)]
        QF[0] += QF[0]
        QF[1] += [R[:, 8192 + n * HALF:8192 + (n + 1) * HALF] for n in range(4)]
        PARTS = WAF[:, 0:1536].bitcast(BF16).rearrange("p (s n q) -> p s n q", s=2, n=NPART)
        RP = WAF[:, 1536:2048]

        PA = ctx.enter_context(nc.psum_tensor("PA", [P, 4, HALF], F32))
        PD = ctx.enter_context(nc.psum_tensor("PD", [P, 4, HALF], F32))
        PDF = PD[:, :, :].rearrange("p s q -> p (s q)").rearrange("p (s q) -> p s q", s=2)
        PTB = PA[:, 3, 0:64].bitcast(BF16)
        DR = nc.dram_tensor("qk_parts", [B, 2, KB, NPART, P, T], BF16, kind="Internal").ap()

        s_vin = sem("vectors_in")
        s_rin = sem("rows_in")
        s_cin = sem("cond_weights_in")
        s_bin = sem("broadcast_rows_in")
        s_xin = [[sem(f"x_in{b}{c}") for c in range(NC)] for b in range(B)]
        s_w1in = [sem("w1_layer0_in"), sem("w1_layer1_in")]
        s_w2in = [sem("w2_layer0_in"), sem("w2_layer1_in")]
        s_wain = sem("attention_weights_in")
        s_w3in = sem("last_attention_weights_in")
        s_l2in = [sem("adapter_weights_in0"), sem("adapter_weights_in1")]
        s_const = sem("constants_ready")
        s_cfull = sem("cond_bank_full")
        s_cev = sem("cond_bank_evacuated")
        s_ada_st = sem("ada_stats")
        s_ada_rs = sem("ada_rstd")
        s_ada = sem("ada_rows_ready")
        s_small = sem("small_bank_full")
        s_ctx = sem("small_bank_copied")
        s_hid = sem("hidden_row_ready")
        s_gelu = sem("hidden_gelu_ready")
        s_ang = sem("angles_ready")
        s_trig = sem("trig_ready")
        s_tab = sem("phase_table_ready")
        s_sb = sem("film_rows_ready")
        s_bx = sem("state_maps_ready")
        s_par = sem("params_ready")
        s_hidz = sem("hidden_columns_zeroed")
        s_lbin = sem("adapter_bias_in")
        s_lowrank = sem("adapter_maps_ready")
        s_lrst = [sem("adapter_rows_spread0"), sem("adapter_rows_spread1")]
        s_vp = sem("v_padding_ready")
        s_afull = sem("act_bank_full")
        s_aev = sem("act_bank_evacuated")
        s_dfull = sem("dve_bank_full")
        s_dev = sem("dve_bank_evacuated")
        s_dstep = sem("dve_step")
        s_gstep = sem("pool_step")
        s_stats = sem("stats_ready")
        s_rstd = sem("rstd_ready")
        s_xn = sem("xn_ready")
        s_pre = sem("bias_added")
        s_split = sem("halves_ready")
        s_used = sem("hidden_block_used")
        s_whigh = sem("weight_high_halves_ready")
        s_wh = sem("weight_halves_ready")
        s_z = sem("states_ready")
        s_zc = sem("states_cos_ready")
        s_zs = sem("states_sin_ready")
        s_sfull = sem("scores_full")
        s_max1 = sem("scores_max")
        s_nmax = sem("negmax_ready")
        s_exp1 = sem("probs1_ready")
        s_hi = sem("qk_high_ready")
        s_rest = sem("qk_rest_ready")
        s_mid = sem("qk_mid_ready")
        s_parts = sem("qk_parts_ready")
        s_ones = sem("ones_rows_ready")
        s_spill = [[sem(f"parts{b}_stored{u}") for u in range(2)] for b in range(B)]
        s_stack = [sem(f"group_stack_in{g}") for g in range(B * NG)]
        s_mfull = sem("maxpass_full")
        s_mred = sem("maxpass_reduced")
        s_nmp = sem("negmax_parts")
        s_nmtf = sem("negmax_t_full")
        s_nmt = sem("negmax_t_ready")
        s_nmrow = [sem(f"negmax_rows{m % 4}") for m in range(4)]
        s_efull = sem("energy_full")
        s_exp3 = sem("probs3_ready")
        s_pv = sem("pv_done")
        s_uo = sem("heads_out_copied")
        s_ut = sem("heads_out_t_full")
        s_on = sem("heads_out_normed")
        s_scaled = sem("out_scaled")
        s_fin = sem("out_ready")
        s_out = sem("out_stored")

        STACKED = 16 * (NC + 1) * NPAIR

        def nmrow_in(e, m):
            e.wait_ge(s_nmrow[m % 4], 16 * NPART * (m // 4 + 1))

        def store_parts(e, j):
            b, r = divmod(j, 2 * KB * NC)
            k, r = divmod(r, 2 * NC)
            side, c = divmod(r, NC)
            e.dma_start(DR[b, side, k, :, :, c * HALF:(c + 1) * HALF].rearrange("s p q -> p s q"),
                        PARTS[:, j % 2]).then_inc(s_spill[b][j % 2], 16)

        def parts_stored(e, j):
            b, r = divmod(j - 2, 2 * KB * NC)
            e.wait_ge(s_spill[b][j % 2], 16 * (r // 2 + 1))

        def turn_step(m):
            return (UNIT * (m + 1) - LEAD) // 2 + 1

        def run(engine_stages):
            for stage, b in SCHED:
                if stage in engine_stages:
                    engine_stages[stage](b)

        QK3_JOBS = [(name, c, k) for k in range(KB) for name in ("q3", "k3") for c in range(NC)]

        block = ctx.enter_context(nc.Block())

        @block.sync
        def _(sp):
            def kp(a):
                return a.rearrange("(k p) n -> p k n", p=P)

            sp.dma_start(VEC[:, :], I["vec"]).then_inc(s_vin, 16)
            sp.dma_start(BX[:, 0:2, :], I["b2x"]).then_inc(s_vin, 16)
            sp.dma_start(TR[:, 0, :], I["t"]).then_inc(s_rin, 16)
            sp.dma_start(LNR[:, :, :], I["lnrow"].partition_broadcast(B)).then_inc(s_rin, 16)
            sp.dma_start(CTX[:, 0, :, :], I["tT"]).then_inc(s_rin, 16)
            sp.dma_start(ROWS, I["bcond"].partition_broadcast(B)).then_inc(s_rin, 16)
            sp.dma_start(WC, kp(I["wcond"])).then_inc(s_cin, 16)
            sp.dma_start(L2W1, kp(I["l2_w1"])).then_inc(s_cin, 16)
            for b in range(B):
                for c in range(NC):
                    sp.dma_start(X[:, b, c * TPC:(c + 1) * TPC, :],
                                 I["x"][b, c * HALF:(c + 1) * HALF, :].rearrange("(t p) d -> p t d", p=P)
                                 ).then_inc(s_xin[b][c], 16)
            sp.dma_start(CT[:, :, :], I["ct"]).then_inc(s_bin, 16)
            sp.dma_start(BC[:, :, :], I["bc"].partition_broadcast(P)).then_inc(s_bin, 16)
            for n in range(NLCH + 2):
                if n < NLCH:
                    if n >= 2:
                        sp.wait_ge(s_dfull, DJ[(n - 2, "lr")] + 1)
                    cols = slice(n * LCH, (n + 1) * LCH)
                    sp.dma_start(W2L[:, n % 2], kp(I["l2_w2"])[:, :, cols]).then_inc(s_l2in[n % 2], 16)
                if n == 1:
                    sp.dma_start(W12[:, 0].rearrange("p (k n) -> p k n", k=KB), kp(I["w1_0"])).then_inc(s_w1in[0], 16)
                    sp.dma_start(W12[:, 1].rearrange("p (f d) -> p f d", f=NF), kp(I["w2_0"])).then_inc(s_w2in[0], 16)
                if n >= 2:
                    i = n - 2
                    sp.wait_ge(s_dev, DJ[(i, "lr")] + 1)
                    which, part = divmod(i * LCH, RANK * D)
                    for b in range(B):
                        src = LRO[b:P:GCOL, i % 2, :]
                        if which < 2:
                            k, p0 = divmod(part // RANK, P)
                            dst = LA[p0:p0 + LCH // RANK, b, which, k, :]
                            src = src.rearrange("a (p r) -> a p r", r=RANK)
                        else:
                            r0 = part // D
                            dst = LB[r0:r0 + LCH // D, b, which - 2, :]
                        sp.dma_start(dst, src).then_inc(s_lrst[i % 2], 16)
            sp.dma_start(LAB[:, :, :, :], I["l2_b2"][0:2 * RANK * D].rearrange("(s k p r) -> p s k r", s=2, k=KB, r=RANK)
                         ).then_inc(s_lbin, 16)
            sp.wait_ge(s_z, B * NC)
            sp.dma_start(LBB, I["l2_b2"][2 * RANK * D:].rearrange("(s r d) -> r s d", s=2, d=D)).then_inc(s_lbin, 16)
            for w in range(2):
                sp.dma_start(WA[:, 2 * w:2 * w + 2], I["wa"][:, 2 * w:2 * w + 2]).then_inc(s_wain, 16)
            for u in range(2):
                sp.wait_ge(s_lrst[u], 16 * B * NLCH // 2)
            sp.dma_start(WQ3[:, :, :, :], I["wqkv3"]).then_inc(s_w3in, 16)
            sp.dma_start(WP3[:, :, :], kp(I["wp3"])).then_inc(s_w3in, 16)
            sp.wait_ge(s_afull, AJ[(1, "h0", NC - 1, NF - 1)] + 1)
            sp.dma_start(W12[:, 0].rearrange("p (k n) -> p k n", k=KB), kp(I["w1_1"])).then_inc(s_w1in[1], 16)
            sp.wait_ge(s_dfull, DJ[(1, "w20", NT - 1)] + 1)
            sp.dma_start(W12[:, 1].rearrange("p (f d) -> p f d", f=NF), kp(I["w2_1"])).then_inc(s_w2in[1], 16)
            loaded = 0

            def stack(upto):
                nonlocal loaded
                while loaded < upto:
                    gg = loaded
                    b, g = divmod(gg, NG)
                    k, r = g // (NG // KB), (g * GH * HD) % P
                    if gg >= NSLOT:
                        sp.wait_ge(s_pv, (gg - NSLOT + 1) * NC * NT)
                    for u in range(2):
                        sp.wait_ge(s_spill[b][u], 16 * 2 * (k + 1))
                    heads = DR[b, :, k, :, r:r + GH * HD, :]
                    for n, pair in enumerate(PAIRS):
                        rows = slice(n * HD, (n + 1) * HD)
                        sp.dma_start(KS[rows, gg % NSLOT], heads[1, pair[1]].rearrange("(h d) t -> d h t", d=HD)
                                     ).then_inc(s_stack[gg], 16)
                        for c in range(NC):
                            sp.dma_start(QS[rows, gg % NSLOT, c],
                                         heads[0, pair[0], :, c * HALF:(c + 1) * HALF].rearrange("(h d) t -> d h t", d=HD)
                                         ).then_inc(s_stack[gg], 16)
                    loaded += 1

            for j in range(2 * KB * NC):
                sp.wait_ge(s_parts, j + 1)
                store_parts(sp, j)
            sp.wait_ge(s_dfull, DJ[(1, "w21", NT - 1)] + 1)
            stack(2)
            for m in range(NUNIT):
                gg, c = divmod(m, NC)
                sp.wait_ge(s_nmt, m + 1)
                for s in range(NPART):
                    sp.dma_start(QS[KSTK + s:KSTK + s + 1, gg % NSLOT, c],
                                 NMT[s * UNIT:(s + 1) * UNIT, :]).then_inc(s_nmrow[m % 4], 16)
                if m == 1:
                    sp.wait_ge(s_parts, B * 2 * KB * NC)
                    stack(NSLOT)
                if c == 0 and gg >= 1 and gg + 2 < B * NG:
                    stack(gg + 3)
            for b in range(B):
                for c in range(NC):
                    sp.wait_ge(s_fin, b * NC + c + 1)
                    sp.dma_start(out[b, c * HALF:(c + 1) * HALF, :].rearrange("(t p) d -> p t d", p=P),
                                 XN[:, b, c * TPC:(c + 1) * TPC, :]).then_inc(s_out, 16)
            sp.wait_ge(s_out, 16 * B * NC)

        @block.gpsimd
        def _(po):
            po.memset(ident[:, :], 0.0).then_inc(s_const, 1)
            po.memset(SEL[:, :, :], 0.0).then_inc(s_const, 1)
            po.memset(MHALF[:, :], -0.5).then_inc(s_const, 1)
            po.memset(HIDC[:, :, :], 0.0).then_inc(s_hidz, 1)
            po.wait_ge(s_const, 3)
            po.affine_select(out=ident[:, :], in_=ident[:, :], compare_op=ALU.not_equal, fill=1.0, base=0,
                             pattern=[[-1, P]], channel_multiplier=1).then_inc(s_const, 1)
            po.affine_select(out=SEL[:, :, :], in_=SEL[:, :, :], compare_op=ALU.not_equal, fill=1.0, base=0,
                             pattern=[[-1, B], [0, P]], channel_multiplier=1).then_inc(s_const, 1)
            po.wait_ge(s_const, 5)
            po.tensor_copy(identb[:, :], ident[:, :]).then_inc(s_const, 1)
            po.wait_ge(s_ada_st, 1)
            po.tensor_scalar(VE[0:B, 0, 0:1], MV[0:B, 0, 0, 1:2], 1e-5, None, ALU.add).then_inc(s_ada_rs, 1)
            po.wait_ge(s_ada_rs, 1)
            po.tensor_tensor(RST[0:B, 0, 0:1], VE[0:B, 0, 0:1], MHALF[0:B, 0:1], ALU.pow).then_inc(s_ada_rs, 1)
            cnt = [0]

            def link(i):
                cnt[0] += 1
                i.then_inc(s_gstep, 1)
                po.wait_ge(s_gstep, cnt[0])

            def rstd(stage, b, eps, rms=False):
                for h in range(NC):
                    po.wait_ge(s_stats, NORM[(stage, b)] * NC + h + 1)
                    t = slice(h * TPC, (h + 1) * TPC)
                    ve_ = VE[:, b, t]
                    if rms:
                        link(po.tensor_tensor(ve_, MV[:, b, t, 0], MV[:, b, t, 0], ALU.mult))
                        link(po.tensor_tensor(ve_, ve_, MV[:, b, t, 1], ALU.add))
                        link(po.tensor_scalar(ve_, ve_, eps, None, ALU.add))
                    else:
                        link(po.tensor_scalar(ve_, MV[:, b, t, 1], eps, None, ALU.add))
                    po.tensor_tensor(RST[:, b, t], ve_, MHALF[:, t], ALU.pow).then_inc(s_rstd, 1)

            def prebias(stage, b, row, sem_, n):
                for h in range(NC):
                    po.wait_ge(sem_, n * NC + h + 1)
                    x = X[:, b, h * TPC:(h + 1) * TPC, :]
                    po.tensor_tensor(x, x, row.unsqueeze(1).to_broadcast([P, TPC, D]), ALU.add).then_inc(s_pre, 1)

            po.wait_ge(s_trig, 1)
            po.memset(C2[:, 0:1], 1.0)
            link(po.memset(S2[:, 0:1], 0.0))
            def table(levels):
                for i in levels:
                    n = 1 << i
                    a, q = slice(0, n), slice(n, 2 * n)
                    cos, sin = TRIG[:, 0, i:i + 1], TRIG[:, 1, i:i + 1]
                    link(po.tensor_scalar(T1[:, a], S2[:, a], sin, None, ALU.mult))
                    link(po.tensor_scalar(T2[:, a], C2[:, a], sin, None, ALU.mult))
                    link(po.tensor_scalar(C2[:, q], C2[:, a], cos, None, ALU.mult))
                    link(po.tensor_scalar(S2[:, q], S2[:, a], cos, None, ALU.mult))
                    link(po.tensor_tensor(C2[:, q], C2[:, q], T1[:, a], ALU.subtract))
                    link(po.tensor_tensor(S2[:, q], S2[:, q], T2[:, a], ALU.add))
            table(range(LEVELS - LATE))

            def rest_of_table(_):
                table(range(LEVELS - LATE, LEVELS))
                po.sem_inc(s_tab, 1)

            def normed(stage, eps, row=None, rms=False):
                def f(b):
                    rstd(stage, b, eps, rms)
                    if row is not None:
                        prebias(stage, b, row(b), s_xn, NORM[(stage, b)])
                return f

            def bu(b):
                for c in range(NC):
                    po.wait_ge(s_z, b * NC + c + 1)
                    q = slice(c * HALF, (c + 1) * HALF)
                    po.tensor_tensor(ZB[b][2][:, q], ZB[b][0][:, q], S2[:, q], ALU.mult).then_inc(s_zs, 1)

            def x2(b):
                if b == 0:
                    return
                po.wait_ge(s_dfull, DJ[(1, "w21", NT - 1)] + 1)
                po.wait_ge(s_gstep, cnt[0])
                po.memset(KS[KSTK:KFULL, 0:2], 1.0).then_inc(s_ones, 1)
                po.wait_ge(s_ones, 1)
                for a in range(B):
                    po.memset(VP[a][:, :, :, HD:2 * HD], 0.0).then_inc(s_vp, 1)
                    po.wait_ge(s_vp, 2 * a + 1)
                    po.memset(VP[a][:, :, :, HD:HD + 1], float(D) ** 0.5).then_inc(s_vp, 1)

            def qk3(b):
                for n in range(2 * KB * NC):
                    j = b * 2 * KB * NC + n
                    src = QF[b][n]
                    hi, mid, low = (PARTS[:, j % 2, i, :] for i in range(NPART))
                    if b == 0:
                        po.wait_ge(s_hi, j + 1)
                    else:
                        po.wait_ge(s_aev, AJ[(b, *QK3_JOBS[n])] + 1)
                        parts_stored(po, j)
                        po.tensor_copy(hi, src).then_inc(s_hi, 1)
                        po.wait_ge(s_hi, j + 1)
                    po.tensor_tensor(RP, src, hi, ALU.subtract).then_inc(s_rest, 1)
                    if b == 1:
                        po.wait_ge(s_rest, j + 1)
                        po.tensor_copy(mid, RP).then_inc(s_mid, 1)
                    po.wait_ge(s_mid, j + 1)
                    po.tensor_tensor(low, RP, mid, ALU.subtract).then_inc(s_parts, 1)
                    po.wait_ge(s_parts, j + 1)
                    if b == 1:
                        store_parts(po, j)
                if b == 1:
                    po.memset(KS[KSTK:KFULL, 2:3], 1.0).then_inc(s_ones, 1)
                    for u in range(2):
                        po.wait_ge(s_spill[1][u], 16 * KB * NC)

            def end(b):
                rstd("end", b, 1e-5)
                prebias("end", b, GB[:, b, B3, :], s_scaled, b)

            run({"n0": normed("n0", 1e-5), "tab": rest_of_table, "bu": bu, "y0": normed("y0", 1e-5, lambda b: BG[:, b, :]),
                 "h0": normed("h0", 1e-6, lambda b: BC[:, BP, :], rms=True),
                 "pr": normed("pr", 1e-6, lambda b: BC[:, MB2, :], rms=True), "x2": x2,
                 "f2": normed("f2", 1e-5, lambda b: BC[:, BP3, :]), "qk3": qk3, "end": end})

        @block.scalar
        def _(act):
            act.wait_ge(s_ang, 1)
            act.activation(TRIG, ARG, ACT.Sin).then_inc(s_trig, 1)
            act.wait_ge(s_hid, 1)
            act.activation(TR[:, 3, :], TR[:, 2, :], ACT.Gelu).then_inc(s_gelu, 1)
            act.wait_ge(s_par, 1)
            seen = [0]

            def bank(*job):
                n = AJ[job]
                assert n == seen[0], (job, n, seen)
                seen[0] += 1
                act.wait_ge(s_afull, n + 1)
                return PA[:, n % 4, :]

            def vec(name, k=0):
                return VEC[:, VC[name] + k:VC[name] + k + 1]

            def tile_to_split(layer, job):
                n = SJ[job]
                if n >= NRING:
                    act.wait_ge(s_split, n - NRING + 1)
                return FT[layer][n % NRING]

            def high_weights(n):
                layer, w = divmod(n, 2)
                if layer == 0:
                    act.wait_ge(s_dfull, DJ[(w, "y0", TWO - 1)] + 1)
                else:
                    act.wait_ge(s_afull, AJ[(1, "o", NC - 1, KB - 1)] + 1)
                act.wait_ge((s_w1in, s_w2in)[w][layer], 16)
                act.activation(WH[layer][w], W12[:, w], ACT.Copy).then_inc(s_whigh, 1)

            def modulated_tile(stage, p, layer):
                def f(b):
                    for _, _, h, k in act_jobs(stage, b):
                        q = p * KB + k
                        dst = tile_to_split(layer, (b, stage, h, k))
                        act.activation(dst, bank(b, stage, h, k), ACT.Identity,
                                       bias=PAR[:, b, q + KB:q + KB + 1], scale=PAR[:, b, q:q + 1]).then_inc(s_aev, 1)
                return f

            def modulated(stage, p):
                def f(b):
                    for h in range(NC):
                        for k in range(KB):
                            q = p * KB + k
                            act.activation(XT[:, b, k, h * HALF:(h + 1) * HALF], bank(b, stage, h, k), ACT.Identity,
                                           bias=PAR[:, b, q + KB:q + KB + 1], scale=PAR[:, b, q:q + 1]).then_inc(s_aev, 1)
                return f

            def copied(stage, dst, func=ACT.Copy):
                def f(b):
                    for h in range(NC):
                        for k in range(KB):
                            act.activation(dst(b)[:, k, h * HALF:(h + 1) * HALF], bank(b, stage, h, k), func).then_inc(s_aev, 1)
                return f

            def hidden(stage, func, bias, layer):
                def f(part):
                    for b, tag, c, f_ in act_jobs(stage, part):
                        dst = tile_to_split(layer, (b, tag, c, f_))
                        act.activation(dst, bank(b, tag, c, f_), func, bias=vec(bias, f_)).then_inc(s_aev, 1)
                return f

            def qkv(b):
                for name, dst in (("q", QT), ("k", KT)):
                    for c in range(NC):
                        for k in range(KB):
                            act.activation(dst[:, k, c * HALF:(c + 1) * HALF], bank(b, name, c, k), ACT.Identity,
                                           bias=vec(name + "_b", k)).then_inc(s_aev, 1)

            def att(b):
                def probs_turn(t):
                    for s in range(2):
                        act.activation(PT[:, 4 * s:4 * s + 4, (t % TPC) * P:(t % TPC + 1) * P],
                                       bank(b, "p", t, s).rearrange("p (k q) -> p k q", k=4), ACT.Copy).then_inc(s_aev, 1)
                    if t % TPC == TPC - 1:
                        c = t // TPC
                        for k in range(KB):
                            act.activation(OT[b][:, k, c * HALF:(c + 1) * HALF], bank(b, "o", c, k),
                                           ACT.Copy).then_inc(s_aev, 1)

                for t in range(NT):
                    act.wait_ge(s_nmax, b * NT + t + 1)
                    act.activation(XT[:, b, t % 2, :], PDF[:, t % 2, :], ACT.Exp, bias=NMS[:, b, t:t + 1],
                                   scale=float(D) ** -0.5, accum_out=SM[:, b, t:t + 1]).then_inc(s_exp1, 1)
                    if t >= 1:
                        probs_turn(t - 1)
                probs_turn(NT - 1)

            def qk3(b):
                n = 0
                for k in range(KB):
                    for name in ("q3", "k3"):
                        for c in range(NC):
                            if b == 0 and n >= 4:
                                act.wait_ge(s_parts, n - 3)
                            act.activation(QF[b][n], bank(b, name, c, k), ACT.Identity,
                                           bias=vec(name + "_b", k)).then_inc(s_aev, 1)
                            n += 1

            def turn_max(m):
                act.wait_ge(s_nmtf, m + 1)
                if m >= 1:
                    nmrow_in(act, m - 1)
                act.activation(NMT[:, :], PTB[0:NPART * UNIT, :], ACT.Copy).then_inc(s_nmt, 1)

            def copy_heads_out(m):
                act.wait_ge(s_pv, (m + 1) * NT)
                if m >= 1:
                    act.wait_ge(s_ut, m)
                act.activation(UO[:, :], PA[:, 2, :], ACT.Copy).then_inc(s_uo, 1)

            def lead(part):
                if part == NLEAD - 1:
                    turn_max(0)

            def step(n):
                m, kt = divmod(n, NT)
                if n == 0:
                    act.wait_ge(s_dfull, DJ[(1, "f2", TWO - 1)] + 1)
                if n >= 2:
                    act.wait_ge(s_pv, n - 1)
                for j in range(GH):
                    if j == 2 and kt == 0 and m >= 1:
                        copy_heads_out(m - 1)
                    e = n * GH + j
                    act.wait_ge(s_efull, e + 1)
                    act.activation(PB[:, n % 2, j, :], PA[:, e % 2, :], ACT.Exp).then_inc(s_exp3, 1)
                for u in range(1, NUNIT):
                    if n == turn_step(u):
                        turn_max(u)
                if n == NSTEP - 1:
                    copy_heads_out(NUNIT - 1)

            run({"ws": high_weights, "n0": modulated("n0", PU), "m": modulated_tile("m", PM, 0), "n1": modulated("n1", P1),
                 "n2": modulated_tile("n2", P2, 1), "n3": modulated("n3", P3),
                 "u0": hidden("u0", ACT.Gelu_apprx_tanh, "b1", 0), "u1": hidden("u1", ACT.Gelu, "mb1", 1),
                 "qkv": qkv, "att": att, "x2": copied("x2", lambda b: X2T[b]),
                 "g": copied("g", lambda b: GT[:, b], ACT.Gelu), "qk3": qk3, "lead": lead, "step": step,
                 "ot": copied("ot", lambda b: XT[:, b])})
            assert seen[0] == len(AJ)

        @block.tensor
        def _(pe):
            def row_bank(o, lhs, w, c0, full):
                for k in range(KB):
                    m = pe.matmul(o, CTX[:, lhs, k, :], w[:, k, c0:c0 + HALF], start=(k == 0), stop=(k == KB - 1))
                m.then_inc(full, 1)

            def row_columns(bank, row):
                for k in range(KB):
                    m = pe.transpose(PA[:, bank, k * B:(k + 1) * B], row[:, k * P:(k + 1) * P], ident[0:B, 0:B])
                m.then_inc(s_small, 1)

            pe.wait_ge(s_const, 6)
            pe.wait_ge(s_rin, 16 * 4)
            pe.wait_ge(s_cin, 16 * 2)
            for n in range(NROWJ):
                if n == 4:
                    pe.wait_ge(s_bx, 1)
                    for s in range(2):
                        for k in range(KB):
                            m = pe.transpose(PA[:, 0, (2 * s + k) * P:(2 * s + k + 1) * P],
                                             BX[:, 2 + s, k * P:(k + 1) * P], ident[:, :])
                    m.then_inc(s_small, 1)
                if n >= 4:
                    pe.wait_ge(s_cev, n - 3)
                row_bank(PD[0:B, n % 4, :], 0, WC, n * HALF, s_cfull)
            pe.wait_ge(s_ada, 1)
            row_columns(1, TR[:, 1, :])
            pe.wait_ge(s_cev, NROWJ)
            for n in range(NCB):
                m = pe.transpose(PA[:, 3, n * B:(n + 1) * B], ROWS[:, n * P:(n + 1) * P], ident[0:B, 0:B])
            m.then_inc(s_small, 1)
            pe.wait_ge(s_ctx, 2)
            for k in range(KB):
                m = pe.matmul(PA[0:B, 2, 0:D], CTX[:, 1, k, :], L2W1[:, k, :], start=(k == 0), stop=(k == KB - 1))
            m.then_inc(s_small, 1)
            pe.wait_ge(s_sb, 1)
            for b in range(B):
                pe.wait_ge(s_ctx, 3 if b == 0 else 4)
                for s, row in enumerate((ROWS[:, CW["gate_a"] * P:CW["gate_a"] * P + D],
                                         ROWS[:, CW["gate_ff"] * P:CW["gate_ff"] * P + D], TR[:, 4, :], TR[:, 5, :])):
                    m = pe.matmul(PA[:, s // 2, (s % 2) * D:(s % 2 + 1) * D], SEL[:, b, :], row, start=True, stop=True)
                m.then_inc(s_small, 1)
            pe.wait_ge(s_gelu, 1)
            row_columns(3, TR[:, 3, :])

            sa, sd = [0], [0]
            hold = {"a": lambda: pe.wait_ge(s_ctx, 6), "d": None}

            def bank(kind, jobs, seen, ps, ev, job, rows_):
                n = jobs[job]
                assert n == seen[0], (job, n, seen)
                seen[0] += 1
                if hold[kind]:
                    hold[kind]()
                    hold[kind] = None
                if n >= 4:
                    pe.wait_ge(ev, n - 3)
                return ps[0:rows_, n % 4, :]

            def abank(*job):
                return bank("a", AJ, sa, PA, s_aev, job, P)

            def dbank(*job, rows_=P):
                return bank("d", DJ, sd, PD, s_dev, job, rows_)

            def turn(stage, src, norm=None):
                def f(b):
                    for h in range(NC):
                        if norm:
                            pe.wait_ge(s_xn, NORM[(norm, b)] * NC + h + 1)
                        elif stage == "x2":
                            pe.wait_ge(s_dev, DJ[(b, "w21", (h + 1) * TPC - 1)] + 1)
                        for k in range(KB):
                            o = abank(b, stage, h, k)
                            for t in range(TPC):
                                m = pe.transpose(o[:, t * P:(t + 1) * P], src(b)[:, h * TPC + t, k * P:(k + 1) * P],
                                                 ident[:, :])
                            m.then_inc(s_afull, 1)
                return f

            def project(o, w, col, b, h, full):
                for k in range(KB):
                    m = pe.matmul(o, w[:, k, col:col + P], XT[:, b, k, h * HALF:(h + 1) * HALF],
                                  start=(k == 0), stop=(k == KB - 1))
                m.then_inc(full, 1)

            def tokens_bank(b, tag, j, lhs, rhs, nk):
                o = dbank(b, tag, j)
                for u in range(2):
                    t = 2 * j + u
                    for k in range(nk):
                        m = pe.matmul(o[:, u * D:(u + 1) * D], lhs(k)[:, t * P:(t + 1) * P], rhs(k),
                                      start=(k == 0), stop=(k == nk - 1))
                m.then_inc(s_dfull, 1)

            def tokens_out(b, tag, lhs, rhs, nk, ready):
                for j in range(TWO):
                    if ready:
                        ready(j)
                    tokens_bank(b, tag, j, lhs, rhs, nk)

            def xt_ready(b, stage, h):
                pe.wait_ge(s_aev, AJ[(b, stage, h, KB - 1)] + 1)

            def lr(n):
                pe.wait_ge(s_ctx, 6)
                pe.wait_ge(s_l2in[n % 2], 16 * (n // 2 + 1))
                o = dbank(n, "lr")
                for k in range(KB):
                    for j in range(P // GCOL):
                        m = pe.matmul(o[GCOL * j:GCOL * (j + 1), 0:LG], HIDC[:, k, :],
                                      W2L[:, n % 2, k, j * LG:(j + 1) * LG], start=(k == 0), stop=(k == KB - 1))
                m.then_inc(s_dfull, 1)

            def bu(b):
                for c in range(NC):
                    xt_ready(b, "n0", c)
                    for s in range(2):
                        project(dbank(b, "bu", c, s), BA[:, s], 0, b, c, s_dfull)

            def y0(b):
                pe.wait_ge(s_par, 2)
                for j in range(TWO):
                    pe.wait_ge(s_zc, b * NC + j // 2 + 1)
                    pe.wait_ge(s_zs, b * NC + j // 2 + 1)
                    o = dbank(b, "y0", j)
                    for u in range(2):
                        tt = slice((2 * j + u) * P, (2 * j + u + 1) * P)
                        pe.matmul(o[:, u * D:(u + 1) * D], ZB[b][1][:, tt], CG[:, b, 0, :], start=True, stop=False)
                        for k in range(KB):
                            pe.matmul(o[:, u * D + k * P:u * D + (k + 1) * P], XT[:, b, k, tt], DG[:, b, k, :],
                                      start=False, stop=False)
                        m = pe.matmul(o[:, u * D:(u + 1) * D], ZB[b][2][:, tt], CG[:, b, 1, :], start=False, stop=True)
                    m.then_inc(s_dfull, 1)

            def up(stage, layer, src):
                parts = [a.rearrange("p (k n) -> p k n", k=KB) for a in (WH[layer][0], WL[0])]

                def f(part):
                    pe.wait_ge(s_wh, 2 * layer + 1)
                    for b, tag, c, f_ in act_jobs(stage, part):
                        pe.wait_ge(s_split, SJ[(b, src, c, KB - 1)] + 1)
                        o = abank(b, tag, c, f_)
                        terms = [(k, w, x) for k in range(KB) for w, x in TERMS]
                        for n, (k, w, x) in enumerate(terms):
                            m = pe.matmul(o, parts[w][:, k, f_ * P:(f_ + 1) * P], XS[:, c, x, k, :],
                                          start=(n == 0), stop=(n == len(terms) - 1))
                        m.then_inc(s_afull, 1)
                return f

            def mlp_down(tag, hidden, layer):
                parts = [a.rearrange("p (f d) -> p f d", f=NF) for a in (WH[layer][1], WL[1])]

                def f(part):
                    b, i = divmod(part, NTILE)
                    c, f_ = divmod(i, NF)
                    n = DJ[(b, tag, c * TPC)]
                    if f_ == 0:
                        pe.wait_ge(s_wh, 2 * layer + 2)
                        if hold["d"]:
                            hold["d"]()
                            hold["d"] = None
                        pe.wait_ge(s_dev, n)
                    pe.wait_ge(s_split, SJ[(b, hidden, c, f_)] + 1)
                    last = f_ == NF - 1
                    for t in range(TPC):
                        for w, x in TERMS:
                            m = pe.matmul(PD[:, (n + t) % 4, 0:D], HS[:, x, f_, t * P:(t + 1) * P], parts[w][:, f_, :],
                                          start=(f_ == 0 and (w, x) == TERMS[0]), stop=(last and (w, x) == TERMS[-1]))
                        if last:
                            m.then_inc(s_dfull, 1)
                    if last:
                        assert n == sd[0]
                        sd[0] += TPC
                    else:
                        m.then_inc(s_used, 1)
                return f

            def qkv(b):
                pe.wait_ge(s_wain, 32)
                for name, w in (("q", 0), ("k", 1)):
                    for c in range(NC):
                        xt_ready(b, "n1", c)
                        for k in range(KB):
                            project(abank(b, name, c, k), WA[:, w], k * P, b, c, s_afull)
                tokens_out(b, "v1", lambda k: XT[:, b, k, :], lambda k: WA[:, 2, k, :], KB, None)

            def att(b):
                def scores(t):
                    if t >= 2:
                        pe.wait_ge(s_exp1, b * NT + t - 1)
                    for c in range(NC):
                        for k in range(KB):
                            m = pe.matmul(PDF[:, t % 2, c * HALF:(c + 1) * HALF], QT[:, k, t * P:(t + 1) * P],
                                          KT[:, k, c * HALF:(c + 1) * HALF], start=(k == 0), stop=(k == KB - 1))
                    m.then_inc(s_sfull, 1)

                def probs_turn(t):
                    pe.wait_ge(s_exp1, b * NT + t + 1)
                    for s in range(2):
                        o = abank(b, "p", t, s)
                        for k in range(4):
                            m = pe.transpose(o[:, k * P:(k + 1) * P], XT[:, b, t % 2, (4 * s + k) * P:(4 * s + k + 1) * P],
                                             ident[:, :])
                        m.then_inc(s_afull, 1)

                pe.wait_ge(s_dev, sd[0])
                pe.wait_ge(s_aev, AJ[(b, "k", NC - 1, KB - 1)] + 1)
                scores(0)
                scores(1)
                for t in range(NT):
                    probs_turn(t)
                    if t + 2 < NT:
                        scores(t + 2)
                    if t % TPC == TPC - 1:
                        c = t // TPC
                        pe.wait_ge(s_aev, AJ[(b, "p", t, 1)] + 1)
                        for k in range(KB):
                            o = abank(b, "o", c, k)
                            for kt in range(NT):
                                m = pe.matmul(o, V[:, kt, k * P:(k + 1) * P], PT[:, kt, :], start=(kt == 0),
                                              stop=(kt == NT - 1))
                            m.then_inc(s_afull, 1)
                hold["d"] = lambda: pe.wait_ge(s_exp1, (b + 1) * NT)

            def pr(b):
                tokens_out(b, "pr", lambda k: OT[b][:, k, :], lambda k: WA[:, 3, k, :], KB,
                           lambda j: pe.wait_ge(s_aev, AJ[(b, "o", j // 2, KB - 1)] + 1))

            def down(tag, src_tag, src, s):
                def f(b):
                    pe.wait_ge(s_lowrank, 1)
                    for c in range(NC):
                        xt_ready(b, src_tag, c)
                        o = dbank(b, tag, c, rows_=RANK)
                        for k in range(KB):
                            m = pe.matmul(o, LA[:, b, s, k, :], src(b)[:, k, c * HALF:(c + 1) * HALF], start=(k == 0),
                                          stop=(k == KB - 1))
                        m.then_inc(s_dfull, 1)
                return f

            def g(b):
                for c in range(NC):
                    pe.wait_ge(s_dev, DJ[(b, "a1", c)] + 1)
                    for k in range(KB):
                        pe.matmul(abank(b, "g", c, k), LB[:, b, 0, k * P:(k + 1) * P], Y8[:, b, 0, c * HALF:(c + 1) * HALF],
                                  start=True, stop=True).then_inc(s_afull, 1)

            def f2(b):
                tokens_out(b, "f2", lambda k: Y8[:, b, 1, :], lambda k: LB[:, b, 1, :], 1,
                           lambda j: pe.wait_ge(s_dev, DJ[(b, "a2", j // 2)] + 1))

            def qk3(b):
                pe.wait_ge(s_w3in, 32)
                for k in range(KB):
                    for w, name in enumerate(("q3", "k3")):
                        for c in range(NC):
                            xt_ready(b, "n3", c)
                            project(abank(b, name, c, k), WQ3[:, w], k * P, b, c, s_afull)
                tokens_out(b, "v3", lambda k: XT[:, b, k, :], lambda k: WQ3[:, 2, k, :], KB, None)

            def maxpass(n):
                m, r = divmod(n, UNIT)
                gg, c = divmod(m, NC)
                j, t = divmod(r, TPC)
                if n >= 2:
                    pe.wait_ge(s_mred, n - 1)
                if n % (NC * UNIT) == 0:
                    pe.wait_ge(s_stack[gg], STACKED)
                for kc in range(NC):
                    i = pe.matmul(PDF[:, n % 2, kc * HALF:(kc + 1) * HALF],
                                  QS[0:KSTK, gg % NSLOT, c, j, t * P:(t + 1) * P],
                                  KS[0:KSTK, gg % NSLOT, j, kc * HALF:(kc + 1) * HALF], start=True, stop=True)
                i.then_inc(s_mfull, 1)

            def turn_max(m):
                pe.wait_ge(s_nmp, m + 1)
                if m >= 2:
                    pe.wait_ge(s_on, m - 1)
                if m >= 1:
                    pe.wait_ge(s_nmt, m)
                pe.transpose(PTB[0:NPART * UNIT, :], NMP[:, :, :].rearrange("p s n -> p (s n)"),
                             identb[:, :]).then_inc(s_nmtf, 1)

            def turn_heads_out(m):
                pe.wait_ge(s_uo, m + 1)
                if m >= 1:
                    pe.wait_ge(s_on, m)
                pe.wait_ge(s_nmt, min(m + 2, NUNIT))
                for t in range(TPC):
                    i = pe.transpose(PA[:, 3, t * P:(t + 1) * P], UO[:, t * P:(t + 1) * P], ident[:, :])
                i.then_inc(s_ut, 1)

            def energy(step, j):
                m, kt = divmod(step, NT)
                gg, c = divmod(m, NC)
                e = step * GH + j
                if e >= 2:
                    pe.wait_ge(s_exp3, e - 1)
                pe.matmul(PA[:, e % 2, :], KS[:, gg % NSLOT, j, kt * P:(kt + 1) * P], QS[:, gg % NSLOT, c, j, :],
                          start=True, stop=True).then_inc(s_efull, 1)

            def times_v(step):
                m, kt = divmod(step, NT)
                gg, c = divmod(m, NC)
                b, g_ = divmod(gg, NG)
                pe.wait_ge(s_exp3, (step + 1) * GH)
                if kt == 0 and m >= 1:
                    pe.wait_ge(s_uo, m)
                for j in range(GH):
                    i = pe.matmul(PA[32 * j:32 * j + 32, 2, :], VP[b][:, kt, g_ * GH + j, :], PB[:, step % 2, j, :],
                                  start=(kt == 0), stop=(kt == NT - 1))
                i.then_inc(s_pv, 1)

            def lead(part):
                pe.wait_ge(s_dev, sd[0])
                per = LEAD // NLEAD
                for n in range(part * per, (part + 1) * per):
                    maxpass(n)
                if part == NLEAD - 1:
                    pe.wait_ge(s_aev, sa[0])
                    turn_max(0)
                hold["d"] = lambda: pe.wait_ge(s_mred, (part + 1) * per)

            def step(n):
                m, kt = divmod(n, NT)
                s = LEAD + 2 * n
                if n == 0:
                    pe.wait_ge(s_ones, 1)
                    pe.wait_ge(s_vp, 2 * B)
                    pe.wait_ge(s_dev, sd[0])
                    nmrow_in(pe, 0)
                    energy(0, 0)
                    energy(0, 1)
                energy(n, 2)
                energy(n, 3)
                if n > SOLO:
                    times_v(n - 1)
                if s < NMAX:
                    maxpass(s)
                    maxpass(s + 1)
                for u in range(1, NUNIT):
                    if n == turn_step(u):
                        turn_max(u)
                if kt == 1 and m >= 1:
                    turn_heads_out(m - 1)
                if n + 1 < NSTEP:
                    if kt == NT - 1:
                        nmrow_in(pe, m + 1)
                        if (m + 1) // NC == 2:
                            pe.wait_ge(s_ones, 2)
                    energy(n + 1, 0)
                    energy(n + 1, 1)
                if n < SOLO or n == NSTEP - 1:
                    times_v(n)
                if n == SOLO - 1:
                    hold["d"] = lambda: pe.wait_ge(s_mred, NMAX)
                if n == NSTEP - 1:
                    turn_heads_out(NUNIT - 1)
                    pe.wait_ge(s_on, NUNIT)

            def turn_first(h):
                for k in range(KB):
                    o = dbank(0, "ot", h, k)
                    for t in range(TPC):
                        m = pe.transpose(o[:, t * P:(t + 1) * P], O[0][:, h * TPC + t, k * P:(k + 1) * P], ident[:, :])
                    m.then_inc(s_dfull, 1)

            def p3(part):
                b, j = divmod(part, TWO)
                if b:
                    xt_ready(b, "ot", j // 2)
                else:
                    pe.wait_ge(s_dev, DJ[(b, "ot", j // 2, KB - 1)] + 1)
                tokens_bank(b, "p3", j, lambda k: XT[:, b, k, :], lambda k: WP3[:, k, :], KB)

            run({"n0": turn("n0", lambda b: XN[:, b], "n0"), "lr": lr, "bu": bu, "y0": y0,
                 "m": turn("m", lambda b: XN[:, b], "y0"), "u0": up("u0", 0, "m"), "d0": mlp_down("w20", "h0", 0),
                 "n1": turn("n1", lambda b: XN[:, b], "h0"), "qkv": qkv, "att": att, "pr": pr,
                 "n2": turn("n2", lambda b: XN[:, b], "pr"), "u1": up("u1", 1, "n2"), "d1": mlp_down("w21", "h1", 1),
                 "x2": turn("x2", lambda b: X[:, b]), "a1": down("a1", "x2", lambda b: X2T[b], 0), "g": g,
                 "a2": down("a2", "g", lambda b: GT[:, b], 1), "f2": f2,
                 "n3": turn("n3", lambda b: XN[:, b], "f2"), "qk3": qk3, "lead": lead, "step": step,
                 "oa": turn_first, "ot": turn("ot", lambda b: O[b]), "p3": p3})
            assert sa[0] == len(AJ) and sd[0] == len(DJ)

        @block.vector
        def _(ve):
            cnt = [0]

            def link(i):
                cnt[0] += 1
                i.then_inc(s_dstep, 1)
                ve.wait_ge(s_dstep, cnt[0])

            l0 = link
            ve.wait_ge(s_vin, 32)
            def tm(n):
                return TM[:, n:n + 1]

            ROUND = 1.5 * 2.0 ** 23
            DT, LR_, TH, RR, A0, A1, A2 = 0, 1, 2, 3, 10, 11, 12

            def exp(o, x):
                l0(ve.tensor_scalar(tm(A0), tm(x), -87.0, 88.0, ALU.max, ALU.min))
                l0(ve.tensor_scalar(tm(A1), tm(A0), 1.4426950408889634, ROUND, ALU.mult, ALU.add))
                l0(ve.tensor_scalar(tm(A1), tm(A1), -ROUND, None, ALU.add))
                l0(ve.scalar_tensor_tensor(tm(A0), tm(A1), -0.693359375, tm(A0), ALU.mult, ALU.add))
                l0(ve.scalar_tensor_tensor(tm(A0), tm(A1), 2.12194440e-4, tm(A0), ALU.mult, ALU.add))
                coef = [1 / 5040, 1 / 720, 1 / 120, 1 / 24, 1 / 6, 0.5, 1.0]
                l0(ve.tensor_scalar(tm(A2), tm(A0), coef[0], coef[1], ALU.mult, ALU.add))
                for q in coef[2:] + [1.0]:
                    l0(ve.tensor_scalar(tm(A2), tm(A2), tm(A0), q, ALU.mult, ALU.add))
                l0(ve.tensor_scalar(tm(A1), tm(A1), 127.0, 2.0 ** 23, ALU.add, ALU.mult))
                l0(ve.tensor_copy(TI[:, :], tm(A1)))
                l0(ve.tensor_tensor(tm(o), tm(A2), TI[:, :].bitcast(F32), ALU.mult))

            lam_re, lam_im = (VEC[:, VC[n]:VC[n] + 1] for n in ("lam_re", "lam_im"))
            l0(ve.tensor_copy(tm(LR_), VEC[:, VC["log_step"]:VC["log_step"] + 1]))
            exp(DT, LR_)
            l0(ve.tensor_tensor(tm(LR_), lam_re, tm(DT), ALU.mult))
            l0(ve.tensor_tensor(tm(TH), lam_im, tm(DT), ALU.mult))
            exp(RR, LR_)
            PI1, PI2, PI3 = 6.28125, 1.93500518798828125e-3, 3.0199159819e-7
            angle = ARG[:, 1, :]
            l0(ve.tensor_copy(ARG[:, 1, 0:1], tm(TH)))
            n = 1
            while n < LEVELS:
                m = min(n, LEVELS - n)
                l0(ve.tensor_scalar(ARG[:, 1, n:n + m], ARG[:, 1, 0:m], 2.0 ** n, None, ALU.mult))
                n *= 2
            l0(ve.tensor_scalar(TURNS, angle, 1.0 / (2 * np.pi), ROUND, ALU.mult, ALU.add))
            l0(ve.tensor_scalar(TURNS, TURNS, -ROUND, None, ALU.add))
            for part in (PI1, PI2, PI3):
                l0(ve.scalar_tensor_tensor(angle, TURNS, -part, angle, ALU.mult, ALU.add))
            l0(ve.tensor_scalar(ARG[:, 0, :], angle, float(np.pi / 2), None, ALU.add))
            l0(ve.tensor_scalar(WRAP, ARG[:, 0, :], float(np.pi), float(-2 * np.pi), ALU.is_gt, ALU.mult))
            l0(ve.tensor_tensor(ARG[:, 0, :], ARG[:, 0, :], WRAP, ALU.add))
            ve.tensor_scalar(ARG, ARG, -3.1415925, 3.1415925, ALU.max, ALU.min).then_inc(s_ang, 1)
            ve.wait_ge(s_trig, 1)
            cos, sin = TRIG[:, 0, 0:1], TRIG[:, 1, 0:1]
            NR, NI, DEN, FR, FI, UU, WW = 14, 15, 16, 17, 18, 4, 5
            l0(ve.tensor_scalar(tm(NR), cos, tm(RR), -1.0, ALU.mult, ALU.add))
            l0(ve.tensor_tensor(tm(NI), sin, tm(RR), ALU.mult))
            l0(ve.tensor_tensor(tm(A0), lam_im, lam_im, ALU.mult))
            l0(ve.scalar_tensor_tensor(tm(DEN), lam_re, lam_re, tm(A0), ALU.mult, ALU.add))
            l0(ve.reciprocal(tm(DEN), tm(DEN)))
            l0(ve.tensor_tensor(tm(A0), tm(NI), lam_im, ALU.mult))
            l0(ve.scalar_tensor_tensor(tm(FR), tm(NR), lam_re, tm(A0), ALU.mult, ALU.add))
            l0(ve.tensor_tensor(tm(FR), tm(FR), tm(DEN), ALU.mult))
            l0(ve.tensor_tensor(tm(A0), tm(NR), lam_im, ALU.mult))
            l0(ve.scalar_tensor_tensor(tm(FI), tm(NI), lam_re, tm(A0), ALU.mult, ALU.subtract))
            l0(ve.tensor_tensor(tm(FI), tm(FI), tm(DEN), ALU.mult))
            lo, hi = slice(0, S5), slice(S5, 2 * S5)
            l0(ve.tensor_copy(TM[lo, UU:UU + 1], TM[lo, FR:FR + 1]))
            l0(ve.tensor_copy(TM[hi, UU:UU + 1], TM[hi, FI:FI + 1]))
            l0(ve.tensor_scalar(TM[lo, WW:WW + 1], TM[lo, FI:FI + 1], -1.0, None, ALU.mult))
            l0(ve.tensor_copy(TM[hi, WW:WW + 1], TM[hi, FR:FR + 1]))
            l0(ve.tensor_scalar(BX[:, 2, :], BX[:, 1, :], tm(WW), None, ALU.mult))
            l0(ve.scalar_tensor_tensor(BX[:, 2, :], BX[:, 0, :], tm(UU), BX[:, 2, :], ALU.mult, ALU.add))
            l0(ve.tensor_scalar(BX[:, 3, :], BX[:, 0, :], tm(WW), None, ALU.mult))
            ve.scalar_tensor_tensor(BX[:, 3, :], BX[:, 1, :], tm(UU), BX[:, 3, :], ALU.mult, ALU.subtract).then_inc(s_bx, 1)
            l0(ve.tensor_copy(RVEC[:, :], tm(RR)))
            l0(ve.memset(SG[lo, 0:1], 2.0))
            l0(ve.memset(SG[hi, 0:1], -2.0))
            l0(ve.memset(SG[:, 1:2], -2.0))
            ve.wait_ge(s_rin, 16 * 4)
            l0(ve.bn_stats(ST[0:B, 0, 0, :], TR[:, 0, :]))
            ve.bn_aggr(MV[0:B, 0, 0, :], ST[0:B, 0, 0, :]).then_inc(s_ada_st, 1)
            ve.wait_ge(s_ada_rs, 2)
            l0(ve.tensor_scalar(TR[:, 1, :], TR[:, 0, :], MV[0:B, 0, 0, 0:1], RST[0:B, 0, 0:1], ALU.subtract, ALU.mult))
            l0(ve.tensor_tensor(TR[:, 1, :], TR[:, 1, :], LNR[:, 0, :], ALU.mult))
            ve.tensor_tensor(TR[:, 1, :], TR[:, 1, :], LNR[:, 1, :], ALU.add).then_inc(s_ada, 1)

            def stats(b, ready, halves=range(NC)):
                for h in halves:
                    ready(h)
                    for t in range(h * TPC, (h + 1) * TPC):
                        i = ve.bn_stats(ST[:, b, t, :], X[:, b, t, :])
                    link(i)
                    for t in range(h * TPC, (h + 1) * TPC):
                        i = ve.bn_aggr(MV[:, b, t, :], ST[:, b, t, :])
                    i.then_inc(s_stats, 1)

            def normalise(stage, b, mean, sem_=s_xn):
                for h in range(NC):
                    ve.wait_ge(s_rstd, NORM[(stage, b)] * NC + h + 1)
                    for t in range(h * TPC, (h + 1) * TPC):
                        if mean:
                            i = ve.tensor_scalar(XN[:, b, t, :], X[:, b, t, :], MV[:, b, t, 0:1], RST[:, b, t:t + 1],
                                                 ALU.subtract, ALU.mult)
                        else:
                            i = ve.tensor_scalar(XN[:, b, t, :], X[:, b, t, :], RST[:, b, t:t + 1], None, ALU.mult)
                    i.then_inc(sem_, 1)

            for n in range(NROWJ):
                ve.wait_ge(s_cfull, n + 1)
                q = slice(n * HALF, (n + 1) * HALF)
                ve.tensor_tensor(ROWS[:, q], PD[0:B, n % 4, :], ROWS[:, q], ALU.add).then_inc(s_cev, 1)
                if n == 3:
                    ve.wait_ge(s_small, 1)
                    ve.tensor_copy(BA[:, :, :, :].rearrange("p s k n -> p (s k n)"), PA[:, 0, :]).then_inc(s_ctx, 1)
            ve.wait_ge(s_cev, NROWJ)
            gamma = ROWS[:, CW["gamma"] * P:CW["gamma"] * P + D]
            beta = ROWS[:, CW["beta"] * P:CW["beta"] * P + D]
            l0(ve.tensor_tensor(TR[:, 4, :], gamma, LNR[:, 3, :], ALU.mult))
            l0(ve.tensor_tensor(TR[:, 5, :], gamma, LNR[:, 4, :], ALU.mult))
            ve.tensor_tensor(TR[:, 5, :], TR[:, 5, :], beta, ALU.add).then_inc(s_sb, 1)
            ve.wait_ge(s_small, 2)
            ve.tensor_copy(CTX[:, 1, :, :].rearrange("p k b -> p (k b)"), PA[:, 1, 0:KB * B]).then_inc(s_ctx, 1)
            for b in range(B):
                stats(b, lambda h: ve.wait_ge(s_xin[b][h], 16))
            ve.wait_ge(s_small, 3)
            ve.tensor_copy(COLR[:, :, :].rearrange("p n b -> p (n b)"), PA[:, 3, 0:NCB * B]).then_inc(s_ctx, 1)
            ve.wait_ge(s_ctx, 3)

            def c(name):
                return COLR[:, CW[name]:CW[name] + KB, :]

            def v(name):
                return VEC[:, VC[name]:VC[name] + KB].unsqueeze(2).to_broadcast([P, KB, B])

            def p(n):
                return PAR[:, :, n * KB:(n + 1) * KB].rearrange("p b k -> p k b")

            sf, sc, gb = (TM[:, 16 + 4 * n:20 + 4 * n].rearrange("p (k b) -> p k b", k=KB) for n in range(3))
            ve.tensor_scalar(p(PU), c("scale_a"), 1.0, None, ALU.add)
            ve.tensor_copy(p(PU + 1), c("shift_a"))
            ve.tensor_scalar(sf, c("scale_ff"), 1.0, None, ALU.add)
            ve.tensor_tensor(gb, c("gamma"), v("ln3_b"), ALU.mult)
            ve.scalar_tensor_tensor(p(P1), c("f1_scale"), 1.0, v("norm1"), ALU.add, ALU.mult)
            ve.tensor_copy(p(P1 + 1), c("f1_shift"))
            ve.scalar_tensor_tensor(p(P2), c("f2_scale"), 1.0, v("norm2"), ALU.add, ALU.mult)
            ve.tensor_copy(p(P2 + 1), c("f2_shift"))
            l0(ve.tensor_tensor(p(P3), c("gamma"), v("ln3_g"), ALU.mult))
            ve.scalar_tensor_tensor(p(PM), c("scale_c"), 1.0, sf, ALU.add, ALU.mult)
            ve.tensor_tensor(p(P3 + 1), gb, c("beta"), ALU.add)
            l0(ve.tensor_tensor(sc, c("shift_c"), sf, ALU.mult))
            ve.tensor_tensor(p(PM + 1), sc, c("shift_ff"), ALU.add).then_inc(s_par, 1)
            ve.wait_ge(s_small, 4)
            ve.tensor_tensor(TR[:, 2, :], PA[0:B, 2, 0:D], LNR[:, 2, :], ALU.add).then_inc(s_hid, 1)
            normalise("n0", 0, True)
            for b in range(B):
                ve.wait_ge(s_small, 5 + b)
                ve.tensor_copy(GB[:, b].rearrange("p (s u) d -> p s (u d)", s=2), PA[:, 0:2, :]).then_inc(s_ctx, 1)
            ve.wait_ge(s_small, 7)
            ve.wait_ge(s_hidz, 1)
            ve.tensor_copy(HIDC[:, :, 0:B], PA[:, 3, 0:KB * B].rearrange("p (k b) -> p k b", b=B)).then_inc(s_ctx, 1)

            sd = [0]

            def bank(*job, rows_=P):
                n = DJ[job]
                assert n == sd[0], (job, n, sd)
                sd[0] += 1
                ve.wait_ge(s_dfull, n + 1)
                return PD[0:rows_, n % 4, :]

            def two(j):
                return slice(2 * j, 2 * j + 2)

            def pair(a):
                return a.rearrange("p (u d) -> p u d", u=2)

            def row2(a):
                return a.unsqueeze(1).to_broadcast([P, 2, D])

            def add_bank(b, tag, j, pre=None):
                if pre:
                    ve.wait_ge(s_pre, PRE[pre] * NC + j // 2 + 1)
                x = X[:, b, two(j), :]
                ve.tensor_tensor(x, pair(bank(b, tag, j)), x, ALU.add).then_inc(s_dev, 1)

            def add_out(b, tag):
                for j in range(TWO):
                    add_bank(b, tag, j)

            def after(b, tag):
                return lambda h: ve.wait_ge(s_dev, DJ[(b, tag, 2 * h + 1)] + 1)

            def n0(b):
                if b:
                    normalise("n0", b, True)

            def lr(n):
                if n >= 2:
                    ve.wait_ge(s_lrst[n % 2], 16 * B * (n // 2))
                ve.tensor_copy(LRO[:, n % 2, :], bank(n, "lr")[:, 0:LG]).then_inc(s_dev, 1)

            def lb(_):
                for u in range(2):
                    ve.wait_ge(s_lrst[u], 16 * B * NLCH // 2)
                ve.wait_ge(s_lbin, 32)
                for b in range(B):
                    ve.tensor_tensor(LA[:, b], LA[:, b], LAB[:, :, :, :], ALU.add)
                    i = ve.tensor_tensor(LB[:, b], LB[:, b], LBB, ALU.add)
                i.then_inc(s_lowrank, 1)

            def bu(b):
                if b == 0:
                    ve.wait_ge(s_bin, 32)
                    for a in range(B):
                        for s in range(2):
                            ve.scalar_tensor_tensor(CG[:, a, s, :], CT[:, s, :], SG[:, s:s + 1], GB[:, a, GA, :],
                                                    ALU.mult, ALU.mult)
                        for k in range(KB):
                            ve.scalar_tensor_tensor(DG[:, a, k, :], ident[:, :], VEC[:, VC["D"] + k:VC["D"] + k + 1],
                                                    GB[:, a, GA, k * P:(k + 1) * P], ALU.mult, ALU.mult)
                        i = ve.tensor_tensor(BG[:, a, :], BC[:, B20, :], GB[:, a, GF, :], ALU.mult)
                    i.then_inc(s_par, 1)
                Z, ZC = ZB[b][0], ZB[b][1]
                ve.wait_ge(s_tab, 1)
                for c in range(NC):
                    q = slice(c * HALF, (c + 1) * HALF)
                    ve.tensor_tensor(T1, bank(b, "bu", c, 0), C2[:, q], ALU.mult).then_inc(s_dev, 1)
                    ve.tensor_tensor(T2, bank(b, "bu", c, 1), S2[:, q], ALU.mult).then_inc(s_dev, 1)
                    ve.wait_ge(s_dev, sd[0])
                    link(ve.tensor_tensor(T1, T1, T2, ALU.add))
                    ve.tensor_tensor_scan(Z[:, q], RVEC[:, 0:1].to_broadcast([P, HALF]), T1,
                                          0.0 if c == 0 else Z[:, c * HALF - 1:c * HALF], ALU.mult, ALU.add).then_inc(s_z, 1)
                    ve.wait_ge(s_z, b * NC + c + 1)
                    ve.tensor_tensor(ZC[:, q], Z[:, q], C2[:, q], ALU.mult).then_inc(s_zc, 1)

            def y0(b):
                add_out(b, "y0")
                stats(b, after(b, "y0"))

            def low_weights(n):
                layer, w = divmod(n, 2)
                ve.wait_ge(s_whigh, n + 1)
                ve.tensor_tensor(WL[w], W12[:, w], WH[layer][w], ALU.subtract).then_inc(s_wh, 1)

            def split(stage):
                def f(part):
                    for job in split_jobs(stage, part):
                        b, tag, c, k = job
                        n, layer = SJ[job], int(stage in ("n2", "u1"))
                        hi, lo = (XS[:, c, x, k, :] if tag in ("m", "n2") else HS[:, x, k, :] for x in range(2))
                        src = FT[layer][n % NRING]
                        ve.wait_ge(s_aev, AJ[job] + 1)
                        chunk = (layer * B + b) * NC + c
                        if tag in ("h0", "h1") and chunk:
                            if k < NF - 1:
                                ve.wait_ge(s_used, (chunk - 1) * (NF - 1) + k + 1)
                            else:
                                lb_, c_ = divmod(chunk - 1, NC)
                                l_, b_ = divmod(lb_, B)
                                ve.wait_ge(s_dfull, DJ[(b_, f"w2{l_}", (c_ + 1) * TPC - 1)] + 1)
                        link(ve.tensor_copy(hi, src))
                        ve.tensor_tensor(lo, src, hi, ALU.subtract).then_inc(s_split, 1)
                return f

            def d0(part):
                for b, _, t in dve_jobs("d0", part):
                    h = t // TPC
                    ve.wait_ge(s_pre, PRE[("y0", b)] * NC + h + 1)
                    y = TG[:, t % 2 * D:(t % 2 + 1) * D]
                    ve.tensor_tensor(y, bank(b, "w20", t)[:, 0:D], GB[:, b, GF, :], ALU.mult).then_inc(s_dev, 1)
                    ve.wait_ge(s_dev, sd[0])
                    link(ve.tensor_tensor(X[:, b, t, :], X[:, b, t, :], y, ALU.add))
                    if t % TPC == TPC - 1:
                        stats(b, lambda h: None, [h])

            def d1(part):
                for b, _, t in dve_jobs("d1", part):
                    ve.wait_ge(s_pre, PRE[("pr", b)] * NC + t // TPC + 1)
                    x = X[:, b, t, :]
                    ve.tensor_tensor(x, bank(b, "w21", t)[:, 0:D], x, ALU.add).then_inc(s_dev, 1)

            def h0(b):
                normalise("h0", b, False)

            def qkv(b):
                for j in range(TWO):
                    ve.tensor_tensor(V[:, two(j), :], pair(bank(b, "v1", j)), row2(BC[:, BV, :]), ALU.add).then_inc(s_dev, 1)

            def att(b):
                for t in range(NT):
                    ve.wait_ge(s_sfull, b * NT + t + 1)
                    ve.tensor_reduce(NM[:, t:t + 1], PDF[:, t % 2, :], axis=AX_X, op=ALU.max, negate=True).then_inc(s_max1, 1)
                    ve.wait_ge(s_max1, b * NT + t + 1)
                    ve.tensor_scalar(NMS[:, b, t:t + 1], NM[:, t:t + 1], float(D) ** -0.5, None, ALU.mult).then_inc(s_nmax, 1)

            def pr(b):
                ve.wait_ge(s_exp1, (b + 1) * NT)
                link(ve.reciprocal(RSM[:, b, :], SM[:, b, :]))
                for j in range(TWO):
                    ve.wait_ge(s_pre, PRE[("h0", b)] * NC + j // 2 + 1)
                    o = bank(b, "pr", j)
                    for u in range(2):
                        t = 2 * j + u
                        x = X[:, b, t, :]
                        i = ve.scalar_tensor_tensor(x, o[:, u * D:(u + 1) * D], RSM[:, b, t:t + 1], x, ALU.mult, ALU.add)
                    i.then_inc(s_dev, 1)
                stats(b, after(b, "pr"))

            def rank_rows(tag, s):
                def f(b):
                    for c in range(NC):
                        ve.tensor_copy(Y8[:, b, s, c * HALF:(c + 1) * HALF], bank(b, tag, c, rows_=RANK)).then_inc(s_dev, 1)
                return f

            def f2(b):
                add_out(b, "f2")
                stats(b, after(b, "f2"))
                normalise("f2", b, True)

            def qk3(b):
                def mid(j):
                    ve.wait_ge(s_rest, j + 1)
                    ve.tensor_copy(PARTS[:, j % 2, 1, :], RP).then_inc(s_mid, 1)

                for j, (name, c, k) in enumerate(QK3_JOBS if b == 0 else []):
                    ve.wait_ge(s_aev, AJ[(b, name, c, k)] + 1)
                    if j >= 2:
                        parts_stored(ve, j)
                    ve.tensor_copy(PARTS[:, j % 2, 0, :], QF[b][j]).then_inc(s_hi, 1)
                    mid(j)
                ve.wait_ge(s_dfull, DJ[(1, "w21", NT - 1)] + 1)
                for j in range(TWO):
                    o = bank(b, "v3", j)
                    for u in range(2):
                        i = ve.tensor_tensor(VP[b][:, 2 * j + u, :, 0:HD],
                                             o[:, u * D:(u + 1) * D].rearrange("p (h d) -> p h d", h=HEADS),
                                             BC[:, BV3, :].rearrange("p (h d) -> p h d", h=HEADS), ALU.add)
                    i.then_inc(s_dev, 1)

            def reduce_max(n):
                ve.wait_ge(s_mfull, n + 1)
                m, r = divmod(n, UNIT)
                ve.tensor_reduce(NMX[:, m % 2, r:r + 1], PDF[:, n % 2, :], axis=AX_X, op=ALU.max,
                                 negate=True).then_inc(s_mred, 1)
                if r == UNIT - 1:
                    split_max(m)

            def split_max(m):
                ve.wait_ge(s_mred, (m + 1) * UNIT)
                if m >= 1:
                    ve.wait_ge(s_nmtf, m)
                f = NMX[:, m % 2, :]
                link(ve.tensor_copy(NMP[:, 0, :], f))
                link(ve.tensor_tensor(NMR[:, :], f, NMP[:, 0, :], ALU.subtract))
                link(ve.tensor_copy(NMP[:, 1, :], NMR[:, :]))
                ve.tensor_tensor(NMP[:, 2, :], NMR[:, :], NMP[:, 1, :], ALU.subtract).then_inc(s_nmp, 1)

            def norm_heads_out(m):
                gg, c = divmod(m, NC)
                b, g = divmod(gg, NG)
                if m == 0 or m == NUNIT // B:
                    ve.wait_ge(s_parts, (b + 1) * 2 * KB * NC)
                ve.wait_ge(s_ut, m + 1)
                o = PA[:, 3, :].rearrange("p (n c) -> p n c", c=32)
                link(ve.reciprocal(RC[:, :], o[:, :, HD]))
                ve.tensor_tensor(
                    O[b][:, c * TPC:(c + 1) * TPC, g * GH * HD:(g + 1) * GH * HD].rearrange("p t (h d) -> p t h d", h=GH),
                    PA[:, 3, :].rearrange("p (t h c) -> p t h c", t=TPC, h=GH)[:, :, :, 0:HD],
                    RC[:, :].rearrange("p (t h) -> p t h", t=TPC).unsqueeze(3).to_broadcast([P, TPC, GH, HD]),
                    ALU.mult).then_inc(s_on, 1)

            def lead(part):
                per = LEAD // NLEAD
                for n in range(part * per, (part + 1) * per):
                    reduce_max(n)

            def step(n):
                m, kt = divmod(n, NT)
                s = LEAD + 2 * n
                if s < NMAX:
                    reduce_max(s)
                    reduce_max(s + 1)
                if kt == 1 and m >= 1:
                    norm_heads_out(m - 1)
                if n == NSTEP - 1:
                    norm_heads_out(NUNIT - 1)

            def turned_first(h):
                for k in range(KB):
                    ve.tensor_copy(XT[:, 0, k, h * HALF:(h + 1) * HALF], bank(0, "ot", h, k)).then_inc(s_dev, 1)

            def p3(part):
                b, j = divmod(part, TWO)
                add_bank(b, "p3", j, ("f2", b))
                if j % 2:
                    ve.wait_ge(s_dev, sd[0])
                    stats(b, lambda h: None, [j // 2])

            def end(b):
                normalise("end", b, True, s_scaled)
                for h in range(NC):
                    y = XN[:, b, h * TPC:(h + 1) * TPC, :]
                    ve.wait_ge(s_scaled, b * NC + h + 1)
                    link(ve.tensor_tensor(y, y, GB[:, b, S3, :].unsqueeze(1).to_broadcast([P, TPC, D]), ALU.mult))
                    ve.wait_ge(s_pre, PRE[("end", b)] * NC + h + 1)
                    ve.tensor_tensor(y, y, X[:, b, h * TPC:(h + 1) * TPC, :], ALU.add).then_inc(s_fin, 1)

            run({"ws": low_weights, "yn": lambda b: normalise("y0", b, True), "pn": lambda b: normalise("pr", b, False),
                  "n0": n0, "lr": lr, "bu": bu, "y0": y0, "m": split("m"), "n2": split("n2"), "u0": split("u0"),
                 "u1": split("u1"), "d0": d0, "h0": h0, "lb": lb, "qkv": qkv, "att": att, "pr": pr, "d1": d1,
                 "a1": rank_rows("a1", 0), "a2": rank_rows("a2", 1), "f2": f2, "qk3": qk3, "lead": lead, "step": step,
                 "oa": turned_first, "p3": p3, "end": end})
            assert sd[0] == len(DJ)


def kernel(**inputs):
    import concourse.bacc as _bacc
    from concourse.bass_utils import run_bass_kernel_spmd as _run

    g = {k: np.asarray(v) for k, v in inputs.items()}

    def blocks(a):
        return a.reshape(-1, P).T

    def twice(a, b):
        return np.concatenate([a, b], axis=0)

    def kpn(w):
        return w.reshape(KB, P, -1).transpose(1, 0, 2)

    t = g["cond_1024"]
    wq3 = g["L3_cond_Wqkv"].reshape(D, 3, D)
    bq3 = g["L3_cond_bqkv"].reshape(D, 3)
    w2 = g["L2_cond_W2"].reshape(D, 4, D, RANK)
    b2 = g["L2_cond_b2"].reshape(4, D, RANK)
    l2_w2 = np.concatenate([w2[:, 0].reshape(D, -1), w2[:, 2].reshape(D, -1),
                            w2[:, 1].transpose(0, 2, 1).reshape(D, -1), w2[:, 3].transpose(0, 2, 1).reshape(D, -1)], axis=1)
    l2_b2 = np.concatenate([b2[0].reshape(-1), b2[2].reshape(-1), b2[1].T.reshape(-1), b2[3].T.reshape(-1)])
    col = lambda n: np.concatenate([g[n], g[n]])[:, None]
    arrays = {
        "x": g["x"], "t": t, "tT": t.T.reshape(KB, P, B).transpose(1, 0, 2),
        "lnrow": np.stack([g["L2_cond_ln_g"], g["L2_cond_ln_b"], g["L2_cond_b1"], g["L3_cond_ln_g"], g["L3_cond_ln_b"]]),
        "vec": np.concatenate(
            [blocks(g[n]) for n in ("L1_cond_norm1_w", "L1_cond_norm2_w", "L3_cond_ln_g", "L3_cond_ln_b", "L1_cond_q_b",
                                    "L1_cond_k_b")] + [blocks(bq3[:, 0]), blocks(bq3[:, 1])]
            + [blocks(g[n]) for n in ("L0_cond_D_diag", "L0_cond_b1", "L1_cond_mlp_b1")]
            + [col(n) for n in ("L0_cond_Lam_re", "L0_cond_Lam_im", "L0_cond_log_step")], axis=1),
        "wcond": np.concatenate([g["L0_cond_Wm"], g["L0_cond_Wc"], g["L1_cond_film1_w"], g["L1_cond_film2_w"],
                                 g["L3_cond_Wg"].T, g["L3_cond_Wb"].T], axis=1),
        "bcond": np.concatenate([g["L0_cond_bm"], g["L0_cond_bc"], g["L1_cond_film1_b"], g["L1_cond_film2_b"],
                                 g["L3_cond_bg"], g["L3_cond_bb"]]),
        "l2_w1": g["L2_cond_W1"], "l2_w2": l2_w2, "l2_b2": l2_b2,
        "b2x": np.stack([twice(g["L0_cond_B_re"], g["L0_cond_B_re"]), twice(g["L0_cond_B_im"], g["L0_cond_B_im"])], axis=1),
        "ct": np.stack([twice(g["L0_cond_C_re"].T, g["L0_cond_C_im"].T), twice(g["L0_cond_C_im"].T, g["L0_cond_C_re"].T)],
                       axis=1),
        "bc": np.stack([g["L1_cond_v_b"], g["L1_cond_proj_b"], g["L1_cond_mlp_b2"], bq3[:, 2], g["L3_cond_bp"],
                        g["L0_cond_b2"]]),
        "wa": np.stack([kpn(g[f"L1_cond_{n}_w"]) for n in ("q", "k", "v", "proj")], axis=1),
        "wqkv3": np.stack([kpn(wq3[:, j].T) for j in range(3)], axis=1),
        "wp3": g["L3_cond_Wp"].T,
        "w1_0": g["L0_cond_W1"], "w2_0": g["L0_cond_W2"], "w1_1": g["L1_cond_mlp_w1"], "w2_1": g["L1_cond_mlp_w2"],
    }
    arrays = {k: np.ascontiguousarray(v) for k, v in arrays.items()}
    nc = _bacc.Bacc("TRN2", target_bir_lowering=False, num_devices=1)
    ins = {k: nc.dram_tensor(f"in_{k}", v.shape, mybir.dt.from_np(v.dtype), kind="ExternalInput").ap()
           for k, v in arrays.items()}
    out = nc.dram_tensor("out_0", (B, T, D), F32, kind="ExternalOutput").ap()
    build(nc, ins, out)
    r = _run(nc, [{f"in_{k}": v for k, v in arrays.items()}], core_ids=[0])
    return r.results[0]["out_0"]
```
